# Optimizing a Trainium2 kernel written in Bass

```python
import numpy as np
import jax
import jax.numpy as jnp

def _softmax(x, axis=-1):
    return jax.nn.softmax(x, axis=axis)

def _gelu(x):
    return jax.nn.gelu(x, approximate=True)

def _silu(x):
    return jax.nn.silu(x)

def _sigmoid(x):
    return jax.nn.sigmoid(x)

def _layernorm(x, axis=-1, eps=1e-05):
    m = jnp.mean(x, axis=axis, keepdims=True)
    v = jnp.var(x, axis=axis, keepdims=True)
    return (x - m) / jnp.sqrt(v + eps)

def _scatter_add(tgt, idx, src, axis=0):
    return tgt.at[idx].add(src)

def _segment_sum(src, seg, n):
    return jax.ops.segment_sum(src, seg, n)
kernel_name = 'mk_perceiver_d1_seqx_r2_e1ccc8'

def setup_inputs(seed: int=0):
    np.random.seed(seed)
    _w = jnp.asarray

    def _rec_inputs():
        import jax
        import jax.numpy as jnp
        _rk = jax.random.key(seed)
        x = -0.0005207 + 1.001 * jax.random.normal(jax.random.fold_in(_rk, 1), (32, 32, 512), jnp.float32)
        _lenS = 32 - jax.random.randint(jax.random.fold_in(_rk, 7), (32,), 0, max(1, 32 // 4) + 1, jnp.int32)
        _lenS2 = 257 - jax.random.randint(jax.random.fold_in(_rk, 8), (32,), 0, max(1, 257 // 4) + 1, jnp.int32)
        _ctx_1024P = jax.random.normal(jax.random.fold_in(_rk, 11), (32, 16, 512), jnp.float32)
        _ctx_1024c = jax.random.dirichlet(jax.random.fold_in(_rk, 511), 0.3 * jnp.ones((16,), jnp.float32), (32, 257))
        _ctx_1024t = jnp.einsum('bsk,bkd->bsd', _ctx_1024c, _ctx_1024P)
        _ctx_1024t = _ctx_1024t * jax.lax.rsqrt(jnp.mean(jnp.square(_ctx_1024t)) + 1e-12) * 0.953939
        ctx_1024 = -1.39393e-06 + 0.999914 * (_ctx_1024t + 0.3 * jax.random.normal(jax.random.fold_in(_rk, 611), (32, 257, 512), jnp.float32))
        _validS = jnp.arange(32)[None, :] < _lenS[:, None]
        _validS2 = jnp.arange(257)[None, :] < _lenS2[:, None]
        _causal = jnp.tril(jnp.ones((32, 32), dtype=bool))
        mask_BxSxS2_bk0 = jnp.logical_not(jnp.broadcast_to(_validS2[:, None, :], (32, 32, 257)))
        return (x, ctx_1024, mask_BxSxS2_bk0)
    x, ctx_1024, mask_BxSxS2_bk0 = _rec_inputs()

    def _L0_xattn_setup():
        import jax, jax.numpy as jnp
        import numpy as np
        DIM = 512
        HEAD_DIM = 64
        NUM_HEADS = DIM // HEAD_DIM
        EPS = 1e-06
        SCALE = HEAD_DIM ** (-0.5)

        def _per_head_ln(t, w):
            mu = jnp.mean(t, axis=-1, keepdims=True)
            var = jnp.mean(jnp.square(t - mu), axis=-1, keepdims=True)
            t = (t - mu) * jax.lax.rsqrt(var + EPS)
            return t * w[None, :, None, :]
        key = jax.random.key(seed)
        ks = jax.random.split(key, 8)
        B, N, M = (2, 512, 1024)
        x = jax.random.normal(ks[0], (B, N, DIM), dtype=jnp.float32)
        context = jax.random.normal(ks[1], (B, M, DIM), dtype=jnp.float32)
        mask = jax.random.randint(ks[2], (B, N, M), 0, 2).astype(jnp.bool_)
        Wq = jax.random.normal(ks[3], (DIM, DIM), dtype=jnp.float32) * 0.02
        Wkv = jax.random.normal(ks[4], (DIM, 2 * DIM), dtype=jnp.float32) * 0.02
        Wo = jax.random.normal(ks[5], (DIM, DIM), dtype=jnp.float32) * 0.02
        qn_w = jnp.ones((NUM_HEADS, HEAD_DIM), dtype=jnp.float32)
        kn_w = jnp.ones((NUM_HEADS, HEAD_DIM), dtype=jnp.float32)
        return {'x': x, 'context': context, 'mask': mask, 'Wq': Wq, 'Wkv': Wkv, 'Wo': Wo, 'qn_w': qn_w, 'kn_w': kn_w}
    _L0_xattn_all = _L0_xattn_setup()
    _L0_xattn_in = {k: v for k, v in _L0_xattn_all.items() if k in ('Wq', 'Wkv', 'Wo', 'qn_w', 'kn_w')}
    del _L0_xattn_all

    def _L0_attn_setup():
        import jax, jax.numpy as jnp
        import numpy as np
        B, N, D = (8, 1024, 512)
        A_STDP, TAU_STDP, W_OFF, T_MAX = (0.9, 0.5, 0.9, 1.0)
        V_TH, EPS = (1.0, 1e-05)

        def _proj(x, W, g, b, m, v):
            h = x @ W
            h = (h - m) * (g * jax.lax.rsqrt(v + EPS)) + b
            return jax.nn.sigmoid(4.0 * (h - V_TH))
        key = jax.random.key(seed)
        ks = jax.random.split(key, 6)
        s = 0.02
        inp = {'x': jax.random.normal(ks[0], (B, N, D), dtype=jnp.float32)}
        for i, nm in enumerate(['q', 'k', 'v']):
            inp[f'W{nm}'] = jax.random.normal(ks[1 + i], (D, D), dtype=jnp.float32) * s
            inp[f'g{nm}'] = jnp.ones((D,), jnp.float32)
            inp[f'b{nm}'] = jnp.zeros((D,), jnp.float32)
            inp[f'm{nm}'] = jnp.zeros((D,), jnp.float32)
            inp[f'v{nm}'] = jnp.ones((D,), jnp.float32)
        inp['Wo'] = jax.random.normal(ks[4], (D, D), dtype=jnp.float32) * s
        inp['bo'] = jnp.zeros((D,), jnp.float32)
        return inp
    _L0_attn_all = _L0_attn_setup()
    _L0_attn_in = {k: v for k, v in _L0_attn_all.items() if k in ('Wq', 'gq', 'bq', 'mq', 'vq', 'Wk', 'gk', 'bk', 'mk', 'vk', 'Wv', 'gv', 'bv', 'mv', 'vv', 'Wo', 'bo')}
    del _L0_attn_all

    def _L0_ffn_setup():
        import jax, jax.numpy as jnp
        import numpy as np
        TOP_K = 2
        key = jax.random.key(seed)
        k_x, k_g, k_w1, k_w2, k_w3 = jax.random.split(key, 5)
        B, S, D, H, E = (2, 256, 512, 256, 8)
        x = jax.random.normal(k_x, (B, S, D), dtype=jnp.float32)
        gate_w = jax.random.normal(k_g, (D, E), dtype=jnp.float32) * D ** (-0.5)
        w1 = jax.random.normal(k_w1, (E, D, H), dtype=jnp.float32) * 0.02
        w2 = jax.random.normal(k_w2, (E, H, D), dtype=jnp.float32) * 0.02
        w3 = jax.random.normal(k_w3, (E, D, H), dtype=jnp.float32) * 0.02
        return {'x': x, 'gate_w': gate_w, 'w1': w1, 'w2': w2, 'w3': w3}
    _L0_ffn_all = _L0_ffn_setup()
    _L0_ffn_in = {k: v for k, v in _L0_ffn_all.items() if k in ('gate_w', 'w1', 'w2', 'w3')}
    del _L0_ffn_all
    return {'x': x, 'ctx_1024': ctx_1024, 'mask_BxSxS2_bk0': mask_BxSxS2_bk0, 'L0_xattn_Wq': _L0_xattn_in['Wq'], 'L0_xattn_Wkv': _L0_xattn_in['Wkv'], 'L0_xattn_Wo': _L0_xattn_in['Wo'], 'L0_xattn_qn_w': _L0_xattn_in['qn_w'], 'L0_xattn_kn_w': _L0_xattn_in['kn_w'], 'L0_attn_Wq': _L0_attn_in['Wq'], 'L0_attn_gq': _L0_attn_in['gq'], 'L0_attn_bq': _L0_attn_in['bq'], 'L0_attn_mq': _L0_attn_in['mq'], 'L0_attn_vq': _L0_attn_in['vq'], 'L0_attn_Wk': _L0_attn_in['Wk'], 'L0_attn_gk': _L0_attn_in['gk'], 'L0_attn_bk': _L0_attn_in['bk'], 'L0_attn_mk': _L0_attn_in['mk'], 'L0_attn_vk': _L0_attn_in['vk'], 'L0_attn_Wv': _L0_attn_in['Wv'], 'L0_attn_gv': _L0_attn_in['gv'], 'L0_attn_bv': _L0_attn_in['bv'], 'L0_attn_mv': _L0_attn_in['mv'], 'L0_attn_vv': _L0_attn_in['vv'], 'L0_attn_Wo': _L0_attn_in['Wo'], 'L0_attn_bo': _L0_attn_in['bo'], 'L0_ffn_gate_w': _L0_ffn_in['gate_w'], 'L0_ffn_w1': _L0_ffn_in['w1'], 'L0_ffn_w2': _L0_ffn_in['w2'], 'L0_ffn_w3': _L0_ffn_in['w3']}

def reference(x, ctx_1024, mask_BxSxS2_bk0, L0_xattn_Wq, L0_xattn_Wkv, L0_xattn_Wo, L0_xattn_qn_w, L0_xattn_kn_w, L0_attn_Wq, L0_attn_gq, L0_attn_bq, L0_attn_mq, L0_attn_vq, L0_attn_Wk, L0_attn_gk, L0_attn_bk, L0_attn_mk, L0_attn_vk, L0_attn_Wv, L0_attn_gv, L0_attn_bv, L0_attn_mv, L0_attn_vv, L0_attn_Wo, L0_attn_bo, L0_ffn_gate_w, L0_ffn_w1, L0_ffn_w2, L0_ffn_w3):
    import jax
    import jax.numpy as jnp

    def _L0_xattn_ref(x, context, mask, Wq, Wkv, Wo, qn_w, kn_w):
        import jax, jax.numpy as jnp
        import numpy as np
        DIM = 512
        HEAD_DIM = 64
        NUM_HEADS = DIM // HEAD_DIM
        EPS = 1e-06
        SCALE = HEAD_DIM ** (-0.5)

        def _per_head_ln(t, w):
            mu = jnp.mean(t, axis=-1, keepdims=True)
            var = jnp.mean(jnp.square(t - mu), axis=-1, keepdims=True)
            t = (t - mu) * jax.lax.rsqrt(var + EPS)
            return t * w[None, :, None, :]
        B, N, C = x.shape
        M = context.shape[1]
        H, D = (NUM_HEADS, HEAD_DIM)
        q = (x @ Wq).reshape(B, N, H, D).transpose(0, 2, 1, 3)
        kv = (context @ Wkv).reshape(B, M, 2, H, D)
        k = kv[:, :, 0].transpose(0, 2, 1, 3)
        v = kv[:, :, 1].transpose(0, 2, 1, 3)
        q = _per_head_ln(q, qn_w)
        k = _per_head_ln(k, kn_w)
        attn = jnp.einsum('bhnd,bhmd->bhnm', q, k) * SCALE
        attn = jnp.where(mask[:, None, :, :], attn, -jnp.inf)
        attn = jax.nn.softmax(attn, axis=-1)
        out = jnp.einsum('bhnm,bhmd->bhnd', attn, v)
        out = out.transpose(0, 2, 1, 3).reshape(B, N, C)
        return out @ Wo

    def _L0_attn_ref(x, Wq, gq, bq, mq, vq, Wk, gk, bk, mk, vk, Wv, gv, bv, mv, vv, Wo, bo):
        import jax, jax.numpy as jnp
        import numpy as np
        B, N, D = (8, 1024, 512)
        A_STDP, TAU_STDP, W_OFF, T_MAX = (0.9, 0.5, 0.9, 1.0)
        V_TH, EPS = (1.0, 1e-05)

        def _proj(x, W, g, b, m, v):
            h = x @ W
            h = (h - m) * (g * jax.lax.rsqrt(v + EPS)) + b
            return jax.nn.sigmoid(4.0 * (h - V_TH))
        Q = _proj(x, Wq, gq, bq, mq, vq)
        K = _proj(x, Wk, gk, bk, mk, vk)
        V = _proj(x, Wv, gv, bv, mv, vv)
        t_Q = T_MAX * (1.0 - Q.mean(axis=-1, keepdims=True))
        t_K = T_MAX * (1.0 - K.mean(axis=-1, keepdims=True))
        delta_t = t_Q - jnp.swapaxes(t_K, 1, 2)
        f_stdp = A_STDP * jnp.exp(-jnp.abs(delta_t) / TAU_STDP)
        A = jnp.where(delta_t < 0, f_stdp, -f_stdp) + W_OFF
        return A @ V @ Wo + bo

    def _L0_ffn_ref(x, gate_w, w1, w2, w3):
        import jax, jax.numpy as jnp
        import numpy as np
        TOP_K = 2
        B, S, D = x.shape
        E = gate_w.shape[1]
        xf = x.reshape(B * S, D)
        T = B * S
        logits = xf @ gate_w
        scores = jax.nn.softmax(logits, axis=-1)
        top_scores, top_idx = jax.lax.top_k(scores, TOP_K)
        scale = jnp.zeros((T, E), dtype=x.dtype).at[jnp.arange(T)[:, None], top_idx].set(top_scores)
        xs = scale.T[:, :, None] * xf[None, :, :]
        h = jax.nn.silu(jnp.einsum('etd,edh->eth', xs, w1)) * jnp.einsum('etd,edh->eth', xs, w3)
        y = jnp.einsum('eth,ehd->etd', h, w2)
        out = y.sum(axis=0)
        return out.reshape(B, S, D)
    x = x + _L0_xattn_ref(_layernorm(x, axis=-1), ctx_1024, mask_BxSxS2_bk0, L0_xattn_Wq, L0_xattn_Wkv, L0_xattn_Wo, L0_xattn_qn_w, L0_xattn_kn_w)
    x = x + _L0_attn_ref(_layernorm(x, axis=-1), L0_attn_Wq, L0_attn_gq, L0_attn_bq, L0_attn_mq, L0_attn_vq, L0_attn_Wk, L0_attn_gk, L0_attn_bk, L0_attn_mk, L0_attn_vk, L0_attn_Wv, L0_attn_gv, L0_attn_bv, L0_attn_mv, L0_attn_vv, L0_attn_Wo, L0_attn_bo)
    x = x + _L0_ffn_ref(_layernorm(x, axis=-1), L0_ffn_gate_w, L0_ffn_w1, L0_ffn_w2, L0_ffn_w3)
    return x

_drawn_inputs = setup_inputs


def setup_inputs(seed=0):
    import zlib

    import numpy as np

    out = dict(_drawn_inputs(seed))
    spreads = {'L0_xattn_qn_w': (1.0, 0.596),
     'L0_xattn_kn_w': (1.0, 0.561),
     'L0_attn_gq': (1.0, 0.2),
     'L0_attn_bq': (0.0, 0.1),
     'L0_attn_mq': (0.0, 0.1),
     'L0_attn_vq': (1.0, 0.2),
     'L0_attn_gk': (1.0, 0.2),
     'L0_attn_bk': (0.0, 0.1),
     'L0_attn_mk': (0.0, 0.1),
     'L0_attn_vk': (1.0, 0.2),
     'L0_attn_gv': (1.0, 0.2),
     'L0_attn_bv': (0.0, 0.1),
     'L0_attn_mv': (0.0, 0.1),
     'L0_attn_vv': (1.0, 0.2),
     'L0_attn_bo': (0.0, 0.1)}
    factors = {'L0_ffn_gate_w': 8.0, 'L0_ffn_w1': 8.0, 'L0_ffn_w2': 8.0, 'L0_ffn_w3': 8.0}
    for name, (base, spread) in spreads.items():
        noise = np.random.default_rng([zlib.crc32(name.encode()), seed]).standard_normal(out[name].shape)
        drawn = base * np.exp(spread * noise) if base else spread * noise
        out[name] = jnp.asarray(drawn.astype(out[name].dtype))
    for name, factor in factors.items():
        out[name] = (out[name] * factor).astype(out[name].dtype)
    return out
```

```python
from contextlib import ExitStack

import concourse.bass as bass
from concourse import mybir

F32 = mybir.dt.float32
F32R = mybir.dt.float32r
U8 = mybir.dt.uint8
ALU = mybir.AluOpType
ACT = mybir.ActivationFunctionType
AX = mybir.AxisListType

P = 128
HI, LO = 0, 1
BIG = 3.0e38
LN_EPS, HEAD_EPS, BN_EPS = 1e-5, 1e-6, 1e-5
V_TH, SLOPE = 1.0, 4.0
A_STDP, TAU, W_OFF = 0.9, 0.5, 0.9


def split_products(pe, out, lhs, rhs, chunks, start=True, stop=True):
    last = None
    for c in range(chunks):
        for n, (a, b) in enumerate(((HI, HI), (HI, LO), (LO, HI))):
            last = pe.matmul(out, lhs(a, c), rhs(b, c), start=start and c == 0 and n == 0,
                             stop=stop and c == chunks - 1 and n == 2)
    return last


def perceiver_block(nc, x, ctx, mask, xWq, xWkv, xWo, qn_w, kn_w, aWq, gq, bq, mq, vq, aWk, gk, bk, mk, vk,
                    aWv, gv, bv, mv, vv, aWo, bo, gate_w, w1, w2, w3, out):
    B, S, D = x.shape
    M = ctx.shape[1]
    H, HD = qn_w.shape
    E, _, F = w1.shape
    TILES = B * S // P
    C = D // P
    BT = P // S
    MT = M // P
    HG = P // S
    G = H // HG
    RAW = C * D + 2 * D
    SCALE = float(HD) ** -0.5
    assert M == MT * P + 1 and MT == 2 and G == 2 and C == 4 and 2 * HD == P and H == 8 and F == 2 * P
    assert B == TILES * BT and TILES == 8 and B % 2 == 0 and E == 8

    x_t = x.rearrange("b s d -> (b s) d").rearrange("(t p) d -> p t d", p=P)
    out_t = out.rearrange("b s d -> (b s) d").rearrange("(t p) d -> p t d", p=P)

    def chunked(w):
        return w.rearrange("(c p) n -> p c n", p=P)

    def spread(v):
        return v.partition_broadcast(P)

    with ExitStack() as es:
        def sb(name, shape, dt=F32):
            return es.enter_context(nc.sbuf_tensor(name, shape, dt))

        def ps(name, shape):
            return es.enter_context(nc.psum_tensor(name, shape, F32))

        def sem(name):
            return es.enter_context(nc.semaphore(name))

        ident = sb("ident", [P, P])
        ones = sb("ones", [P, P])
        same_seq = sb("same_seq", [P, P])
        col = sb("col", [P, P])
        x_all = sb("x_all", [P, TILES, D])
        bias = sb("bias", [P, 4])
        LN_B, HEAD_B, BN_B, SIG_B = (bias[:, i:i + 1] for i in range(4))
        xn = sb("xn", [P, 2, D])
        bst = sb("bst", [P, 2, 6])
        mean_var = sb("mean_var", [P, 2, 2])
        ln_log = sb("ln_log", [P, 2, 1])
        ln_rs = sb("ln_rs", [P, 2, 1])
        wide = sb("wide", [P, 2 * RAW])
        w_raw = wide[:, 0:2 * C * D].rearrange("p (u c n) -> p u c n", u=2, c=C)
        ctx_raw = wide[:, 2 * C * D:2 * RAW].rearrange("p (u t d) -> p u t d", u=2, t=MT)
        e_raw = wide[:, :].rearrange("p (u n) -> p u n", u=2)
        qoT = sb("qoT", [P, C, TILES * P])
        v_self = qoT[:, :, :].rearrange("p c n -> p (c n)").rearrange("p (t d) -> p t d", t=TILES)
        sq = sb("sq", [P, 2, D])
        kn = sb("kn", [P, 2, D])
        head_ss = sb("head_ss", [P, 2, H])
        head_log = sb("head_log", [P, 2, H])
        head_rs = sb("head_rs", [P, 2, H])
        head_mean = sb("head_mean", [P, C, H])
        qkw = sb("qkw", [P, 2, D])
        kT_rem = sb("kT_rem", [P, C, B])
        v_rem = sb("v_rem", [P, D])
        s_m = sb("s_m", [P, G, M + 1])
        prob = sb("prob", [P, G, M + 1])
        neg_max = sb("neg_max", [P, G])
        p_sum = sb("p_sum", [P, G])
        p_den = sb("p_den", [P, G])
        p_inv = sb("p_inv", [P, G])
        p_scale = sb("p_scale", [P, G])
        p_rem = sb("p_rem", [P, G, P])
        pT_rem = sb("pT_rem", [P, G * P])
        mask_f = sb("mask_f", [P, B * M // 4])
        masked = mask_f[:, :].bitcast(U8).rearrange("p (b m) -> p b m", b=B)
        bn_vec = mask_f[:, 0:4 * D].rearrange("p (v d) -> p v d", v=4)
        rows = sb("rows", [P, 2, TILES])
        gw_raw = sb("gw_raw", [P, C, E])
        tri = sb("tri", [P, E, E])
        gates = sb("gates", [P, TILES, E])
        g_tmp = sb("g_tmp", [P, TILES, E])
        g_red = sb("g_red", [P, TILES])
        g_now = sb("g_now", [P, 2, TILES])
        parts = sb("parts", [P, 8 * C * D], F32R)
        wkv = parts[:, 0:4 * C * D].rearrange("p (s c n) -> p s c n", s=2, c=C)
        ctxT = parts[:, 4 * C * D:6 * C * D].rearrange("p (u s c n) -> p u s c n", u=2, s=2, c=C)
        v_p = parts[:, 6 * C * D:8 * C * D].rearrange("p (u s t d) -> p u s t d", u=2, s=2, t=MT)
        xT = parts[:, 0:4 * C * D].rearrange("p (s c n) -> p s c n", s=2, c=C)
        lhs_p = parts[:, 7 * C * D:8 * C * D].rearrange("p (u s c n) -> p u s c n", u=2, s=2, c=C)
        hT = parts[:, 7 * C * D:7 * C * D + 8 * P].rearrange("p (u s c n) -> p u s c n", u=2, s=2, c=2)
        kT = sb("kT", [P, 2, C, M + 1], F32R)
        qblk = sb("qblk", [P, 2, C, P], F32R)
        pT = sb("pT", [P, 2, MT, G * P], F32R)
        w_p = sb("w_p", [P, 4 * C * D], F32R)
        w_slot = w_p[:, :].rearrange("p (u s c n) -> p u s c n", u=2, s=2, c=C)
        gw_p = sb("gw_p", [P, 2, C, E], F32R)
        e_p = [parts[:, 4 * C * D:4 * C * D + 2 * RAW].rearrange("p (s n) -> p s n", s=2),
               w_p[:, 0:2 * RAW].rearrange("p (s n) -> p s n", s=2)]

        pK0, pK1, pV1 = ps("pK0", [P, D]), ps("pK1", [P, D]), ps("pV1", [P, D])
        pT0, pT1 = ps("pT0", [P, C, P]), ps("pT1", [P, C, P])
        pS = ps("pS", [P, G, 512])
        pP = ps("pP", [P, MT, G * P])
        pKV, pTT, pZ = (pK0, pK1), (pT0, pT1), (pK0, pK1, pV1)

        const_set = sem("const_set")
        ident_step = sem("ident_step")
        x_in = [sem("x_in0"), sem("x_in1")]
        qn_in, kn_in, rem_in, mask_in, gate_in, bo_in = (sem(n) for n in (
            "qn_in", "kn_in", "rem_in", "mask_in", "gate_in", "bo_in"))
        JOBS = ("xq", "xk", "xv", "xo", "aq", "ak", "av", "ao")
        w_in, w_pre, w_hi, w_lo = ([sem(f"{what}_{j}") for j in JOBS] for what in ("w_in", "w_pre", "w_hi", "w_lo"))
        w_sum = sem("w_sum")
        ln_bst, ln_mv, ln_lg, ln_rsd, ln_x, ln_t, ln_hi, ln_lo = (sem(n) for n in (
            "ln_bst", "ln_mv", "ln_lg", "ln_rsd", "ln_x", "ln_t", "ln_hi", "ln_lo"))
        qkw_set = sem("qkw_set")
        q_mm, q_sq, q_ss, q_lg, q_rs, q_n, q_w, q_t, q_out = (sem(n) for n in (
            "q_mm", "q_sq", "q_ss", "q_lg", "q_rs", "q_n", "q_w", "q_t", "q_out"))
        rem_pe, rem_act, rem_dve = sem("rem_pe"), sem("rem_act"), sem("rem_dve")
        not_mask = sem("not_mask")
        ctx_in = [sem("ctx_in0"), sem("ctx_in1")]
        ctx_t, ctx_hi, ctx_lo = sem("ctx_t"), sem("ctx_hi"), sem("ctx_lo")
        k_mm, k_sq, k_ss, k_lg, k_rs, k_n, k_t, k_hi, k_lo, k_rem = (sem(n) for n in (
            "k_mm", "k_sq", "k_ss", "k_lg", "k_rs", "k_n", "k_t", "k_hi", "k_lo", "k_rem"))
        v_mm, v_hi, v_lo = sem("v_mm"), sem("v_hi"), sem("v_lo")
        qb_hi, qb_lo = sem("qb_hi"), sem("qb_lo")
        sc_mm, sc_m, sc_max, sc_exp, sc_step, p_n, p_r = (sem(n) for n in (
            "sc_mm", "sc_m", "sc_max", "sc_exp", "sc_step", "p_n", "p_r"))
        p_t, p_rt, p_hi, p_lo, p_rc, o_mm, o_out = (sem(n) for n in (
            "p_t", "p_rt", "p_hi", "p_lo", "p_rc", "o_mm", "o_out"))
        oT_hi, oT_lo, xo_mm, x1_add = sem("oT_hi"), sem("oT_lo"), sem("xo_mm"), sem("x1_add")
        bn_in = [sem(f"bn_in{i}") for i in range(3)]
        bn_lg, bn_rs, bn_a, bn_ma, bn_c = (sem(n) for n in ("bn_lg", "bn_rs", "bn_a", "bn_ma", "bn_c"))
        z_mm, z_c, z_sig = sem("z_mm"), sem("z_c"), sem("z_sig")
        t_step, t_pe, t_act = sem("t_step"), sem("t_pe"), sem("t_act")
        av_mm, av_hi, av_lo, ao_mm, bo_add, x2_add = (sem(n) for n in (
            "av_mm", "av_hi", "av_lo", "ao_mm", "bo_add", "x2_add"))
        gw_hi, gw_lo, g_mm, g_step, g_exp = (sem(n) for n in ("gw_hi", "gw_lo", "g_mm", "g_step", "g_exp"))
        e_in = [sem("e_in0"), sem("e_in1")]
        e_hi, e_lo, g_col = sem("e_hi"), sem("e_lo"), sem("g_col")
        u_mm, u_sig, u_z, u_h, h_t, h_hi, h_lo, y_mm, y_add = (sem(n) for n in (
            "u_mm", "u_sig", "u_z", "u_h", "h_t", "h_hi", "h_lo", "y_mm", "y_add"))
        stored = sem("stored")

        jobs = {
            "xq": (chunked(xWq), w_slot[:, 0]),
            "xk": (chunked(xWkv[:, 0:D]), wkv[:, :, :, 0:D]),
            "xv": (chunked(xWkv[:, D:2 * D]), wkv[:, :, :, D:2 * D]),
            "xo": (chunked(xWo), w_slot[:, 1]),
            "aq": (chunked(aWq), w_slot[:, 0]),
            "ak": (chunked(aWk), w_slot[:, 1]),
            "av": (chunked(aWv), w_slot[:, 0]),
            "ao": (chunked(aWo), w_slot[:, 1]),
        }
        JOB = {n: i for i, n in enumerate(JOBS)}
        bn_src = ((gq, bq, mq, vq), (gk, bk, mk, vk), (gv, bv, mv, vv))
        bn_ac = ((qkw[:, 0, :], qkw[:, 1, :]),
                 (s_m[:, :, :].rearrange("p g m -> p (g m)")[:, 0:D], prob[:, :, :].rearrange("p g m -> p (g m)")[:, 0:D]),
                 (qkw[:, 0, :], qkw[:, 1, :]))
        heads = lambda ap: ap.rearrange("p (h d) -> p h d", h=H)
        per_head = lambda ap: ap.unsqueeze(2).broadcast_to([P, H, HD])

        dt_all = xn[:, :, :].rearrange("p u d -> p (u d)").rearrange("p (t n) -> p t n", t=TILES)
        a_all = kn[:, :, :].rearrange("p u d -> p (u d)").rearrange("p (t n) -> p t n", t=TILES)
        pAV = (pP[:, :, :].rearrange("p t n -> p (t n)").rearrange("p (c n) -> p c n", c=C),
               pV1[:, :].rearrange("p (c n) -> p c n", c=C))
        pY = (pV1[:, :], pP[:, :, :].rearrange("p t n -> p (t n)"))
        p_gate = pS[:, 0, 0:TILES * E].rearrange("p (t e) -> p t e", t=TILES)
        cmp_gt = s_m[:, :, :].rearrange("p g m -> p (g m)")[:, 0:TILES * E * E].rearrange(
            "p (t e j) -> p t e j", t=TILES, e=E)
        cmp_eq = prob[:, :, :].rearrange("p g m -> p (g m)")[:, 0:TILES * E * E].rearrange(
            "p (t e j) -> p t e j", t=TILES, e=E)

        block = es.enter_context(nc.Block())

        @block.sync
        def _(sp):
            def load_weight(name, freed_by=None):
                j = JOB[name]
                if freed_by is not None:
                    sp.wait_ge(w_lo[JOB[freed_by]], 1)
                    sp.wait_ge(w_hi[JOB[freed_by]], 1)
                sp.dma_start(w_raw[:, j % 2], jobs[name][0]).then_inc(w_in[j], 16)

            sp.dma_start(x_all[:, 0:2, :], x_t[:, 0:2, :]).then_inc(x_in[0], 16)
            load_weight("xq")
            sp.dma_start(x_all[:, 2:TILES, :], x_t[:, 2:TILES, :]).then_inc(x_in[1], 16)
            sp.dma_start(qkw[:, 0, :], spread(qn_w.rearrange("h d -> (h d)"))).then_inc(qn_in, 16)
            sp.dma_start(qkw[:, 1, :], spread(kn_w.rearrange("h d -> (h d)"))).then_inc(kn_in, 16)
            load_weight("xk")
            sp.wait_ge(const_set, 1)
            sp.dma_start(v_rem[0:B, :], ctx[:, M - 1, :]).then_inc(rem_in, 16)
            for g in range(HG):
                sp.dma_start(masked[g * S:(g + 1) * S], mask.rearrange("b s m -> s b m")).then_inc(mask_in, 16)
            load_weight("xv", "xq")
            for b in range(2):
                sp.dma_start(ctx_raw[:, b], ctx[b, 0:MT * P, :].rearrange("(t p) d -> p t d", p=P)).then_inc(ctx_in[b], 16)
            sp.dma_start(gw_raw[:, :, :], chunked(gate_w)).then_inc(gate_in, 16)
            load_weight("xo", "xk")
            load_weight("aq", "xv")

            with sp.Fori(0, (B - 2) // 2) as k:
                for u in range(2):
                    sp.wait_ge(ctx_t, (k * 2 + u + 1) * MT)
                    src = ctx[bass.ds(k * 2 + u + 2, 1), 0:MT * P, :].rearrange("b (t p) d -> p (b t) d", p=P)
                    sp.dma_start(ctx_raw[:, u], src).then_inc(ctx_in[u], 16)
            sp.wait_ge(sc_m, B)
            for w in range(3):
                if w:
                    sp.wait_ge(bn_c, w)
                for i in range(4):
                    sp.dma_start(bn_vec[:, i, :], spread(bn_src[w][i])).then_inc(bn_in[w], 16)
                if w == 0:
                    load_weight("ak", "xo")
                    sp.wait_ge(o_mm, B)
                    sp.dma_start(v_rem[:, :], spread(bo)).then_inc(bo_in, 16)
                if w == 1:
                    load_weight("av", "aq")
            load_weight("ao", "ak")
            for n in ("av", "ao"):
                sp.wait_ge(w_hi[JOB[n]], 1)
                sp.wait_ge(w_lo[JOB[n]], 1)

            def load_expert(e, u):
                w13 = e_raw[:, u, 0:C * D].rearrange("p (c n) -> p c n", c=C)
                for lo, w in ((0, w1), (F, w3)):
                    sp.dma_start(w13[:, :, lo:lo + F],
                                 w[bass.ds(e, 1)].rearrange("e (c p) f -> p (e c) f", p=P)).then_inc(e_in[u], 16)
                sp.dma_start(e_raw[:, u, C * D:RAW].rearrange("p (c n) -> p c n", c=2),
                             w2[bass.ds(e, 1)].rearrange("e (c p) d -> p (e c) d", p=P)).then_inc(e_in[u], 16)

            load_expert(0, 0)
            load_expert(1, 1)
            with sp.Fori(0, (E - 2) // 2) as k:
                for u in range(2):
                    sp.wait_ge(e_hi, (k * 2 + u) + 1)
                    sp.wait_ge(e_lo, (k * 2 + u) + 1)
                    load_expert(k * 2 + u + 2, u)
            for t in range(TILES):
                sp.wait_ge(y_add, (E - 1) * TILES + t + 1)
                sp.dma_start(out_t[:, t, :], x_all[:, t, :]).then_inc(stored, 16)
            sp.wait_ge(stored, 16 * TILES)

        @block.gpsimd
        def _(pool):
            nc.gpsimd.memset(v_rem[:, :], 0.0).then_inc(const_set, 1)
            nc.gpsimd.memset(ident[:, :], 0.0).then_inc(ident_step, 1)
            nc.gpsimd.memset(ones[:, :], 1.0)
            nc.gpsimd.memset(same_seq[:, :], 0.0)
            nc.gpsimd.memset(bias[:, 0:1], LN_EPS)
            nc.gpsimd.memset(bias[:, 1:2], HEAD_EPS)
            nc.gpsimd.memset(bias[:, 2:3], BN_EPS)
            nc.gpsimd.memset(bias[:, 3:4], -SLOPE * V_TH)
            nc.gpsimd.memset(kT[:, :, :, M:M + 1].bitcast(F32), 0.0)
            nc.gpsimd.memset(qblk[:, :, :, :].bitcast(F32), 0.0)
            nc.gpsimd.memset(tri[:, :, :], 1.0)
            nc.gpsimd.iota(col[:, :], [[1, P]], base=0, channel_multiplier=0, allow_small_or_imprecise_dtypes=True).then_inc(ident_step, 1)
            pool.wait_ge(ident_step, 2)
            for g in range(BT):
                nc.gpsimd.memset(same_seq[g * S:(g + 1) * S, g * S:(g + 1) * S], 1.0).then_inc(ident_step, 1)
                pool.wait_ge(ident_step, 3 + g)
            nc.gpsimd.affine_select(out=tri[:, :, :], in_=tri[:, :, :], compare_op=ALU.is_ge, fill=0.0, base=-1,
                                    pattern=[[1, E], [-1, E]], channel_multiplier=0)
            nc.gpsimd.affine_select(out=ident[:, :], in_=ident[:, :], compare_op=ALU.not_equal, fill=1.0, base=0,
                                    pattern=[[-1, P]], channel_multiplier=1).then_inc(const_set, 1)

            def low_part(name):
                j = JOB[name]
                pool.wait_ge(w_hi[j], 1)
                dst = jobs[name][1]
                nc.gpsimd.tensor_tensor(dst[:, LO], w_raw[:, j % 2], dst[:, HI].bitcast(F32),
                                        ALU.subtract).then_inc(w_lo[j], 1)

            for name in JOBS[:3]:
                low_part(name)
            pool.wait_ge(mask_in, 16 * HG)
            nc.gpsimd.tensor_scalar(mask_f[:, :].bitcast(U8), mask_f[:, :].bitcast(U8), -1.0, 1.0,
                                    ALU.mult, ALU.add).then_inc(not_mask, 1)
            for name in JOBS[3:6]:
                low_part(name)
            pool.wait_ge(bo_in, 16)
            for t in range(TILES):
                pool.wait_ge(ln_x, TILES + t + 1)
                nc.gpsimd.tensor_tensor(x_all[:, t, :], x_all[:, t, :], v_rem[:, :], ALU.add).then_inc(bo_add, 1)
            for name in JOBS[6:]:
                low_part(name)

            def expert_low(e, u):
                pool.wait_ge(e_hi, e + 1)
                nc.gpsimd.tensor_tensor(e_p[u][:, LO, :], e_raw[:, u, :], e_p[u][:, HI, :].bitcast(F32),
                                        ALU.subtract).then_inc(e_lo, 1)

            expert_low(0, 0)
            with pool.Fori(0, (E - 2) // 2) as k:
                expert_low(k * 2 + 1, 1)
                expert_low(k * 2 + 2, 0)
            expert_low(E - 1, 1)

        @block.scalar
        def _(act):
            def ln_root(n):
                act.wait_ge(ln_mv, n + 1)
                act.activation(ln_log[:, n % 2], mean_var[:, n % 2, 1:2], ACT.Ln, bias=LN_B).then_inc(ln_lg, 1)
                act.wait_ge(ln_lg, n + 1)
                act.activation(ln_rs[:, n % 2], ln_log[:, n % 2], ACT.Exp, scale=-0.5).then_inc(ln_rsd, 1)

            def ln_high(n, dst):
                act.wait_ge(ln_t, n + 1)
                act.activation(dst, pTT[n % 2][:, :, :], ACT.Copy).then_inc(ln_hi, 1)

            def high_part(name):
                j = JOB[name]
                if name in ("xv", "xo", "ao"):
                    act.wait_ge(w_in[j], 16)
                else:
                    act.wait_ge(w_pre[j], 1)
                act.activation(jobs[name][1][:, HI], w_raw[:, j % 2], ACT.Copy).then_inc(w_hi[j], 1)

            act.wait_ge(const_set, 2)
            ln_root(0)
            high_part("xq")
            for s in range(TILES + 2):
                if s + 1 < TILES:
                    ln_root(s + 1)
                if s < TILES:
                    if s >= 2:
                        act.wait_ge(q_mm, s - 1)
                    ln_high(s, lhs_p[:, s % 2, HI])
                t = s - 1
                if 0 <= t < TILES:
                    act.wait_ge(q_mm, t + 1)
                    if t >= 2:
                        act.wait_ge(q_ss, t - 1)
                    act.activation(sq[:, t % 2], pKV[t % 2][:, :], ACT.Square).then_inc(q_sq, 1)
                    act.wait_ge(q_ss, t + 1)
                    act.activation(head_log[:, t % 2], head_ss[:, t % 2], ACT.Ln, bias=HEAD_B,
                                   scale=1.0 / HD).then_inc(q_lg, 1)
                    act.wait_ge(q_lg, t + 1)
                    if t >= 2:
                        act.wait_ge(q_n, t - 1)
                    act.activation(head_rs[:, t % 2], head_log[:, t % 2], ACT.Exp, scale=-0.5).then_inc(q_rs, 1)
                if s == 3:
                    high_part("xk")
                if s == 6:
                    high_part("xv")
                t = s - 2
                if t >= 0:
                    act.wait_ge(q_t, t + 1)
                    act.activation(qoT[:, :, t * P:(t + 1) * P], pS[:, t % 2, :].rearrange("p (c n) -> p c n", c=C),
                                   ACT.Copy).then_inc(q_out, 1)
            act.wait_ge(rem_pe, 1)
            act.activation(ctxT[:, 0, HI, :, 0:P], pT0[:, :, :], ACT.Copy).then_inc(rem_act, 1)
            act.wait_ge(rem_pe, 2)
            act.activation(sq[:, 0], pK0[:, :], ACT.Square).then_inc(rem_act, 1)
            act.wait_ge(rem_dve, 2)
            act.activation(head_log[:, 0], head_ss[:, 0], ACT.Ln, bias=HEAD_B, scale=1.0 / HD).then_inc(rem_act, 1)
            act.wait_ge(rem_act, 3)
            act.activation(head_rs[:, 0], head_log[:, 0], ACT.Exp, scale=-0.5).then_inc(rem_act, 1)
            act.wait_ge(rem_pe, 3)
            act.activation(v_rem[:, :], pK1[:, :], ACT.Copy).then_inc(rem_act, 1)
            act.wait_ge(rem_pe, 4)
            act.activation(kT_rem[:, :, :], pT1[:, :, 0:B], ACT.Copy).then_inc(rem_act, 1)

            def ctx_high(n, u):
                for t in range(MT):
                    act.wait_ge(ctx_t, n * MT + t + 1)
                    act.activation(ctxT[:, u, HI, :, t * P:(t + 1) * P], pTT[t][:, :, :], ACT.Copy).then_inc(ctx_hi, 1)

            def k_root(b, t):
                act.wait_ge(k_ss, b * MT + t + 1)
                act.activation(head_log[:, t], head_ss[:, t], ACT.Ln, bias=HEAD_B, scale=1.0 / HD).then_inc(k_lg, 1)
                act.wait_ge(k_lg, b * MT + t + 1)
                act.activation(head_rs[:, t], head_log[:, t], ACT.Exp, scale=-0.5).then_inc(k_rs, 1)

            def batch(b, u, main=True, prev=True, nxt=True):
                if main:
                    act.wait_ge(k_mm, b * MT + 1)
                    act.activation(sq[:, 0], pK0[:, :], ACT.Square).then_inc(k_sq, 1)
                    k_root(b, 0)
                if prev:
                    act.wait_ge(sc_max, b)
                    if main is False or not isinstance(b, int) or b >= 2:
                        act.wait_ge(p_rt, b - 1)
                    for g in range(G):
                        act.activation(prob[:, g, 0:M], s_m[:, g, 0:M], ACT.Exp, bias=neg_max[:, g:g + 1],
                                       accum_out=p_sum[:, g:g + 1]).then_inc(sc_exp, 1)
                if main:
                    act.wait_ge(k_mm, b * MT + 2)
                    act.activation(sq[:, 1], pK1[:, :], ACT.Square).then_inc(k_sq, 1)
                if nxt:
                    if prev:
                        act.wait_ge(v_mm, b * MT)
                    ctx_high(b + 1, 1 - u)
                if main:
                    k_root(b, 1)
                    act.wait_ge(v_mm, b * MT + 1)
                    if prev:
                        act.wait_ge(o_mm, b - 1)
                    act.activation(v_p[:, u, HI, 0, :], pK0[:, :], ACT.Copy).then_inc(v_hi, 1)
                if prev:
                    act.wait_ge(p_t, b)
                    act.wait_ge(o_mm, b - 1)
                    act.activation(pT[:, HI], pP[:, :, :], ACT.Copy).then_inc(p_hi, 1)
                    act.wait_ge(p_rt, b)
                    act.activation(pT_rem[:, :], pS[:, 1, 0:G * P], ACT.Copy).then_inc(p_rc, 1)
                if main:
                    act.wait_ge(v_mm, b * MT + 2)
                    act.activation(v_p[:, u, HI, 1, :], pV1[:, :], ACT.Copy).then_inc(v_hi, 1)
                    for t in range(MT):
                        act.wait_ge(k_t, b * MT + t + 1)
                        if prev and t == 0:
                            act.wait_ge(sc_mm, b)
                        act.activation(kT[:, HI, :, t * P:(t + 1) * P], pTT[t][:, :, :], ACT.Copy).then_inc(k_hi, 1)

            act.wait_ge(rem_pe, 3)
            ctx_high(0, 0)
            batch(0, 0, prev=False)
            high_part("xo")
            with act.Fori(0, (B - 2) // 2) as k:
                batch(k * 2 + 1, 1)
                batch(k * 2 + 2, 0)
            batch(B - 1, 1, nxt=False)
            batch(B, 0, main=False, nxt=False)

            def bn_root(w):
                act.wait_ge(bn_in[w], 64)
                act.activation(bn_vec[:, 3, :], bn_vec[:, 3, :], ACT.Ln, bias=BN_B).then_inc(bn_lg, 1)
                act.wait_ge(bn_lg, w + 1)
                act.activation(bn_vec[:, 3, :], bn_vec[:, 3, :], ACT.Exp, scale=-0.5).then_inc(bn_rs, 1)

            act.wait_ge(o_out, B * 2)
            for s in range(TILES + 2):
                if s < TILES:
                    if s >= 2:
                        act.wait_ge(xo_mm, s - 1)
                    act.activation(lhs_p[:, s % 2, HI], qoT[:, :, s * P:(s + 1) * P], ACT.Copy).then_inc(oT_hi, 1)
                if 0 <= s - 1 < TILES:
                    ln_root(TILES + s - 1)
                if s - 2 >= 0:
                    t = s - 2
                    ln_high(TILES + t, xT[:, HI, :, t * P:(t + 1) * P])
                if s == 1:
                    bn_root(0)
                if s == 5:
                    high_part("aq")
            bn_root(1)
            act.wait_ge(xo_mm, TILES)
            high_part("ak")
            for n in range(3 * TILES):
                w, t = divmod(n, TILES)
                act.wait_ge(z_c, n + 1)
                if w < 2:
                    act.wait_ge(ln_t, 2 * TILES)
                    if n >= 2:
                        act.wait_ge(z_sig, n - 1)
                    act.activation(xn[:, n % 2], sq[:, n % 2], ACT.Sigmoid, bias=SIG_B, scale=SLOPE,
                                   accum_out=rows[:, w, t:t + 1]).then_inc(z_sig, 1)
                else:
                    act.activation(v_self[:, t], sq[:, n % 2], ACT.Sigmoid, bias=SIG_B, scale=SLOPE).then_inc(z_sig, 1)
                if n == TILES + 1:
                    bn_root(2)
                    high_part("av")
            act.wait_ge(t_step, TILES + 4)
            act.activation(kn[:, :, :], kn[:, :, :], ACT.Exp, scale=-1.0 / TAU).then_inc(t_act, 1)
            high_part("ao")
            act.wait_ge(gate_in, 16)
            act.activation(gw_p[:, HI], gw_raw[:, :, :], ACT.Copy).then_inc(gw_hi, 1)
            for s in range(TILES + 2):
                if s < TILES:
                    act.wait_ge(av_mm, s + 1)
                    if s >= 2:
                        act.wait_ge(ao_mm, s - 1)
                    act.activation(lhs_p[:, s % 2, HI], pAV[s % 2], ACT.Copy).then_inc(av_hi, 1)
                if 0 <= s - 1 < TILES:
                    ln_root(2 * TILES + s - 1)
                if s - 2 >= 0:
                    t = s - 2
                    ln_high(2 * TILES + t, xT[:, HI, :, t * P:(t + 1) * P])
            act.wait_ge(g_step, 2)
            act.activation(gates[:, :, :], g_tmp[:, :, :], ACT.Exp).then_inc(g_exp, 1)

            def expert_high(e, u, turn):
                act.wait_ge(e_in[u], turn * 48)
                act.activation(e_p[u][:, HI, :], e_raw[:, u, :], ACT.Copy).then_inc(e_hi, 1)

            expert_high(0, 0, 1)

            def expert(e, u, prev=True, nxt=None):
                act.wait_ge(g_col, e + 1)
                for t in range(TILES):
                    act.wait_ge(u_mm, e * TILES + t + 1)
                    if prev or t >= 2:
                        act.wait_ge(u_h, e * TILES + t - 1)
                    sg = sq[:, t % 2, 0:F]
                    act.activation(sg, pKV[t % 2][:, 0:F], ACT.Silu, scale=g_now[:, u, t:t + 1]).then_inc(u_sig, 1)
                    if prev or t >= 1:
                        hidden_high(e * TILES + t - 1, (t - 1) % 2, prev or t >= 3)
                    if nxt is not None and t == 3:
                        act.wait_ge(y_mm, e * TILES)
                        expert_high(e + 1, 1 - u, nxt)

            def hidden_high(n, u, reused):
                act.wait_ge(h_t, n + 1)
                if reused:
                    act.wait_ge(y_mm, n - 1)
                act.activation(hT[:, u, HI], pTT[u][:, 0:2, :], ACT.Copy).then_inc(h_hi, 1)

            expert(0, 0, prev=False, nxt=1)
            with act.Fori(0, (E - 2) // 2) as k:
                expert(k * 2 + 1, 1, nxt=k + 2)
                expert(k * 2 + 2, 0, nxt=k + 2)
            expert(E - 1, 1)
            hidden_high(E * TILES - 1, 1, True)

        @block.vector
        def _(dve):
            tt, ts, stt = nc.vector.tensor_tensor, nc.vector.tensor_scalar, nc.vector.scalar_tensor_tensor

            def ln_stats(n, src):
                nc.vector.bn_stats(bst[:, n % 2], src).then_inc(ln_bst, 1)
                dve.wait_ge(ln_bst, n + 1)
                nc.vector.bn_aggr(mean_var[:, n % 2], bst[:, n % 2]).then_inc(ln_mv, 1)

            def ln_norm(n, src):
                dve.wait_ge(ln_rsd, n + 1)
                if n >= 2:
                    dve.wait_ge(ln_t, n - 1)
                ts(xn[:, n % 2], src, mean_var[:, n % 2, 0:1], ln_rs[:, n % 2], ALU.subtract,
                   ALU.mult).then_inc(ln_x, 1)

            def ln_low(n, dst_lo, dst_hi):
                dve.wait_ge(ln_hi, n + 1)
                tt(dst_lo, pTT[n % 2][:, :, :], dst_hi.bitcast(F32), ALU.subtract).then_inc(ln_lo, 1)

            def centre(name, k):
                j = JOB[name]
                dve.wait_ge(w_in[j], 16)
                w = w_raw[:, j % 2].rearrange("p c (h d) -> p (c h) d", d=HD)
                hm = head_mean[:, :, :].rearrange("p c h -> p (c h)")
                nc.vector.tensor_reduce(hm, w, AX.X, ALU.add).then_inc(w_sum, 1)
                dve.wait_ge(w_sum, k)
                stt(w, hm.unsqueeze(2).broadcast_to([P, C * H, HD]), -1.0 / HD, w, ALU.mult,
                    ALU.add).then_inc(w_pre[j], 1)

            dve.wait_ge(const_set, 2)
            dve.wait_ge(x_in[0], 16)
            ln_stats(0, x_all[:, 0])
            ln_norm(0, x_all[:, 0])
            centre("xq", 1)
            dve.wait_ge(qn_in, 16)
            dve.wait_ge(kn_in, 16)
            stt(qkw[:, 0, :], qkw[:, 0, :], SCALE, qkw[:, 1, :], ALU.mult, ALU.mult).then_inc(qkw_set, 1)
            for s in range(TILES + 1):
                if s + 1 < TILES:
                    if s == 1:
                        dve.wait_ge(x_in[1], 16)
                    ln_stats(s + 1, x_all[:, s + 1])
                    ln_norm(s + 1, x_all[:, s + 1])
                if s < TILES:
                    ln_low(s, lhs_p[:, s % 2, LO], lhs_p[:, s % 2, HI])
                t = s - 1
                if t >= 0:
                    dve.wait_ge(q_sq, t + 1)
                    nc.vector.tensor_reduce(head_ss[:, t % 2], heads(sq[:, t % 2]), AX.X, ALU.add).then_inc(q_ss, 1)
                    dve.wait_ge(q_rs, t + 1)
                    if t >= 2:
                        dve.wait_ge(q_t, t - 1)
                    tt(heads(kn[:, t % 2]), heads(pKV[t % 2][:, :]), per_head(head_rs[:, t % 2]),
                       ALU.mult).then_inc(q_n, 1)
                    dve.wait_ge(q_n, t + 1)
                    if t == 0:
                        dve.wait_ge(qkw_set, 1)
                    tt(kn[:, t % 2], kn[:, t % 2], qkw[:, 0, :], ALU.mult).then_inc(q_w, 1)
                if s == 1:
                    centre("xk", 2)
            dve.wait_ge(rem_act, 1)
            tt(ctxT[:, 0, LO, :, 0:P], pT0[:, :, :], ctxT[:, 0, HI, :, 0:P].bitcast(F32),
               ALU.subtract).then_inc(rem_dve, 1)
            dve.wait_ge(rem_act, 2)
            nc.vector.tensor_reduce(head_ss[:, 0], heads(sq[:, 0]), AX.X, ALU.add).then_inc(rem_dve, 1)
            dve.wait_ge(rem_act, 4)
            dve.wait_ge(q_t, TILES)
            tt(heads(kn[:, 0]), heads(pK0[:, :]), per_head(head_rs[:, 0]), ALU.mult).then_inc(rem_dve, 1)

            def ctx_low(n, u):
                for t in range(MT):
                    dve.wait_ge(ctx_hi, n * MT + t + 1)
                    tt(ctxT[:, u, LO, :, t * P:(t + 1) * P], pTT[t][:, :, :],
                       ctxT[:, u, HI, :, t * P:(t + 1) * P].bitcast(F32), ALU.subtract).then_inc(ctx_lo, 1)

            def k_sum(b, t):
                dve.wait_ge(k_sq, b * MT + t + 1)
                nc.vector.tensor_reduce(head_ss[:, t], heads(sq[:, t]), AX.X, ALU.add).then_inc(k_ss, 1)

            def k_norm(b, t, prev):
                dve.wait_ge(k_rs, b * MT + t + 1)
                if prev:
                    dve.wait_ge(k_t, b * MT + t - 1)
                tt(heads(kn[:, t]), heads(pKV[t][:, :]), per_head(head_rs[:, t]), ALU.mult).then_inc(k_n, 1)

            def v_low(b, t, u, bank):
                dve.wait_ge(v_hi, b * MT + t + 1)
                tt(v_p[:, u, LO, t, :], bank[:, :], v_p[:, u, HI, t, :].bitcast(F32), ALU.subtract).then_inc(v_lo, 1)

            def batch(b, u, main=True, prev=True, nxt=True):
                p = b - 1
                if main:
                    k_sum(b, 0)
                if prev:
                    dve.wait_ge(sc_mm, b)
                    stt(s_m[:, :, 0:M], masked[:, bass.ds(p, 1), :].broadcast_to([P, G, M]), -BIG,
                        pS[:, :, 0:M], ALU.mult, ALU.add).then_inc(sc_m, 1)
                    dve.wait_ge(sc_m, b)
                    nc.vector.tensor_reduce(neg_max[:, :], s_m[:, :, 0:M], AX.X, ALU.max, negate=True).then_inc(sc_max, 1)
                if main:
                    k_norm(b, 0, prev)
                if prev:
                    dve.wait_ge(sc_exp, b * G)
                    stt(p_den[:, :], neg_max[:, :], BIG / 2, p_sum[:, :], ALU.is_lt, ALU.mult).then_inc(sc_step, 1)
                    dve.wait_ge(sc_step, p * 3 + 1)
                    nc.vector.reciprocal(p_inv[:, :], p_den[:, :]).then_inc(sc_step, 1)
                    dve.wait_ge(sc_step, p * 3 + 2)
                    stt(p_scale[:, :], neg_max[:, :], BIG / 2, p_inv[:, :], ALU.is_lt, ALU.mult).then_inc(sc_step, 1)
                    dve.wait_ge(sc_step, p * 3 + 3)
                    for g in range(G):
                        ts(prob[:, g, 0:M], prob[:, g, 0:M], p_scale[:, g:g + 1], None, ALU.mult).then_inc(p_n, 1)
                    dve.wait_ge(p_n, b * G)
                    if main is False or not isinstance(b, int) or b >= 2:
                        dve.wait_ge(p_rt, p)
                    for g in range(G):
                        ts(p_rem[:, g, :], col[:, :], col[:, bass.ds(p, 1)], prob[:, g, M - 1:M], ALU.is_equal,
                           ALU.mult).then_inc(p_r, 1)
                if main:
                    k_sum(b, 1)
                if nxt:
                    ctx_low(b + 1, 1 - u)
                if main:
                    k_norm(b, 1, prev)
                    v_low(b, 0, u, pK0)
                if prev:
                    dve.wait_ge(p_hi, b)
                    tt(pT[:, LO], pP[:, :, :], pT[:, HI].bitcast(F32), ALU.subtract).then_inc(p_lo, 1)
                if main:
                    if prev:
                        dve.wait_ge(sc_mm, b)
                    for r in range(2):
                        a = slice(r * HD, (r + 1) * HD)
                        ts(qblk[a, HI, :, r * S:(r + 1) * S], qoT[a, :, bass.ds(b * S, S)], 1.0, None,
                           ALU.mult).then_inc(qb_hi, 1)
                    dve.wait_ge(qb_hi, b * 2 + 2)
                    for r in range(2):
                        a = slice(r * HD, (r + 1) * HD)
                        tt(qblk[a, LO, :, r * S:(r + 1) * S], qoT[a, :, bass.ds(b * S, S)],
                           qblk[a, HI, :, r * S:(r + 1) * S].bitcast(F32), ALU.subtract).then_inc(qb_lo, 1)
                    v_low(b, 1, u, pV1)
                    ts(kT[:, HI, :, M - 1:M], kT_rem[:, :, bass.ds(b, 1)], 1.0, None, ALU.mult).then_inc(k_rem, 1)
                    dve.wait_ge(k_rem, b * 2 + 1)
                    tt(kT[:, LO, :, M - 1:M], kT_rem[:, :, bass.ds(b, 1)], kT[:, HI, :, M - 1:M].bitcast(F32),
                       ALU.subtract).then_inc(k_rem, 1)
                    for t in range(MT):
                        dve.wait_ge(k_hi, b * MT + t + 1)
                        tt(kT[:, LO, :, t * P:(t + 1) * P], pTT[t][:, :, :],
                           kT[:, HI, :, t * P:(t + 1) * P].bitcast(F32), ALU.subtract).then_inc(k_lo, 1)
                if prev:
                    dve.wait_ge(o_mm, b)
                    for r in range(2):
                        a = slice(r * HD, (r + 1) * HD)
                        o = pS[a, 0, 0:G * P].rearrange("p (c n) -> p c n", c=C)[:, :, r * S:(r + 1) * S]
                        ts(qoT[a, :, bass.ds(p * S, S)], o, 1.0, None, ALU.mult).then_inc(o_out, 1)

            dve.wait_ge(q_out, TILES)
            dve.wait_ge(rem_act, 6)
            dve.wait_ge(rem_pe, 4)
            ctx_low(0, 0)
            batch(0, 0, prev=False)
            dve.wait_ge(not_mask, 1)
            with dve.Fori(0, (B - 2) // 2) as k:
                batch(k * 2 + 1, 1)
                batch(k * 2 + 2, 0)
            batch(B - 1, 1, nxt=False)
            batch(B, 0, main=False, nxt=False)

            def bn_fold(w):
                j = JOB[("aq", "ak", "av")[w]]
                a, c = bn_ac[w]
                dve.wait_ge(bn_rs, w + 1)
                tt(a, bn_vec[:, 0, :], bn_vec[:, 3, :], ALU.mult).then_inc(bn_a, 1)
                dve.wait_ge(bn_a, w + 1)
                tt(bn_vec[:, 2, :], bn_vec[:, 2, :], a, ALU.mult).then_inc(bn_ma, 1)
                dve.wait_ge(bn_ma, w + 1)
                tt(c, bn_vec[:, 1, :], bn_vec[:, 2, :], ALU.subtract).then_inc(bn_c, 1)
                dve.wait_ge(w_in[j], 16)
                tt(w_raw[:, j % 2], w_raw[:, j % 2], a.unsqueeze(1).broadcast_to([P, C, D]),
                   ALU.mult).then_inc(w_pre[j], 1)

            dve.wait_ge(o_out, B * 2)
            for s in range(TILES + 2):
                if s < TILES:
                    dve.wait_ge(oT_hi, s + 1)
                    tt(lhs_p[:, s % 2, LO], qoT[:, :, s * P:(s + 1) * P], lhs_p[:, s % 2, HI].bitcast(F32),
                       ALU.subtract).then_inc(oT_lo, 1)
                t = s - 1
                if 0 <= t < TILES:
                    dve.wait_ge(xo_mm, t + 1)
                    tt(x_all[:, t], x_all[:, t], pKV[t % 2][:, :], ALU.add).then_inc(x1_add, 1)
                    dve.wait_ge(x1_add, t + 1)
                    ln_stats(TILES + t, x_all[:, t])
                    ln_norm(TILES + t, x_all[:, t])
                t = s - 2
                if t >= 0:
                    ln_low(TILES + t, xT[:, LO, :, t * P:(t + 1) * P], xT[:, HI, :, t * P:(t + 1) * P])
                if s == 3:
                    bn_fold(0)
            bn_fold(1)
            dve.wait_ge(bn_c, 2)
            for n in range(3 * TILES):
                w, t = divmod(n, TILES)
                if n == 2 * TILES:
                    dve.wait_ge(z_sig, 2 * TILES)
                    for r in range(TILES):
                        ts(a_all[:, r, :], ident[:, :], rows[:, 0, r:r + 1], 1.0 / D, ALU.mult,
                           ALU.mult).then_inc(t_step, 1)
                    ts(rows[:, 1, :], rows[:, 1, :], 1.0 / D, None, ALU.mult).then_inc(t_step, 1)
                if n == 2 * TILES + 4:
                    dve.wait_ge(t_pe, 1)
                    dve.wait_ge(t_step, TILES + 1)
                    for g in range(2):
                        half = slice(g * C, (g + 1) * C)
                        tt(dt_all[:, half, :], rows[:, 1, half].unsqueeze(2).broadcast_to([P, C, P]),
                           pS[:, g, :].rearrange("p (t n) -> p t n", t=C), ALU.subtract).then_inc(t_step, 1)
                    dve.wait_ge(t_step, TILES + 3)
                    stt(a_all[:, :, :], dt_all[:, :, :], -1.0, dt_all[:, :, :], ALU.mult, ALU.max).then_inc(t_step, 1)
                dve.wait_ge(z_mm, n + 1)
                if n >= 2:
                    dve.wait_ge(z_sig, n - 1)
                tt(sq[:, n % 2], pZ[n % 3][:, :], bn_ac[w][1], ALU.add).then_inc(z_c, 1)
                if n == TILES + 1:
                    bn_fold(2)
                    dve.wait_ge(bn_c, 3)
            ts(dt_all[:, :, :], dt_all[:, :, :], 0.0, 2 * A_STDP, ALU.is_lt, ALU.mult).then_inc(t_step, 1)
            dve.wait_ge(t_step, TILES + 5)
            dve.wait_ge(t_act, 1)
            stt(dt_all[:, :, :], dt_all[:, :, :], -A_STDP, a_all[:, :, :], ALU.add, ALU.mult).then_inc(t_step, 1)
            dve.wait_ge(t_step, TILES + 6)
            stt(a_all[:, :, :], dt_all[:, :, :], W_OFF, same_seq[:, :].unsqueeze(1).broadcast_to([P, TILES, P]),
                ALU.add, ALU.mult).then_inc(t_step, 1)
            dve.wait_ge(gw_hi, 1)
            tt(gw_p[:, LO], gw_raw[:, :, :], gw_p[:, HI].bitcast(F32), ALU.subtract).then_inc(gw_lo, 1)
            for s in range(TILES + 2):
                if s < TILES:
                    dve.wait_ge(av_hi, s + 1)
                    tt(lhs_p[:, s % 2, LO], pAV[s % 2], lhs_p[:, s % 2, HI].bitcast(F32), ALU.subtract).then_inc(av_lo, 1)
                t = s - 1
                if 0 <= t < TILES:
                    dve.wait_ge(ao_mm, t + 1)
                    dve.wait_ge(bo_add, t + 1)
                    tt(x_all[:, t], x_all[:, t], pKV[t % 2][:, :], ALU.add).then_inc(x2_add, 1)
                    dve.wait_ge(x2_add, t + 1)
                    ln_stats(2 * TILES + t, x_all[:, t])
                    ln_norm(2 * TILES + t, x_all[:, t])
                t = s - 2
                if t >= 0:
                    ln_low(2 * TILES + t, xT[:, LO, :, t * P:(t + 1) * P], xT[:, HI, :, t * P:(t + 1) * P])
            step = [0]

            def gate(ins):
                step[0] += 1
                ins.then_inc(g_step, 1)

            per_token = lambda ap: ap.unsqueeze(2).broadcast_to([P, TILES, E])
            dve.wait_ge(g_mm, TILES)
            gate(nc.vector.tensor_reduce(g_red[:, :], p_gate, AX.X, ALU.max))
            dve.wait_ge(g_step, 1)
            gate(tt(g_tmp[:, :, :], p_gate, per_token(g_red[:, :]), ALU.subtract))
            dve.wait_ge(g_exp, 1)
            gate(nc.vector.tensor_reduce(g_red[:, :], gates[:, :, :], AX.X, ALU.add))
            dve.wait_ge(g_step, 3)
            gate(nc.vector.reciprocal(g_red[:, :], g_red[:, :]))
            dve.wait_ge(g_step, 4)
            gate(tt(gates[:, :, :], gates[:, :, :], per_token(g_red[:, :]), ALU.mult))
            dve.wait_ge(g_step, 5)
            other = gates[:, :, :].unsqueeze(2).broadcast_to([P, TILES, E, E])
            own = gates[:, :, :].unsqueeze(3).broadcast_to([P, TILES, E, E])
            gate(tt(cmp_gt, other, own, ALU.is_gt))
            gate(tt(cmp_eq, other, own, ALU.is_equal))
            dve.wait_ge(g_step, 7)
            gate(tt(cmp_eq, cmp_eq, tri[:, :, :].unsqueeze(1).broadcast_to([P, TILES, E, E]), ALU.mult))
            dve.wait_ge(g_step, 8)
            gate(tt(cmp_gt, cmp_gt, cmp_eq, ALU.add))
            dve.wait_ge(g_step, 9)
            gate(nc.vector.tensor_reduce(g_tmp[:, :, :], cmp_gt, AX.X, ALU.add))
            dve.wait_ge(g_step, 10)
            gate(stt(gates[:, :, :], g_tmp[:, :, :], 1.5, gates[:, :, :], ALU.is_lt, ALU.mult))
            dve.wait_ge(g_step, 11)

            def hidden_low(n, u):
                dve.wait_ge(h_hi, n + 1)
                tt(hT[:, u, LO], pTT[u][:, 0:2, :], hT[:, u, HI].bitcast(F32), ALU.subtract).then_inc(h_lo, 1)

            def expert_add(n, t):
                dve.wait_ge(y_mm, n + 1)
                tt(x_all[:, t % TILES], x_all[:, t % TILES], pY[t % 2], ALU.add).then_inc(y_add, 1)

            def expert(e, u, prev=True):
                ts(g_now[:, u, :], gates[:, :, bass.ds(e, 1)].rearrange("p t e -> p (t e)"), 1.0, None,
                   ALU.mult).then_inc(g_col, 1)
                dve.wait_ge(g_col, e + 1)
                for t in range(TILES):
                    n = e * TILES + t
                    dve.wait_ge(u_sig, n + 1)
                    if prev or t >= 2:
                        dve.wait_ge(h_t, n - 1)
                    stt(xn[:, t % 2, 0:F], pKV[t % 2][:, F:2 * F], g_now[:, u, t:t + 1], sq[:, t % 2, 0:F],
                        ALU.mult, ALU.mult).then_inc(u_h, 1)
                    if prev or t >= 1:
                        hidden_low(n - 1, (t - 1) % 2)
                    if prev or t >= 2:
                        expert_add(n - 2, t - 2)

            expert(0, 0, prev=False)
            with dve.Fori(0, (E - 2) // 2) as k:
                expert(k * 2 + 1, 1)
                expert(k * 2 + 2, 0)
            expert(E - 1, 1)
            hidden_low(E * TILES - 1, 1)
            expert_add(E * TILES - 2, TILES - 2)
            expert_add(E * TILES - 1, TILES - 1)

        @block.tensor
        def _(pe):
            def ln_turn(n):
                pe.wait_ge(ln_x, n + 1)
                if n >= 2:
                    pe.wait_ge(ln_lo, n - 1)
                for c in range(C):
                    last = pe.transpose(pTT[n % 2][:, c, :], xn[:, n % 2, c * P:(c + 1) * P], ident[:, :])
                last.then_inc(ln_t, 1)

            def tile_of(buf, u):
                return lambda s, c: buf[:, u, s, c, :]

            def rows_of(buf, t):
                return lambda s, c: buf[:, s, c, t * P:(t + 1) * P]

            def weight(buf, lo=0, hi=D):
                return lambda s, c: buf[:, s, c, lo:hi]

            pe.wait_ge(const_set, 2)
            for s in range(TILES + 2):
                if s < TILES:
                    ln_turn(s)
                t = s - 1
                if 0 <= t < TILES:
                    pe.wait_ge(ln_lo, t + 1)
                    if t == 0:
                        pe.wait_ge(w_lo[JOB["xq"]], 1)
                    if t >= 2:
                        pe.wait_ge(q_n, t - 1)
                    split_products(pe, pKV[t % 2][:, :], tile_of(lhs_p, t % 2), weight(w_slot[:, 0]),
                                   C).then_inc(q_mm, 1)
                t = s - 2
                if t >= 0:
                    pe.wait_ge(q_w, t + 1)
                    if t >= 2:
                        pe.wait_ge(q_out, t - 1)
                    for c in range(C):
                        last = pe.transpose(pS[:, t % 2, c * P:(c + 1) * P], kn[:, t % 2, c * P:(c + 1) * P], ident[:, :])
                    last.then_inc(q_t, 1)
            pe.wait_ge(rem_in, 16)
            pe.wait_ge(ln_lo, TILES)
            for c in range(C):
                last = pe.transpose(pT0[:, c, :], v_rem[:, c * P:(c + 1) * P], ident[:, :])
            last.then_inc(rem_pe, 1)
            pe.wait_ge(rem_dve, 1)
            pe.wait_ge(q_n, TILES)
            pe.wait_ge(w_lo[JOB["xk"]], 1)
            ctx_rows = lambda u, t: (lambda s, c: ctxT[:, u, s, c, t * P:(t + 1) * P])
            wk, wv = weight(wkv, 0, D), weight(wkv, D, 2 * D)
            split_products(pe, pK0[:, :], ctx_rows(0, 0), wk, C).then_inc(rem_pe, 1)
            pe.wait_ge(w_lo[JOB["xv"]], 1)
            split_products(pe, pK1[:, :], ctx_rows(0, 0), wv, C).then_inc(rem_pe, 1)
            pe.wait_ge(rem_dve, 3)
            for c in range(C):
                last = pe.transpose(pT1[:, c, :], kn[:, 0, c * P:(c + 1) * P], ident[:, :])
            last.then_inc(rem_pe, 1)

            def ctx_turn(n, u, turn):
                pe.wait_ge(ctx_in[u], turn * 16)
                for t in range(MT):
                    for c in range(C):
                        last = pe.transpose(pTT[t][:, c, :], ctx_raw[:, u, t, c * P:(c + 1) * P], ident[:, :])
                    last.then_inc(ctx_t, 1)

            def batch(b, u, main=True, prev=True, turn=None):
                if main:
                    pe.wait_ge(ctx_lo, b * MT + 1)
                    if prev:
                        pe.wait_ge(v_lo, b * MT - 1)
                    split_products(pe, pK0[:, :], ctx_rows(u, 0), wk, C).then_inc(k_mm, 1)
                if prev:
                    pe.wait_ge(k_lo, b * MT)
                    if main is False or not isinstance(b, int) or b >= 2:
                        pe.wait_ge(o_out, b * 2 - 2)
                    for g in range(G):
                        for r in range(2):
                            c = 2 * g + r
                            qb = lambda s, _: qblk[:, s].rearrange("p c n -> p (c n)")[:, c * P - r * HD:(c + 1) * P - r * HD]
                            last = split_products(pe, pS[:, g, 0:M + 1], qb, lambda s, _: kT[:, s, c, :], 1,
                                                  start=r == 0, stop=r == 1)
                    last.then_inc(sc_mm, 1)
                if main:
                    pe.wait_ge(ctx_lo, b * MT + 2)
                    if prev:
                        pe.wait_ge(k_n, b * MT)
                    split_products(pe, pK1[:, :], ctx_rows(u, 1), wk, C).then_inc(k_mm, 1)
                if turn is not None:
                    ctx_turn(b + 1, 1 - u, turn)
                if main:
                    pe.wait_ge(k_n, b * MT + 1)
                    split_products(pe, pK0[:, :], ctx_rows(u, 0), wv, C).then_inc(v_mm, 1)
                if prev:
                    pe.wait_ge(p_n, b * G)
                    if main is False or not isinstance(b, int) or b >= 2:
                        pe.wait_ge(p_lo, b - 1)
                    for t in range(MT):
                        for g in range(G):
                            last = pe.transpose(pP[:, t, g * P:(g + 1) * P], prob[:, g, t * P:(t + 1) * P], ident[:, :])
                    last.then_inc(p_t, 1)
                    pe.wait_ge(p_r, b * G)
                    for g in range(G):
                        last = pe.transpose(pS[:, 1, g * P:(g + 1) * P], p_rem[:, g, :], ident[:, :])
                    last.then_inc(p_rt, 1)
                if main:
                    if prev:
                        pe.wait_ge(v_lo, b * MT)
                    split_products(pe, pV1[:, :], ctx_rows(u, 1), wv, C).then_inc(v_mm, 1)
                    pe.wait_ge(k_n, b * MT + 2)
                    pe.wait_ge(ctx_lo, (b * MT + 4) if turn is not None else (b * MT + 2))
                    for t in range(MT):
                        for c in range(C):
                            last = pe.transpose(pTT[t][:, c, :], kn[:, t, c * P:(c + 1) * P], ident[:, :])
                        last.then_inc(k_t, 1)
                if prev:
                    pe.wait_ge(p_rc, b)
                    pe.wait_ge(p_lo, b)
                    if main is False:
                        pe.wait_ge(v_lo, b * MT)
                    for c in range(C):
                        cols = slice(c * 2 * S, (c + 1) * 2 * S)
                        o = pS[:, 0, cols]
                        pe.matmul(o, v_rem[:, c * P:(c + 1) * P], pT_rem[:, cols], start=True, stop=False)
                        last = split_products(pe, o, lambda s, t: v_p[:, 1 - u, s, t, c * P:(c + 1) * P],
                                              lambda s, t: pT[:, s, t, cols], MT, start=False)
                    last.then_inc(o_mm, 1)

            pe.wait_ge(rem_act, 6)
            ctx_turn(0, 0, 1)
            batch(0, 0, prev=False, turn=1)
            pe.wait_ge(q_out, TILES)
            with pe.Fori(0, (B - 2) // 2) as k:
                batch(k * 2 + 1, 1, turn=k + 2)
                batch(k * 2 + 2, 0, turn=k + 2)
            batch(B - 1, 1)
            batch(B, 0, main=False)

            pe.wait_ge(w_lo[JOB["xo"]], 1)
            for s in range(TILES + 2):
                if s < TILES:
                    pe.wait_ge(oT_lo, s + 1)
                    if s >= 2:
                        pe.wait_ge(x1_add, s - 1)
                    split_products(pe, pKV[s % 2][:, :], tile_of(lhs_p, s % 2), weight(w_slot[:, 1]),
                                   C).then_inc(xo_mm, 1)
                if s >= 2:
                    ln_turn(TILES + s - 2)
            for n in range(3 * TILES):
                w, t = divmod(n, TILES)
                if t == 0:
                    pe.wait_ge(w_lo[JOB[("aq", "ak", "av")[w]]], 1)
                if w == 0:
                    pe.wait_ge(ln_lo, TILES + t + 1)
                if n >= 3:
                    pe.wait_ge(z_c, n - 2)
                split_products(pe, pZ[n % 3][:, :], rows_of(xT, t), weight(w_slot[:, w % 2]), C).then_inc(z_mm, 1)
                if n == 2 * TILES + 1:
                    pe.wait_ge(t_step, TILES)
                    for g in range(2):
                        last = pe.matmul(pS[:, g, :], ones[:, :],
                                         a_all[:, g * C:(g + 1) * C, :].rearrange("p t n -> p (t n)"),
                                         start=True, stop=True)
                    last.then_inc(t_pe, 1)
            pe.wait_ge(z_c, 3 * TILES)
            pe.wait_ge(z_sig, 3 * TILES)
            pe.wait_ge(t_step, TILES + 7)
            pe.wait_ge(gw_lo, 1)
            for s in range(TILES + 3):
                if s < TILES:
                    if s >= 2:
                        pe.wait_ge(av_lo, s - 1)
                    for c in range(C):
                        last = pe.matmul(pAV[s % 2][:, c, :], v_self[:, s, c * P:(c + 1) * P], a_all[:, s, :],
                                         start=True, stop=True)
                    last.then_inc(av_mm, 1)
                t = s - 1
                if 0 <= t < TILES:
                    pe.wait_ge(av_lo, t + 1)
                    if t == 0:
                        pe.wait_ge(w_lo[JOB["ao"]], 1)
                    if t >= 2:
                        pe.wait_ge(x2_add, t - 1)
                    split_products(pe, pKV[t % 2][:, :], tile_of(lhs_p, t % 2), weight(w_slot[:, 1]),
                                   C).then_inc(ao_mm, 1)
                t = s - 2
                if 0 <= t < TILES:
                    ln_turn(2 * TILES + t)
                t = s - 3
                if t >= 0:
                    pe.wait_ge(ln_lo, 2 * TILES + t + 1)
                    split_products(pe, p_gate[:, t, :], rows_of(xT, t), weight(gw_p, 0, E), C).then_inc(g_mm, 1)

            def hidden_turn(n, u, reused):
                pe.wait_ge(u_h, n + 1)
                if reused:
                    pe.wait_ge(h_lo, n - 1)
                for c in range(2):
                    last = pe.transpose(pTT[u][:, c, :], xn[:, u, c * P:(c + 1) * P], ident[:, :])
                last.then_inc(h_t, 1)

            def hidden_out(n, u, w, reused):
                pe.wait_ge(h_lo, n + 1)
                if reused:
                    pe.wait_ge(y_add, n - 1)
                w2_of = lambda s, c: e_p[w][:, s, (C + c) * D:(C + c + 1) * D]
                split_products(pe, pY[u], tile_of(hT, u), w2_of, 2).then_inc(y_mm, 1)

            def expert(e, u, prev=True):
                pe.wait_ge(e_lo, e + 1)
                w13 = lambda s, c: e_p[u][:, s, c * D:(c + 1) * D]
                for t in range(TILES):
                    n = e * TILES + t
                    if prev or t >= 2:
                        pe.wait_ge(u_h, n - 1)
                    split_products(pe, pKV[t % 2][:, :], rows_of(xT, t), w13, C).then_inc(u_mm, 1)
                    if prev or t >= 1:
                        hidden_turn(n - 1, (t - 1) % 2, prev or t >= 3)
                    if prev or t >= 2:
                        hidden_out(n - 2, t % 2, u if t >= 2 else 1 - u, prev or t >= 4)

            expert(0, 0, prev=False)
            with pe.Fori(0, (E - 2) // 2) as k:
                expert(k * 2 + 1, 1)
                expert(k * 2 + 2, 0)
            expert(E - 1, 1)
            hidden_turn(E * TILES - 1, 1, True)
            hidden_out(E * TILES - 2, 0, 1, True)
            hidden_out(E * TILES - 1, 1, 1, True)


_INS = ["x", "ctx_1024", "mask_BxSxS2_bk0", "L0_xattn_Wq", "L0_xattn_Wkv", "L0_xattn_Wo", "L0_xattn_qn_w",
        "L0_xattn_kn_w", "L0_attn_Wq", "L0_attn_gq", "L0_attn_bq", "L0_attn_mq", "L0_attn_vq", "L0_attn_Wk",
        "L0_attn_gk", "L0_attn_bk", "L0_attn_mk", "L0_attn_vk", "L0_attn_Wv", "L0_attn_gv", "L0_attn_bv",
        "L0_attn_mv", "L0_attn_vv", "L0_attn_Wo", "L0_attn_bo", "L0_ffn_gate_w", "L0_ffn_w1", "L0_ffn_w2",
        "L0_ffn_w3"]


def kernel(**inputs):
    import numpy as _np
    import concourse.bacc as _bacc
    from concourse import mybir as _mybir
    from concourse.bass_utils import run_bass_kernel_spmd as _run

    nc = _bacc.Bacc("TRN2", target_bir_lowering=False, num_devices=1)
    arrays, args = {}, []
    for name in _INS:
        a = _np.ascontiguousarray(inputs[name])
        arrays[f"in_{name}_dram"] = a
        args.append(nc.dram_tensor(f"in_{name}_dram", a.shape, _mybir.dt.from_np(a.dtype), kind="ExternalInput").ap())
    shape = inputs["x"].shape
    args.append(nc.dram_tensor("out_0_dram", shape, _mybir.dt.float32, kind="ExternalOutput").ap())
    perceiver_block(nc, *args)
    r = _run(nc, [arrays], core_ids=[0])
    return r.results[0]["out_0_dram"]
```

```python
from contextlib import ExitStack

import concourse.bass as bass
from concourse import mybir

F32 = mybir.dt.float32
F32R = mybir.dt.float32r
U8 = mybir.dt.uint8
ALU = mybir.AluOpType
ACT = mybir.ActivationFunctionType
AX = mybir.AxisListType

P = 128
HI, LO = 0, 1
BIG = 3.0e38
ROOTS = "natural_log_exp_and_others"
LN_EPS, HEAD_EPS, BN_EPS = 1e-5, 1e-6, 1e-5
V_TH, SLOPE = 1.0, 4.0
A_STDP, TAU, W_OFF = 0.9, 0.5, 0.9


def split_products(pe, out, lhs, rhs, chunks, start=True, stop=True, first=0):
    last = None
    for c in range(first, chunks):
        for n, (a, b) in enumerate(((HI, HI), (HI, LO), (LO, HI))):
            last = pe.matmul(out, lhs(a, c), rhs(b, c), start=start and c == first and n == 0,
                             stop=stop and c == chunks - 1 and n == 2)
    return last


def perceiver_block(nc, x, ctx, mask, xWq, xWkv, xWo, qn_w, kn_w, aWq, gq, bq, mq, vq, aWk, gk, bk, mk, vk,
                    aWv, gv, bv, mv, vv, aWo, bo, gate_w, w1, w2, w3, out):
    B, S, D = x.shape
    M = ctx.shape[1]
    H, HD = qn_w.shape
    E, _, F = w1.shape
    TILES = B * S // P
    C = D // P
    BT = P // S
    MT = M // P
    HG = P // S
    G = H // HG
    RAW = C * D + 2 * D
    SCALE = float(HD) ** -0.5
    assert M == MT * P + 1 and MT == 2 and G == 2 and C == 4 and 2 * HD == P and H == 8 and F == 2 * P
    assert B == TILES * BT and TILES == 8 and B % 2 == 0 and E == 8

    x_t = x.rearrange("b s d -> (b s) d").rearrange("(t p) d -> p t d", p=P)
    out_t = out.rearrange("b s d -> (b s) d").rearrange("(t p) d -> p t d", p=P)

    def chunked(w):
        return w.rearrange("(c p) n -> p c n", p=P)

    def spread(v):
        return v.partition_broadcast(P)

    with ExitStack() as es:
        def sb(name, shape, dt=F32):
            return es.enter_context(nc.sbuf_tensor(name, shape, dt))

        def ps(name, shape):
            return es.enter_context(nc.psum_tensor(name, shape, F32))

        def sem(name):
            return es.enter_context(nc.semaphore(name))

        ident = sb("ident", [P, P])
        ones = sb("ones", [P, P])
        same_seq = sb("same_seq", [P, P])
        col = sb("col", [P, P])
        batch_col = sb("batch_col", [P, P])
        x_all = sb("x_all", [P, TILES, D])
        bias = sb("bias", [P, 4])
        LN_B, HEAD_B, BN_B, SIG_B = (bias[:, i:i + 1] for i in range(4))
        xn = sb("xn", [P, 2, D])
        bst = sb("bst", [P, 2, 6])
        mean_var = sb("mean_var", [P, 2, 2])
        ln_log = sb("ln_log", [P, 2, 1])
        ln_rs = sb("ln_rs", [P, 2, 1])
        wide = sb("wide", [P, 2 * RAW])
        w_raw = wide[:, 0:2 * C * D].rearrange("p (u c n) -> p u c n", u=2, c=C)
        ctx_raw = wide[:, 2 * C * D:2 * RAW].rearrange("p (u t d) -> p u t d", u=2, t=MT)
        raw_of = {"ao": wide[:, 2 * C * D:3 * C * D].rearrange("p (c n) -> p c n", c=C)}
        e_raw = wide[:, :].rearrange("p (u n) -> p u n", u=2)
        qoT = sb("qoT", [P, C, TILES * P])
        v_self = qoT[:, :, :].rearrange("p c n -> p (c n)").rearrange("p (t d) -> p t d", t=TILES)
        sq = sb("sq", [P, 2, D])
        kn = sb("kn", [P, 2, D])
        head_ss = sb("head_ss", [P, 2, H])
        head_log = sb("head_log", [P, 2, H])
        head_rs = sb("head_rs", [P, 2, H])
        head_mean = sb("head_mean", [P, C, H])
        qkw = sb("qkw", [P, 2, D])
        kT_rem = sb("kT_rem", [P, C, B])
        rem_raw = sb("rem_raw", [P, D])
        s_m = sb("s_m", [P, G, M + 1])
        prob = sb("prob", [P, G, M + 1])
        neg_max = sb("neg_max", [P, G])
        p_sum = sb("p_sum", [P, G])
        p_den = sb("p_den", [P, G])
        p_inv = sb("p_inv", [P, G])
        p_scale = sb("p_scale", [P, G])
        p_rem = sb("p_rem", [P, G, P])
        mask_f = sb("mask_f", [P, B * M // 4])
        masked = mask_f[:, :].bitcast(U8).rearrange("p (b m) -> p b m", b=B)
        bn_vec = mask_f[:, 0:4 * D].rearrange("p (v d) -> p v d", v=4)
        rows = sb("rows", [P, 2, TILES])
        gw_raw = sb("gw_raw", [P, C, E])
        tri = sb("tri", [P, E, E])
        gates = sb("gates", [P, TILES, E])
        g_tmp = sb("g_tmp", [P, TILES, E])
        g_red = sb("g_red", [P, TILES])
        g_now = sb("g_now", [P, 2, TILES])
        parts = sb("parts", [P, 8 * C * D], F32R)
        wkv = parts[:, 0:4 * C * D].rearrange("p (s c n) -> p s c n", s=2, c=C)
        ctxT = parts[:, 4 * C * D:6 * C * D].rearrange("p (u s c n) -> p u s c n", u=2, s=2, c=C)
        ctxN = parts[:, 6 * C * D:8 * C * D].rearrange("p (u s t d) -> p u s t d", u=2, s=2, t=MT)
        xT = parts[:, 0:4 * C * D].rearrange("p (s c n) -> p s c n", s=2, c=C)
        lhs_p = parts[:, 7 * C * D:8 * C * D].rearrange("p (u s c n) -> p u s c n", u=2, s=2, c=C)
        hT = parts[:, 7 * C * D:7 * C * D + 8 * P].rearrange("p (u s c n) -> p u s c n", u=2, s=2, c=2)
        kT = sb("kT", [P, 2, C, M + 1], F32R)
        qblk = sb("qblk", [P, 2, C, P], F32R)
        pT = sb("pT", [P, 2, MT, G * P], F32R)
        w_p = sb("w_p", [P, 4 * C * D], F32R)
        w_slot = w_p[:, :].rearrange("p (u s c n) -> p u s c n", u=2, s=2, c=C)
        z_p = w_p[:, :].rearrange("p (s c n) -> p s c n", s=2, c=C)
        z_b = w_p[:, :].rearrange("p (s c h b q) -> p s c h b q", s=2, c=C, h=H, b=BT)
        rem_p = sb("rem_p", [P, D], F32R)
        pT_rem = sb("pT_rem", [P, G * P], F32R)
        gw_p = sb("gw_p", [P, 2, C, E], F32R)
        e_p = [parts[:, 4 * C * D:4 * C * D + 2 * RAW].rearrange("p (s n) -> p s n", s=2),
               w_p[:, 0:2 * RAW].rearrange("p (s n) -> p s n", s=2)]

        pK0, pK1, pV1 = ps("pK0", [P, D]), ps("pK1", [P, D]), ps("pV1", [P, D])
        pT0, pT1 = ps("pT0", [P, C, P]), ps("pT1", [P, C, P])
        pS = ps("pS", [P, G, 512])
        pP = ps("pP", [P, MT, G * P])
        pKV, pTT, pZ = (pK0, pK1), (pT0, pT1), (pK0, pK1, pV1)

        const_set = sem("const_set")
        ident_step = sem("ident_step")
        x_in = [sem("x_in0"), sem("x_in1")]
        qn_in, kn_in, rem_in, mask_in, gate_in, bo_in = (sem(n) for n in (
            "qn_in", "kn_in", "rem_in", "mask_in", "gate_in", "bo_in"))
        JOBS = ("xq", "xk", "xv", "xo", "aq", "ak", "av", "ao")
        w_in, w_pre, w_hi, w_lo = ([sem(f"{what}_{j}") for j in JOBS] for what in ("w_in", "w_pre", "w_hi", "w_lo"))
        w_sum = sem("w_sum")
        ln_bst, ln_mv, ln_lg, ln_rsd, ln_x, ln_t, ln_hi, ln_lo = (sem(n) for n in (
            "ln_bst", "ln_mv", "ln_lg", "ln_rsd", "ln_x", "ln_t", "ln_hi", "ln_lo"))
        qkw_set = sem("qkw_set")
        q_mm, q_sq, q_ss, q_lg, q_rs, q_n, q_w, q_t, q_out = (sem(n) for n in (
            "q_mm", "q_sq", "q_ss", "q_lg", "q_rs", "q_n", "q_w", "q_t", "q_out"))
        rem_pe, rem_act, rem_dve = sem("rem_pe"), sem("rem_act"), sem("rem_dve")
        not_mask = sem("not_mask")
        ctx_in = [sem("ctx_in0"), sem("ctx_in1")]
        ctx_t, ctx_hi, ctx_lo = sem("ctx_t"), sem("ctx_hi"), sem("ctx_lo")
        k_mm, k_sq, k_ss, k_lg, k_rs, k_n, k_t, k_hi, k_lo, k_rem = (sem(n) for n in (
            "k_mm", "k_sq", "k_ss", "k_lg", "k_rs", "k_n", "k_t", "k_hi", "k_lo", "k_rem"))
        cn_hi, cn_lo = sem("cn_hi"), sem("cn_lo")
        pc_mm, pc_hi, pc_lo = sem("pc_mm"), sem("pc_hi"), sem("pc_lo")
        qb_hi, qb_lo = sem("qb_hi"), sem("qb_lo")
        sc_mm, sc_m, sc_max, sc_exp, sc_step, p_n, p_r = (sem(n) for n in (
            "sc_mm", "sc_m", "sc_max", "sc_exp", "sc_step", "p_n", "p_r"))
        p_t, p_rt, p_hi, p_lo, p_rh, p_rl, o_mm, o_out = (sem(n) for n in (
            "p_t", "p_rt", "p_hi", "p_lo", "p_rh", "p_rl", "o_mm", "o_out"))
        oT_hi, oT_lo, xo_mm, x1_add = sem("oT_hi"), sem("oT_lo"), sem("xo_mm"), sem("x1_add")
        bn_in = [sem(f"bn_in{i}") for i in range(3)]
        bn_lg, bn_rs, bn_a, bn_ma, bn_c = (sem(n) for n in ("bn_lg", "bn_rs", "bn_a", "bn_ma", "bn_c"))
        z_mm, z_c, z_sig = sem("z_mm"), sem("z_c"), sem("z_sig")
        t_step, t_pe, t_act = sem("t_step"), sem("t_pe"), sem("t_act")
        av_mm, av_hi, av_lo, ao_mm, bo_add, x2_add = (sem(n) for n in (
            "av_mm", "av_hi", "av_lo", "ao_mm", "bo_add", "x2_add"))
        gw_hi, gw_lo, g_mm, g_step, g_exp = (sem(n) for n in ("gw_hi", "gw_lo", "g_mm", "g_step", "g_exp"))
        e_in = [sem("e_in0"), sem("e_in1")]
        e_hi, e_lo, g_col = sem("e_hi"), sem("e_lo"), sem("g_col")
        u_mm, u_sig, u_z, u_h, h_t, h_hi, h_lo, y_mm, y_add = (sem(n) for n in (
            "u_mm", "u_sig", "u_z", "u_h", "h_t", "h_hi", "h_lo", "y_mm", "y_add"))
        stored = sem("stored")

        xo_p = parts[:, 4 * C * D:6 * C * D].rearrange("p (s c n) -> p s c n", s=2, c=C)
        jobs = {
            "xq": (chunked(xWq), w_slot[:, 0]),
            "xk": (chunked(xWkv[:, 0:D]), wkv[:, :, :, 0:D]),
            "xv": (chunked(xWkv[:, D:2 * D]), wkv[:, :, :, D:2 * D]),
            "xo": (chunked(xWo), xo_p),
            "aq": (chunked(aWq), w_slot[:, 0]),
            "ak": (chunked(aWk), w_slot[:, 1]),
            "av": (chunked(aWv), w_slot[:, 0]),
            "ao": (chunked(aWo), w_slot[:, 1]),
        }
        JOB = {n: i for i, n in enumerate(JOBS)}
        bn_src = ((gq, bq, mq, vq), (gk, bk, mk, vk), (gv, bv, mv, vv))
        bn_ac = ((qkw[:, 0, :], qkw[:, 1, :]),
                 (s_m[:, :, :].rearrange("p g m -> p (g m)")[:, 0:D], prob[:, :, :].rearrange("p g m -> p (g m)")[:, 0:D]),
                 (qkw[:, 0, :], qkw[:, 1, :]))
        raw = lambda name: raw_of.get(name, w_raw[:, JOB[name] % 2])
        heads = lambda ap: ap.rearrange("p (h d) -> p h d", h=H)
        per_head = lambda ap: ap.unsqueeze(2).broadcast_to([P, H, HD])

        dt_all = xn[:, :, :].rearrange("p u d -> p (u d)").rearrange("p (t n) -> p t n", t=TILES)
        a_all = kn[:, :, :].rearrange("p u d -> p (u d)").rearrange("p (t n) -> p t n", t=TILES)
        pAV = (pP[:, :, :].rearrange("p t n -> p (t n)").rearrange("p (c n) -> p c n", c=C),
               pV1[:, :].rearrange("p (c n) -> p c n", c=C))
        pY = (pV1[:, :], pP[:, :, :].rearrange("p t n -> p (t n)"))
        pP_flat = pP[:, :, :].rearrange("p t n -> p (t n)")
        p_gate = pS[:, 0, 0:TILES * E].rearrange("p (t e) -> p t e", t=TILES)
        cmp_gt = s_m[:, :, :].rearrange("p g m -> p (g m)")[:, 0:TILES * E * E].rearrange(
            "p (t e j) -> p t e j", t=TILES, e=E)
        cmp_eq = prob[:, :, :].rearrange("p g m -> p (g m)")[:, 0:TILES * E * E].rearrange(
            "p (t e j) -> p t e j", t=TILES, e=E)

        pC = (pV1[:, :], pP_flat)
        prob_ctx = lambda g: pC[g].rearrange("p (c h q) -> p c h q", c=2, h=H)

        block = es.enter_context(nc.Block())

        @block.sync
        def _(sp):
            def load_weight(name, freed_by=None):
                j = JOB[name]
                if freed_by is not None:
                    sp.wait_ge(w_lo[JOB[freed_by]], 1)
                    sp.wait_ge(w_hi[JOB[freed_by]], 1)
                sp.dma_start(raw(name), jobs[name][0]).then_inc(w_in[j], 16)

            sp.dma_start(x_all[:, 0:2, :], x_t[:, 0:2, :]).then_inc(x_in[0], 16)
            load_weight("xq")
            sp.dma_start(x_all[:, 2:TILES, :], x_t[:, 2:TILES, :]).then_inc(x_in[1], 16)
            sp.dma_start(qkw[:, 0, :], spread(qn_w.rearrange("h d -> (h d)"))).then_inc(qn_in, 16)
            sp.dma_start(qkw[:, 1, :], spread(kn_w.rearrange("h d -> (h d)"))).then_inc(kn_in, 16)
            load_weight("xk")
            sp.wait_ge(const_set, 1)
            for r in range(3):
                sp.dma_start(rem_raw[r * B:(r + 1) * B, :], ctx[:, M - 1, :]).then_inc(rem_in, 16)
            load_weight("xv", "xq")
            for b in range(2):
                sp.dma_start(ctx_raw[:, b], ctx[b, 0:MT * P, :].rearrange("(t p) d -> p t d", p=P)).then_inc(ctx_in[b], 16)
            for g in range(HG):
                sp.dma_start(masked[g * S:(g + 1) * S], mask.rearrange("b s m -> s b m")).then_inc(mask_in, 16)
            sp.dma_start(gw_raw[:, :, :], chunked(gate_w)).then_inc(gate_in, 16)
            load_weight("xo", "xk")
            load_weight("aq", "xv")

            with sp.Fori(0, (B - 2) // 2) as k:
                for u in range(2):
                    sp.wait_ge(ctx_t, (k * 2 + u + 1) * MT)
                    sp.wait_ge(cn_lo, (k * 2 + u + 1))
                    src = ctx[bass.ds(k * 2 + u + 2, 1), 0:MT * P, :].rearrange("b (t p) d -> p (b t) d", p=P)
                    sp.dma_start(ctx_raw[:, u], src).then_inc(ctx_in[u], 16)
            sp.wait_ge(sc_m, B)
            for i in range(4):
                sp.dma_start(bn_vec[:, i, :], spread(bn_src[0][i])).then_inc(bn_in[0], 16)
            sp.dma_start(rem_raw[:, :], spread(bo)).then_inc(bo_in, 16)
            sp.wait_ge(cn_lo, B)
            load_weight("ao")
            load_weight("ak", "xo")
            for w in range(1, 3):
                sp.wait_ge(bn_c, w)
                for i in range(4):
                    sp.dma_start(bn_vec[:, i, :], spread(bn_src[w][i])).then_inc(bn_in[w], 16)
                if w == 1:
                    load_weight("av", "aq")

            def load_expert(e, u):
                w13 = e_raw[:, u, 0:C * D].rearrange("p (c n) -> p c n", c=C)
                for lo, w in ((0, w1), (F, w3)):
                    sp.dma_start(w13[:, :, lo:lo + F],
                                 w[bass.ds(e, 1)].rearrange("e (c p) f -> p (e c) f", p=P)).then_inc(e_in[u], 16)
                sp.dma_start(e_raw[:, u, C * D:RAW].rearrange("p (c n) -> p c n", c=2),
                             w2[bass.ds(e, 1)].rearrange("e (c p) d -> p (e c) d", p=P)).then_inc(e_in[u], 16)

            for e, name in enumerate(("av", "ao")):
                sp.wait_ge(w_hi[JOB[name]], 1)
                sp.wait_ge(w_lo[JOB[name]], 1)
                load_expert(e, e)
            with sp.Fori(0, (E - 2) // 2) as k:
                for u in range(2):
                    sp.wait_ge(e_hi, (k * 2 + u) + 1)
                    sp.wait_ge(e_lo, (k * 2 + u) + 1)
                    load_expert(k * 2 + u + 2, u)
            for t in range(TILES):
                sp.wait_ge(y_add, (E - 1) * TILES + t + 1)
                sp.dma_start(out_t[:, t, :], x_all[:, t, :]).then_inc(stored, 16)
            sp.wait_ge(stored, 16 * TILES)

        @block.gpsimd
        def _(pool):
            nc.gpsimd.memset(rem_raw[:, :], 0.0).then_inc(const_set, 1)
            nc.gpsimd.memset(ident[:, :], 0.0).then_inc(ident_step, 1)
            nc.gpsimd.memset(ones[:, :], 1.0)
            nc.gpsimd.memset(same_seq[:, :], 0.0)
            nc.gpsimd.memset(bias[:, 0:1], LN_EPS)
            nc.gpsimd.memset(bias[:, 1:2], HEAD_EPS)
            nc.gpsimd.memset(bias[:, 2:3], BN_EPS)
            nc.gpsimd.memset(bias[:, 3:4], -SLOPE * V_TH)
            nc.gpsimd.memset(kT[:, :, :, M:M + 1].bitcast(F32), 0.0)
            nc.gpsimd.memset(qblk[:, :, :, :].bitcast(F32), 0.0)
            nc.gpsimd.memset(tri[:, :, :], 1.0)
            nc.gpsimd.memset(rem_p[:, :].bitcast(F32), 0.0)
            nc.gpsimd.memset(batch_col[:, 3 * B:P], -1.0)
            nc.gpsimd.iota(col[:, :], [[1, P]], base=0, channel_multiplier=0, allow_small_or_imprecise_dtypes=True).then_inc(ident_step, 1)
            nc.gpsimd.iota(batch_col[:, 0:3 * B], [[0, 3], [1, B]], base=0, channel_multiplier=0,
                           allow_small_or_imprecise_dtypes=True).then_inc(ident_step, 1)
            pool.wait_ge(ident_step, 3)
            for g in range(BT):
                nc.gpsimd.memset(same_seq[g * S:(g + 1) * S, g * S:(g + 1) * S], 1.0).then_inc(ident_step, 1)
                pool.wait_ge(ident_step, 4 + g)
            nc.gpsimd.affine_select(out=tri[:, :, :], in_=tri[:, :, :], compare_op=ALU.is_ge, fill=0.0, base=-1,
                                    pattern=[[1, E], [-1, E]], channel_multiplier=0)
            nc.gpsimd.affine_select(out=ident[:, :], in_=ident[:, :], compare_op=ALU.not_equal, fill=1.0, base=0,
                                    pattern=[[-1, P]], channel_multiplier=1).then_inc(const_set, 1)

            def low_part(name):
                j = JOB[name]
                pool.wait_ge(w_hi[j], 1)
                dst = jobs[name][1]
                nc.gpsimd.tensor_tensor(dst[:, LO], raw(name), dst[:, HI].bitcast(F32),
                                        ALU.subtract).then_inc(w_lo[j], 1)

            for name in JOBS[:3]:
                low_part(name)
            pool.wait_ge(mask_in, 16 * HG)
            nc.gpsimd.tensor_scalar(mask_f[:, :].bitcast(U8), mask_f[:, :].bitcast(U8), -1.0, 1.0,
                                    ALU.mult, ALU.add).then_inc(not_mask, 1)
            def ctx_parts(b, u):
                pool.wait_ge(cn_hi, b + 1)
                nc.gpsimd.tensor_tensor(ctxN[:, u, LO], ctx_raw[:, u], ctxN[:, u, HI].bitcast(F32),
                                        ALU.subtract).then_inc(cn_lo, 1)

            with pool.Fori(0, B // 2) as k:
                ctx_parts(k * 2, 0)
                ctx_parts(k * 2 + 1, 1)
            for name in ("xo", "aq", "ak"):
                low_part(name)
            pool.wait_ge(bo_in, 16)
            for t in range(TILES):
                pool.wait_ge(ln_x, TILES + t + 1)
                nc.gpsimd.tensor_tensor(x_all[:, t, :], x_all[:, t, :], rem_raw[:, :], ALU.add).then_inc(bo_add, 1)
            for name in ("av", "ao"):
                low_part(name)

            def expert_low(e, u):
                pool.wait_ge(e_hi, e + 1)
                nc.gpsimd.tensor_tensor(e_p[u][:, LO, :], e_raw[:, u, :], e_p[u][:, HI, :].bitcast(F32),
                                        ALU.subtract).then_inc(e_lo, 1)

            expert_low(0, 0)
            with pool.Fori(0, (E - 2) // 2) as k:
                expert_low(k * 2 + 1, 1)
                expert_low(k * 2 + 2, 0)
            expert_low(E - 1, 1)

        @block.scalar
        def _(act):
            def ln_root(n):
                act.wait_ge(ln_mv, n + 1)
                act.activation(ln_log[:, n % 2], mean_var[:, n % 2, 1:2], ACT.Ln, bias=LN_B).then_inc(ln_lg, 1)
                act.wait_ge(ln_lg, n + 1)
                act.activation(ln_rs[:, n % 2], ln_log[:, n % 2], ACT.Exp, scale=-0.5).then_inc(ln_rsd, 1)

            def ln_high(n, dst):
                act.wait_ge(ln_t, n + 1)
                act.activation(dst, pTT[n % 2][:, :, :], ACT.Copy).then_inc(ln_hi, 1)

            def high_part(name):
                j = JOB[name]
                if name in ("xv", "xo", "ao"):
                    act.wait_ge(w_in[j], 16)
                else:
                    act.wait_ge(w_pre[j], 1)
                act.activation(jobs[name][1][:, HI], raw(name), ACT.Copy).then_inc(w_hi[j], 1)

            act.preload_act_table_set(ROOTS)
            act.wait_ge(const_set, 2)
            ln_root(0)
            high_part("xq")
            for s in range(TILES + 2):
                if s + 1 < TILES:
                    ln_root(s + 1)
                if s < TILES:
                    if s >= 2:
                        act.wait_ge(q_mm, s - 1)
                    ln_high(s, lhs_p[:, s % 2, HI])
                t = s - 1
                if 0 <= t < TILES:
                    act.wait_ge(q_mm, t + 1)
                    if t >= 2:
                        act.wait_ge(q_ss, t - 1)
                    act.activation(sq[:, t % 2], pKV[t % 2][:, :], ACT.Square).then_inc(q_sq, 1)
                    act.wait_ge(q_ss, t + 1)
                    act.activation(head_log[:, t % 2], head_ss[:, t % 2], ACT.Ln, bias=HEAD_B,
                                   scale=1.0 / HD).then_inc(q_lg, 1)
                    act.wait_ge(q_lg, t + 1)
                    if t >= 2:
                        act.wait_ge(q_n, t - 1)
                    act.activation(head_rs[:, t % 2], head_log[:, t % 2], ACT.Exp, scale=-0.5).then_inc(q_rs, 1)
                if s == 3:
                    high_part("xk")
                if s == 6:
                    high_part("xv")
                t = s - 2
                if t >= 0:
                    act.wait_ge(q_t, t + 1)
                    act.activation(qoT[:, :, t * P:(t + 1) * P], pS[:, t % 2, :].rearrange("p (c n) -> p c n", c=C),
                                   ACT.Copy).then_inc(q_out, 1)
            act.wait_ge(rem_in, 48)
            act.activation(rem_p[0:3 * B, :], rem_raw[0:3 * B, :], ACT.Copy).then_inc(rem_act, 1)
            act.wait_ge(rem_pe, 1)
            act.activation(ctxT[:, 0, HI, :, 0:P], pT0[:, :, :], ACT.Copy).then_inc(rem_act, 1)
            act.wait_ge(rem_pe, 2)
            act.activation(sq[:, 0], pK0[:, :], ACT.Square).then_inc(rem_act, 1)
            act.wait_ge(rem_dve, 3)
            act.activation(head_log[:, 0], head_ss[:, 0], ACT.Ln, bias=HEAD_B, scale=1.0 / HD).then_inc(rem_act, 1)
            act.wait_ge(rem_act, 4)
            act.activation(head_rs[:, 0], head_log[:, 0], ACT.Exp, scale=-0.5).then_inc(rem_act, 1)
            act.wait_ge(rem_pe, 3)
            act.activation(kT_rem[:, :, :], pT1[:, :, 0:B], ACT.Copy).then_inc(rem_act, 1)

            def ctx_high(n, u):
                for t in range(MT):
                    act.wait_ge(ctx_t, n * MT + t + 1)
                    act.activation(ctxT[:, u, HI, :, t * P:(t + 1) * P], pTT[t][:, :, :], ACT.Copy).then_inc(ctx_hi, 1)

            def k_square(b, t):
                act.wait_ge(k_mm, b * MT + t + 1)
                act.activation(sq[:, t], pKV[t][:, :], ACT.Square).then_inc(k_sq, 1)

            def k_root(b, t):
                act.wait_ge(k_ss, b * MT + t + 1)
                act.activation(head_log[:, t], head_ss[:, t], ACT.Ln, bias=HEAD_B, scale=1.0 / HD).then_inc(k_lg, 1)
                act.wait_ge(k_lg, b * MT + t + 1)
                act.activation(head_rs[:, t], head_log[:, t], ACT.Exp, scale=-0.5).then_inc(k_rs, 1)

            def batch(tile, r, main=True, prev=True, nxt=True, first=False):
                b = tile * BT + r
                u, pr = r % 2, (r - 1) % BT
                if nxt:
                    ctx_high(b + 1, 1 - u)
                if prev:
                    act.wait_ge(sc_max, b)
                    if not first:
                        act.wait_ge(p_rt, b - 1)
                    for g in range(G):
                        act.activation(prob[:, g, 0:M], s_m[:, g, 0:M], ACT.Exp, bias=neg_max[:, g:g + 1],
                                       accum_out=p_sum[:, g:g + 1]).then_inc(sc_exp, 1)
                if main:
                    act.activation(ctxN[:, u, HI], ctx_raw[:, u], ACT.Copy).then_inc(cn_hi, 1)
                    k_square(b, 1)
                if prev:
                    act.wait_ge(sc_step, b * 3)
                    for g in range(G):
                        act.activation(prob[:, g, 0:M], prob[:, g, 0:M], ACT.Copy,
                                       scale=p_scale[:, g:g + 1]).then_inc(p_n, 1)
                if main:
                    k_root(b, 1)
                if prev:
                    act.wait_ge(p_t, b)
                    act.activation(pT[:, HI], pP[:, :, :], ACT.Copy).then_inc(p_hi, 1)
                    act.wait_ge(p_rt, b)
                    act.activation(pT_rem[:, :], pV1[:, 0:G * P], ACT.Copy).then_inc(p_rh, 1)
                if nxt:
                    k_square(b + 1, 0)
                    k_root(b + 1, 0)
                if main:
                    for t in range(MT):
                        act.wait_ge(k_t, b * MT + t + 1)
                        act.activation(kT[:, HI, :, t * P:(t + 1) * P], pTT[t][:, :, :], ACT.Copy).then_inc(k_hi, 1)
                if prev:
                    if pr == 0 and not first:
                        act.wait_ge(o_mm, tile * 2)
                    for g in range(2):
                        act.wait_ge(pc_mm, (b - 1) * 2 + g + 1)
                        act.activation(z_b[:, HI, 2 * g:2 * g + 2, :, pr, :], prob_ctx(g), ACT.Copy).then_inc(pc_hi, 1)

            ctx_high(0, 0)
            k_square(0, 0)
            k_root(0, 0)
            for r in range(BT):
                batch(0, r, prev=r > 0, first=r == 1)
            with act.Fori(1, TILES - 1) as k:
                for r in range(BT):
                    batch(k, r)
            for r in range(BT):
                batch(TILES - 1, r, nxt=r < BT - 1)
            high_part("xo")
            batch(TILES, 0, main=False, nxt=False)

            def bn_root(w):
                act.wait_ge(bn_in[w], 64)
                act.activation(bn_vec[:, 3, :], bn_vec[:, 3, :], ACT.Ln, bias=BN_B).then_inc(bn_lg, 1)
                act.wait_ge(bn_lg, w + 1)
                act.activation(bn_vec[:, 3, :], bn_vec[:, 3, :], ACT.Exp, scale=-0.5).then_inc(bn_rs, 1)

            def out_high(t):
                if t >= 2:
                    act.wait_ge(xo_mm, t - 1)
                act.activation(lhs_p[:, t % 2, HI], qoT[:, :, t * P:(t + 1) * P], ACT.Copy).then_inc(oT_hi, 1)

            act.wait_ge(o_out, 4 * TILES)
            out_high(0)
            for s in range(TILES + 2):
                if s + 1 < TILES:
                    out_high(s + 1)
                if 0 <= s - 1 < TILES:
                    ln_root(TILES + s - 1)
                if s - 2 >= 0:
                    t = s - 2
                    ln_high(TILES + t, xT[:, HI, :, t * P:(t + 1) * P])
                if s == 1:
                    bn_root(0)
                if s == 6:
                    high_part("aq")
            def expert_high(e, u, turn):
                act.wait_ge(e_in[u], turn * 48)
                act.activation(e_p[u][:, HI, :], e_raw[:, u, :], ACT.Copy).then_inc(e_hi, 1)

            bn_root(1)
            act.wait_ge(xo_mm, TILES)
            high_part("ak")
            bn_root(2)
            for n in range(3 * TILES):
                w, t = divmod(n, TILES)
                act.wait_ge(z_c, n + 1)
                if w < 2:
                    act.wait_ge(ln_t, 2 * TILES)
                    if n >= 2:
                        act.wait_ge(z_sig, n - 1)
                    act.activation(xn[:, n % 2], sq[:, n % 2], ACT.Sigmoid, bias=SIG_B, scale=SLOPE,
                                   accum_out=rows[:, w, t:t + 1]).then_inc(z_sig, 1)
                else:
                    act.activation(v_self[:, t], sq[:, n % 2], ACT.Sigmoid, bias=SIG_B, scale=SLOPE).then_inc(z_sig, 1)
                if n == TILES + 1:
                    high_part("av")
                if n == 2 * TILES:
                    high_part("ao")
                if n == 2 * TILES + 2:
                    expert_high(0, 0, 1)
            act.preload_act_table_set(ROOTS)
            act.wait_ge(t_step, TILES + 4)
            act.activation(kn[:, :, :], kn[:, :, :], ACT.Exp, scale=-1.0 / TAU).then_inc(t_act, 1)
            act.wait_ge(gate_in, 16)
            act.activation(gw_p[:, HI], gw_raw[:, :, :], ACT.Copy).then_inc(gw_hi, 1)
            def self_high(t):
                act.wait_ge(av_mm, t + 1)
                if t >= 2:
                    act.wait_ge(ao_mm, t - 1)
                act.activation(lhs_p[:, t % 2, HI], pAV[t % 2], ACT.Copy).then_inc(av_hi, 1)

            self_high(0)
            for s in range(TILES + 2):
                if s + 1 < TILES:
                    self_high(s + 1)
                if 0 <= s - 1 < TILES:
                    ln_root(2 * TILES + s - 1)
                if s - 2 >= 0:
                    t = s - 2
                    ln_high(2 * TILES + t, xT[:, HI, :, t * P:(t + 1) * P])
            act.wait_ge(g_step, 2)
            act.activation(gates[:, :, :], g_tmp[:, :, :], ACT.Exp).then_inc(g_exp, 1)

            def expert(e, u, prev=True, nxt=None):
                act.wait_ge(g_col, e + 1)
                for t in range(TILES):
                    act.wait_ge(u_mm, e * TILES + t + 1)
                    if prev or t >= 2:
                        act.wait_ge(u_h, e * TILES + t - 1)
                    sg = sq[:, t % 2, 0:F]
                    act.activation(sg, pKV[t % 2][:, 0:F], ACT.Silu, scale=g_now[:, u, t:t + 1]).then_inc(u_sig, 1)
                    if prev or t >= 1:
                        hidden_high(e * TILES + t - 1, (t - 1) % 2, prev or t >= 3)
                    if nxt is not None and t == 3:
                        act.wait_ge(y_mm, e * TILES)
                        expert_high(e + 1, 1 - u, nxt)

            def hidden_high(n, u, reused):
                act.wait_ge(h_t, n + 1)
                if reused:
                    act.wait_ge(y_mm, n - 1)
                act.activation(hT[:, u, HI], pTT[u][:, 0:2, :], ACT.Copy).then_inc(h_hi, 1)

            expert(0, 0, prev=False, nxt=1)
            with act.Fori(0, (E - 2) // 2) as k:
                expert(k * 2 + 1, 1, nxt=k + 2)
                expert(k * 2 + 2, 0, nxt=k + 2)
            expert(E - 1, 1)
            hidden_high(E * TILES - 1, 1, True)

        @block.vector
        def _(dve):
            tt, ts, stt = nc.vector.tensor_tensor, nc.vector.tensor_scalar, nc.vector.scalar_tensor_tensor

            def ln_stats(n, src):
                nc.vector.bn_stats(bst[:, n % 2], src).then_inc(ln_bst, 1)
                dve.wait_ge(ln_bst, n + 1)
                nc.vector.bn_aggr(mean_var[:, n % 2], bst[:, n % 2]).then_inc(ln_mv, 1)

            def ln_norm(n, src):
                dve.wait_ge(ln_rsd, n + 1)
                if n >= 2:
                    dve.wait_ge(ln_t, n - 1)
                ts(xn[:, n % 2], src, mean_var[:, n % 2, 0:1], ln_rs[:, n % 2], ALU.subtract,
                   ALU.mult).then_inc(ln_x, 1)

            def ln_low(n, dst_lo, dst_hi):
                dve.wait_ge(ln_hi, n + 1)
                tt(dst_lo, pTT[n % 2][:, :, :], dst_hi.bitcast(F32), ALU.subtract).then_inc(ln_lo, 1)

            def centre(name, k):
                j = JOB[name]
                dve.wait_ge(w_in[j], 16)
                w = raw(name).rearrange("p c (h d) -> p (c h) d", d=HD)
                hm = head_mean[:, :, :].rearrange("p c h -> p (c h)")
                nc.vector.tensor_reduce(hm, w, AX.X, ALU.add).then_inc(w_sum, 1)
                dve.wait_ge(w_sum, k)
                stt(w, hm.unsqueeze(2).broadcast_to([P, C * H, HD]), -1.0 / HD, w, ALU.mult,
                    ALU.add).then_inc(w_pre[j], 1)

            dve.wait_ge(const_set, 2)
            dve.wait_ge(x_in[0], 16)
            ln_stats(0, x_all[:, 0])
            ln_norm(0, x_all[:, 0])
            centre("xq", 1)
            dve.wait_ge(qn_in, 16)
            dve.wait_ge(kn_in, 16)
            stt(qkw[:, 0, :], qkw[:, 0, :], SCALE, qkw[:, 1, :], ALU.mult, ALU.mult).then_inc(qkw_set, 1)
            for s in range(TILES + 1):
                if s + 1 < TILES:
                    if s == 1:
                        dve.wait_ge(x_in[1], 16)
                    ln_stats(s + 1, x_all[:, s + 1])
                    ln_norm(s + 1, x_all[:, s + 1])
                if s < TILES:
                    ln_low(s, lhs_p[:, s % 2, LO], lhs_p[:, s % 2, HI])
                t = s - 1
                if t >= 0:
                    dve.wait_ge(q_sq, t + 1)
                    nc.vector.tensor_reduce(head_ss[:, t % 2], heads(sq[:, t % 2]), AX.X, ALU.add).then_inc(q_ss, 1)
                    dve.wait_ge(q_rs, t + 1)
                    if t >= 2:
                        dve.wait_ge(q_t, t - 1)
                    tt(heads(kn[:, t % 2]), heads(pKV[t % 2][:, :]), per_head(head_rs[:, t % 2]),
                       ALU.mult).then_inc(q_n, 1)
                    dve.wait_ge(q_n, t + 1)
                    if t == 0:
                        dve.wait_ge(qkw_set, 1)
                    tt(kn[:, t % 2], kn[:, t % 2], qkw[:, 0, :], ALU.mult).then_inc(q_w, 1)
                if s == 1:
                    centre("xk", 2)
            dve.wait_ge(rem_act, 1)
            tt(rem_p[B:2 * B, :], rem_raw[B:2 * B, :], rem_p[B:2 * B, :].bitcast(F32), ALU.subtract).then_inc(rem_dve, 1)
            dve.wait_ge(rem_act, 2)
            tt(ctxT[:, 0, LO, :, 0:P], pT0[:, :, :], ctxT[:, 0, HI, :, 0:P].bitcast(F32),
               ALU.subtract).then_inc(rem_dve, 1)
            dve.wait_ge(rem_act, 3)
            nc.vector.tensor_reduce(head_ss[:, 0], heads(sq[:, 0]), AX.X, ALU.add).then_inc(rem_dve, 1)
            dve.wait_ge(rem_act, 5)
            dve.wait_ge(q_t, TILES)
            tt(heads(kn[:, 0]), heads(pK0[:, :]), per_head(head_rs[:, 0]), ALU.mult).then_inc(rem_dve, 1)

            def ctx_low(n, u):
                for t in range(MT):
                    dve.wait_ge(ctx_hi, n * MT + t + 1)
                    tt(ctxT[:, u, LO, :, t * P:(t + 1) * P], pTT[t][:, :, :],
                       ctxT[:, u, HI, :, t * P:(t + 1) * P].bitcast(F32), ALU.subtract).then_inc(ctx_lo, 1)

            def k_sum(b, t):
                dve.wait_ge(k_sq, b * MT + t + 1)
                nc.vector.tensor_reduce(head_ss[:, t], heads(sq[:, t]), AX.X, ALU.add).then_inc(k_ss, 1)

            def k_norm(b, t, reused=True):
                dve.wait_ge(k_rs, b * MT + t + 1)
                if reused:
                    dve.wait_ge(k_t, b * MT + t - 1)
                tt(heads(kn[:, t]), heads(pKV[t][:, :]), per_head(head_rs[:, t]), ALU.mult).then_inc(k_n, 1)

            def out_copy(t):
                for i, bank in enumerate((pV1[:, :], pP_flat)):
                    dve.wait_ge(o_mm, t * 2 + i + 1)
                    o = bank.rearrange("p (c e n) -> p c e n", c=2, e=2)
                    for e in range(2):
                        a = slice(e * HD, (e + 1) * HD)
                        ts(qoT[a, 2 * i:2 * i + 2, bass.ds(t * P, P)], o[a, :, e, :], 1.0, None,
                           ALU.mult).then_inc(o_out, 1)

            def batch(tile, r, main=True, prev=True, nxt=True, first=False):
                b = tile * BT + r
                p = b - 1
                u, pr = r % 2, (r - 1) % BT
                if prev:
                    dve.wait_ge(sc_mm, b)
                    stt(s_m[:, :, 0:M], masked[:, bass.ds(p, 1), :].broadcast_to([P, G, M]), -BIG,
                        pS[:, :, 0:M], ALU.mult, ALU.add).then_inc(sc_m, 1)
                    dve.wait_ge(sc_m, b)
                    nc.vector.tensor_reduce(neg_max[:, :], s_m[:, :, 0:M], AX.X, ALU.max, negate=True).then_inc(sc_max, 1)
                if nxt:
                    ctx_low(b + 1, 1 - u)
                if prev:
                    dve.wait_ge(sc_exp, b * G)
                    stt(p_den[:, :], neg_max[:, :], BIG / 2, p_sum[:, :], ALU.is_lt, ALU.mult).then_inc(sc_step, 1)
                    dve.wait_ge(sc_step, p * 3 + 1)
                    nc.vector.reciprocal(p_inv[:, :], p_den[:, :]).then_inc(sc_step, 1)
                    dve.wait_ge(sc_step, p * 3 + 2)
                    stt(p_scale[:, :], neg_max[:, :], BIG / 2, p_inv[:, :], ALU.is_lt, ALU.mult).then_inc(sc_step, 1)
                if main:
                    for e in range(2):
                        a = slice(e * HD, (e + 1) * HD)
                        ts(qblk[a, HI, :, e * S:(e + 1) * S], qoT[a, :, bass.ds(b * S, S)], 1.0, None,
                           ALU.mult).then_inc(qb_hi, 1)
                    dve.wait_ge(qb_hi, b * 2 + 2)
                    for e in range(2):
                        a = slice(e * HD, (e + 1) * HD)
                        tt(qblk[a, LO, :, e * S:(e + 1) * S], qoT[a, :, bass.ds(b * S, S)],
                           qblk[a, HI, :, e * S:(e + 1) * S].bitcast(F32), ALU.subtract).then_inc(qb_lo, 1)
                    ts(kT[:, HI, :, M - 1:M], kT_rem[:, :, bass.ds(b, 1)], 1.0, None, ALU.mult).then_inc(k_rem, 1)
                    dve.wait_ge(k_rem, b * 2 + 1)
                    tt(kT[:, LO, :, M - 1:M], kT_rem[:, :, bass.ds(b, 1)], kT[:, HI, :, M - 1:M].bitcast(F32),
                       ALU.subtract).then_inc(k_rem, 1)
                    k_sum(b, 1)
                if prev:
                    dve.wait_ge(p_n, b * G)
                    if not first:
                        dve.wait_ge(p_rt, p)
                    for g in range(G):
                        ts(p_rem[:, g, :], batch_col[:, :], batch_col[:, bass.ds(p, 1)], prob[:, g, M - 1:M],
                           ALU.is_equal, ALU.mult).then_inc(p_r, 1)
                if main:
                    k_norm(b, 1, reused=prev)
                if prev and pr == 0 and not first:
                    out_copy(tile - 1)
                if prev:
                    dve.wait_ge(p_hi, b)
                    tt(pT[:, LO], pP[:, :, :], pT[:, HI].bitcast(F32), ALU.subtract).then_inc(p_lo, 1)
                    dve.wait_ge(p_rh, b)
                    a = slice(2 * B, 3 * B)
                    tt(pT_rem[a, :], pV1[a, 0:G * P], pT_rem[a, :].bitcast(F32), ALU.subtract).then_inc(p_rl, 1)
                if nxt:
                    k_sum(b + 1, 0)
                if main:
                    for t in range(MT):
                        dve.wait_ge(k_hi, b * MT + t + 1)
                        tt(kT[:, LO, :, t * P:(t + 1) * P], pTT[t][:, :, :],
                           kT[:, HI, :, t * P:(t + 1) * P].bitcast(F32), ALU.subtract).then_inc(k_lo, 1)
                if nxt:
                    k_norm(b + 1, 0)
                if prev:
                    for g in range(2):
                        dve.wait_ge(pc_hi, p * 2 + g + 1)
                        z = z_b[:, :, 2 * g:2 * g + 2, :, pr, :]
                        tt(z[:, LO], prob_ctx(g), z[:, HI].bitcast(F32), ALU.subtract).then_inc(pc_lo, 1)

            dve.wait_ge(q_out, TILES)
            dve.wait_ge(rem_act, 6)
            ctx_low(0, 0)
            k_sum(0, 0)
            k_norm(0, 0, reused=False)
            for r in range(BT):
                if r == 1:
                    dve.wait_ge(not_mask, 1)
                batch(0, r, prev=r > 0, first=r == 1)
            with dve.Fori(1, TILES - 1) as k:
                for r in range(BT):
                    batch(k, r)
            for r in range(BT):
                batch(TILES - 1, r, nxt=r < BT - 1)
            batch(TILES, 0, main=False, nxt=False)
            out_copy(TILES - 1)

            def bn_fold(w):
                name = ("aq", "ak", "av")[w]
                j = JOB[name]
                a, c = bn_ac[w]
                dve.wait_ge(bn_rs, w + 1)
                tt(a, bn_vec[:, 0, :], bn_vec[:, 3, :], ALU.mult).then_inc(bn_a, 1)
                dve.wait_ge(bn_a, w + 1)
                tt(bn_vec[:, 2, :], bn_vec[:, 2, :], a, ALU.mult).then_inc(bn_ma, 1)
                dve.wait_ge(bn_ma, w + 1)
                tt(c, bn_vec[:, 1, :], bn_vec[:, 2, :], ALU.subtract).then_inc(bn_c, 1)
                dve.wait_ge(w_in[j], 16)
                tt(raw(name), raw(name), a.unsqueeze(1).broadcast_to([P, C, D]),
                   ALU.mult).then_inc(w_pre[j], 1)

            def out_low(t):
                dve.wait_ge(oT_hi, t + 1)
                tt(lhs_p[:, t % 2, LO], qoT[:, :, t * P:(t + 1) * P], lhs_p[:, t % 2, HI].bitcast(F32),
                   ALU.subtract).then_inc(oT_lo, 1)

            dve.wait_ge(o_out, 4 * TILES)
            out_low(0)
            for s in range(TILES + 2):
                t = s - 1
                if 0 <= t < TILES:
                    dve.wait_ge(xo_mm, t + 1)
                    tt(x_all[:, t], x_all[:, t], pKV[t % 2][:, :], ALU.add).then_inc(x1_add, 1)
                    dve.wait_ge(x1_add, t + 1)
                    ln_stats(TILES + t, x_all[:, t])
                if s + 1 < TILES:
                    out_low(s + 1)
                if 0 <= t < TILES:
                    ln_norm(TILES + t, x_all[:, t])
                t = s - 2
                if t >= 0:
                    ln_low(TILES + t, xT[:, LO, :, t * P:(t + 1) * P], xT[:, HI, :, t * P:(t + 1) * P])
                if s == 4:
                    bn_fold(0)
            bn_fold(1)
            dve.wait_ge(bn_c, 2)
            for n in range(3 * TILES):
                w, t = divmod(n, TILES)
                if n == 2 * TILES:
                    dve.wait_ge(z_sig, 2 * TILES)
                    for r in range(TILES):
                        ts(a_all[:, r, :], ident[:, :], rows[:, 0, r:r + 1], 1.0 / D, ALU.mult,
                           ALU.mult).then_inc(t_step, 1)
                    ts(rows[:, 1, :], rows[:, 1, :], 1.0 / D, None, ALU.mult).then_inc(t_step, 1)
                if n == 2 * TILES + 4:
                    dve.wait_ge(t_pe, 1)
                    dve.wait_ge(t_step, TILES + 1)
                    for g in range(2):
                        half = slice(g * C, (g + 1) * C)
                        tt(dt_all[:, half, :], rows[:, 1, half].unsqueeze(2).broadcast_to([P, C, P]),
                           pS[:, g, :].rearrange("p (t n) -> p t n", t=C), ALU.subtract).then_inc(t_step, 1)
                    dve.wait_ge(t_step, TILES + 3)
                    stt(a_all[:, :, :], dt_all[:, :, :], -1.0, dt_all[:, :, :], ALU.mult, ALU.max).then_inc(t_step, 1)
                dve.wait_ge(z_mm, n + 1)
                if n >= 2:
                    dve.wait_ge(z_sig, n - 1)
                tt(sq[:, n % 2], pZ[n % 3][:, :], bn_ac[w][1], ALU.add).then_inc(z_c, 1)
                if n == TILES + 1:
                    bn_fold(2)
                    dve.wait_ge(bn_c, 3)
            ts(dt_all[:, :, :], dt_all[:, :, :], 0.0, 2 * A_STDP, ALU.is_lt, ALU.mult).then_inc(t_step, 1)
            dve.wait_ge(t_step, TILES + 5)
            dve.wait_ge(t_act, 1)
            stt(dt_all[:, :, :], dt_all[:, :, :], -A_STDP, a_all[:, :, :], ALU.add, ALU.mult).then_inc(t_step, 1)
            dve.wait_ge(t_step, TILES + 6)
            stt(a_all[:, :, :], dt_all[:, :, :], W_OFF, same_seq[:, :].unsqueeze(1).broadcast_to([P, TILES, P]),
                ALU.add, ALU.mult).then_inc(t_step, 1)
            dve.wait_ge(gw_hi, 1)
            tt(gw_p[:, LO], gw_raw[:, :, :], gw_p[:, HI].bitcast(F32), ALU.subtract).then_inc(gw_lo, 1)
            def self_low(t):
                dve.wait_ge(av_hi, t + 1)
                tt(lhs_p[:, t % 2, LO], pAV[t % 2], lhs_p[:, t % 2, HI].bitcast(F32), ALU.subtract).then_inc(av_lo, 1)

            self_low(0)
            for s in range(TILES + 2):
                t = s - 1
                if 0 <= t < TILES:
                    dve.wait_ge(ao_mm, t + 1)
                    dve.wait_ge(bo_add, t + 1)
                    tt(x_all[:, t], x_all[:, t], pKV[t % 2][:, :], ALU.add).then_inc(x2_add, 1)
                    dve.wait_ge(x2_add, t + 1)
                    ln_stats(2 * TILES + t, x_all[:, t])
                if s + 1 < TILES:
                    self_low(s + 1)
                if 0 <= t < TILES:
                    ln_norm(2 * TILES + t, x_all[:, t])
                t = s - 2
                if t >= 0:
                    ln_low(2 * TILES + t, xT[:, LO, :, t * P:(t + 1) * P], xT[:, HI, :, t * P:(t + 1) * P])
            step = [0]

            def gate(ins):
                step[0] += 1
                ins.then_inc(g_step, 1)

            per_token = lambda ap: ap.unsqueeze(2).broadcast_to([P, TILES, E])
            dve.wait_ge(g_mm, TILES)
            gate(nc.vector.tensor_reduce(g_red[:, :], p_gate, AX.X, ALU.max))
            dve.wait_ge(g_step, 1)
            gate(tt(g_tmp[:, :, :], p_gate, per_token(g_red[:, :]), ALU.subtract))
            dve.wait_ge(g_exp, 1)
            gate(nc.vector.tensor_reduce(g_red[:, :], gates[:, :, :], AX.X, ALU.add))
            dve.wait_ge(g_step, 3)
            gate(nc.vector.reciprocal(g_red[:, :], g_red[:, :]))
            dve.wait_ge(g_step, 4)
            gate(tt(gates[:, :, :], gates[:, :, :], per_token(g_red[:, :]), ALU.mult))
            dve.wait_ge(g_step, 5)
            other = gates[:, :, :].unsqueeze(2).broadcast_to([P, TILES, E, E])
            own = gates[:, :, :].unsqueeze(3).broadcast_to([P, TILES, E, E])
            gate(tt(cmp_gt, other, own, ALU.is_gt))
            gate(tt(cmp_eq, other, own, ALU.is_equal))
            dve.wait_ge(g_step, 7)
            gate(tt(cmp_eq, cmp_eq, tri[:, :, :].unsqueeze(1).broadcast_to([P, TILES, E, E]), ALU.mult))
            dve.wait_ge(g_step, 8)
            gate(tt(cmp_gt, cmp_gt, cmp_eq, ALU.add))
            dve.wait_ge(g_step, 9)
            gate(nc.vector.tensor_reduce(g_tmp[:, :, :], cmp_gt, AX.X, ALU.add))
            dve.wait_ge(g_step, 10)
            gate(stt(gates[:, :, :], g_tmp[:, :, :], 1.5, gates[:, :, :], ALU.is_lt, ALU.mult))
            dve.wait_ge(g_step, 11)

            def hidden_low(n, u):
                dve.wait_ge(h_hi, n + 1)
                tt(hT[:, u, LO], pTT[u][:, 0:2, :], hT[:, u, HI].bitcast(F32), ALU.subtract).then_inc(h_lo, 1)

            def expert_add(n, t):
                dve.wait_ge(y_mm, n + 1)
                tt(x_all[:, t % TILES], x_all[:, t % TILES], pY[t % 2], ALU.add).then_inc(y_add, 1)

            def expert(e, u, prev=True):
                ts(g_now[:, u, :], gates[:, :, bass.ds(e, 1)].rearrange("p t e -> p (t e)"), 1.0, None,
                   ALU.mult).then_inc(g_col, 1)
                dve.wait_ge(g_col, e + 1)
                for t in range(TILES):
                    n = e * TILES + t
                    dve.wait_ge(u_sig, n + 1)
                    if prev or t >= 2:
                        dve.wait_ge(h_t, n - 1)
                    stt(xn[:, t % 2, 0:F], pKV[t % 2][:, F:2 * F], g_now[:, u, t:t + 1], sq[:, t % 2, 0:F],
                        ALU.mult, ALU.mult).then_inc(u_h, 1)
                    if prev or t >= 1:
                        hidden_low(n - 1, (t - 1) % 2)
                    if prev or t >= 2:
                        expert_add(n - 2, t - 2)

            expert(0, 0, prev=False)
            with dve.Fori(0, (E - 2) // 2) as k:
                expert(k * 2 + 1, 1)
                expert(k * 2 + 2, 0)
            expert(E - 1, 1)
            hidden_low(E * TILES - 1, 1)
            expert_add(E * TILES - 2, TILES - 2)
            expert_add(E * TILES - 1, TILES - 1)

        @block.tensor
        def _(pe):
            def ln_turn(n):
                pe.wait_ge(ln_x, n + 1)
                if n >= 2:
                    pe.wait_ge(ln_lo, n - 1)
                for c in range(C):
                    last = pe.transpose(pTT[n % 2][:, c, :], xn[:, n % 2, c * P:(c + 1) * P], ident[:, :])
                last.then_inc(ln_t, 1)

            def tile_of(buf, u):
                return lambda s, c: buf[:, u, s, c, :]

            def rows_of(buf, t):
                return lambda s, c: buf[:, s, c, t * P:(t + 1) * P]

            def weight(buf, lo=0, hi=D):
                return lambda s, c: buf[:, s, c, lo:hi]

            pe.wait_ge(const_set, 2)
            for s in range(TILES + 2):
                if s < TILES:
                    ln_turn(s)
                t = s - 1
                if 0 <= t < TILES:
                    pe.wait_ge(ln_lo, t + 1)
                    if t == 0:
                        pe.wait_ge(w_lo[JOB["xq"]], 1)
                    if t >= 2:
                        pe.wait_ge(q_n, t - 1)
                    split_products(pe, pKV[t % 2][:, :], tile_of(lhs_p, t % 2), weight(w_slot[:, 0]),
                                   C).then_inc(q_mm, 1)
                t = s - 2
                if t >= 0:
                    pe.wait_ge(q_w, t + 1)
                    if t >= 2:
                        pe.wait_ge(q_out, t - 1)
                    for c in range(C):
                        last = pe.transpose(pS[:, t % 2, c * P:(c + 1) * P], kn[:, t % 2, c * P:(c + 1) * P], ident[:, :])
                    last.then_inc(q_t, 1)
            pe.wait_ge(rem_in, 48)
            pe.wait_ge(ln_lo, TILES)
            for c in range(C):
                last = pe.transpose(pT0[:, c, :], rem_raw[:, c * P:(c + 1) * P], ident[:, :])
            last.then_inc(rem_pe, 1)
            pe.wait_ge(rem_dve, 2)
            pe.wait_ge(q_n, TILES)
            pe.wait_ge(w_lo[JOB["xk"]], 1)
            ctx_rows = lambda u, t: (lambda s, c: ctxT[:, u, s, c, t * P:(t + 1) * P])
            wk = weight(wkv, 0, D)
            split_products(pe, pK0[:, :], ctx_rows(0, 0), wk, C).then_inc(rem_pe, 1)
            pe.wait_ge(rem_dve, 4)
            for c in range(C):
                last = pe.transpose(pT1[:, c, :], kn[:, 0, c * P:(c + 1) * P], ident[:, :])
            last.then_inc(rem_pe, 1)

            def ctx_turn(n, u, turn):
                pe.wait_ge(ctx_in[u], turn * 16)
                for t in range(MT):
                    for c in range(C):
                        last = pe.transpose(pTT[t][:, c, :], ctx_raw[:, u, t, c * P:(c + 1) * P], ident[:, :])
                    last.then_inc(ctx_t, 1)

            def k_half(b, t, u):
                pe.wait_ge(ctx_lo, b * MT + t + 1)
                split_products(pe, pKV[t][:, :], ctx_rows(u, t), wk, C).then_inc(k_mm, 1)

            def out_tile(t):
                pe.wait_ge(pc_lo, (t + 1) * BT * 2)
                for c in range(C):
                    o = (pV1[:, :], pP_flat)[c // 2][:, (c % 2) * 2 * P:(c % 2 + 1) * 2 * P]
                    last = split_products(pe, o, lambda s, k: wkv[:, s, k, D + c * P:D + (c + 1) * P],
                                          lambda s, k: z_p[:, s, k, c * 2 * P:(c + 1) * 2 * P], C)
                    if c % 2:
                        last.then_inc(o_mm, 1)

            def batch(tile, r, main=True, prev=True, nxt=True, first=False):
                b = tile * BT + r
                u, pr = r % 2, (r - 1) % BT
                if prev:
                    pe.wait_ge(k_lo, b * MT)
                    for g in range(G):
                        for j in range(2):
                            c = 2 * g + j
                            qb = lambda s, _: qblk[:, s].rearrange("p c n -> p (c n)")[:, c * P - j * HD:(c + 1) * P - j * HD]
                            last = split_products(pe, pS[:, g, 0:M + 1], qb, lambda s, _: kT[:, s, c, :], 1,
                                                  start=j == 0, stop=j == 1)
                    last.then_inc(sc_mm, 1)
                if nxt:
                    if not prev:
                        pe.wait_ge(ctx_lo, b * MT + 2)
                    ctx_turn(b + 1, 1 - u, tile * 2 + (r + 1) // 2 + 1)
                if main:
                    if prev:
                        pe.wait_ge(k_n, b * MT)
                    k_half(b, 1, u)
                if prev and pr == 0 and not first:
                    out_tile(tile - 1)
                if nxt:
                    pe.wait_ge(k_n, b * MT + 1)
                    pe.wait_ge(ctx_lo, b * MT + 3)
                    split_products(pe, pK0[:, :], ctx_rows(1 - u, 0), wk, C - 1, stop=False)
                if prev:
                    pe.wait_ge(p_n, b * G)
                    if not first:
                        pe.wait_ge(pc_lo, b * 2 - 2)
                        if pr == 0:
                            pe.wait_ge(o_out, tile * 4)
                    for t in range(MT):
                        for g in range(G):
                            last = pe.transpose(pP[:, t, g * P:(g + 1) * P], prob[:, g, t * P:(t + 1) * P], ident[:, :])
                    last.then_inc(p_t, 1)
                if nxt:
                    split_products(pe, pK0[:, :], ctx_rows(1 - u, 0), wk, C, start=False, first=C - 1).then_inc(k_mm, 1)
                if prev:
                    pe.wait_ge(p_r, b * G)
                    for g in range(G):
                        last = pe.transpose(pV1[:, g * P:(g + 1) * P], p_rem[:, g, :], ident[:, :])
                    last.then_inc(p_rt, 1)
                if main:
                    pe.wait_ge(k_n, b * MT + 2)
                    if nxt:
                        pe.wait_ge(ctx_lo, b * MT + 4)
                    for t in range(MT):
                        for c in range(C):
                            last = pe.transpose(pTT[t][:, c, :], kn[:, t, c * P:(c + 1) * P], ident[:, :])
                        last.then_inc(k_t, 1)
                if prev:
                    pe.wait_ge(cn_lo, b)
                    for g in range(2):
                        if g == 0:
                            pe.wait_ge(p_rl, b)
                        pe.wait_ge(p_lo, b)
                        for j in range(2):
                            c = 2 * g + j
                            o = pC[g][:, j * G * P:(j + 1) * G * P]
                            pe.matmul(o, rem_p[:, c * P:(c + 1) * P], pT_rem[:, :], start=True, stop=False)
                            last = split_products(pe, o, lambda s, t: ctxN[:, 1 - u, s, t, c * P:(c + 1) * P],
                                                  lambda s, t: pT[:, s, t, :], MT, start=False)
                        last.then_inc(pc_mm, 1)

            pe.wait_ge(rem_act, 6)
            ctx_turn(0, 0, 1)
            k_half(0, 0, 0)
            for r in range(BT):
                if r == 1:
                    pe.wait_ge(q_out, TILES)
                    pe.wait_ge(w_lo[JOB["xv"]], 1)
                batch(0, r, prev=r > 0, first=r == 1)
            with pe.Fori(1, TILES - 1) as k:
                for r in range(BT):
                    batch(k, r)
            for r in range(BT):
                batch(TILES - 1, r, nxt=r < BT - 1)
            batch(TILES, 0, main=False, nxt=False)
            out_tile(TILES - 1)

            pe.wait_ge(w_lo[JOB["xo"]], 1)
            for s in range(TILES + 2):
                if s < TILES:
                    pe.wait_ge(oT_lo, s + 1)
                    if s >= 2:
                        pe.wait_ge(x1_add, s - 1)
                    split_products(pe, pKV[s % 2][:, :], tile_of(lhs_p, s % 2), weight(xo_p),
                                   C).then_inc(xo_mm, 1)
                if s >= 2:
                    ln_turn(TILES + s - 2)
            for n in range(3 * TILES):
                w, t = divmod(n, TILES)
                if t == 0:
                    pe.wait_ge(w_lo[JOB[("aq", "ak", "av")[w]]], 1)
                if w == 0:
                    pe.wait_ge(ln_lo, TILES + t + 1)
                if n >= 3:
                    pe.wait_ge(z_c, n - 2)
                split_products(pe, pZ[n % 3][:, :], rows_of(xT, t), weight(w_slot[:, w % 2]), C).then_inc(z_mm, 1)
                if n == 2 * TILES + 1:
                    pe.wait_ge(t_step, TILES)
                    for g in range(2):
                        last = pe.matmul(pS[:, g, :], ones[:, :],
                                         a_all[:, g * C:(g + 1) * C, :].rearrange("p t n -> p (t n)"),
                                         start=True, stop=True)
                    last.then_inc(t_pe, 1)
            pe.wait_ge(z_c, 3 * TILES)
            pe.wait_ge(z_sig, 3 * TILES)
            pe.wait_ge(t_step, TILES + 7)
            pe.wait_ge(gw_lo, 1)
            for s in range(TILES + 3):
                if s < TILES:
                    if s >= 2:
                        pe.wait_ge(av_lo, s - 1)
                    for c in range(C):
                        last = pe.matmul(pAV[s % 2][:, c, :], v_self[:, s, c * P:(c + 1) * P], a_all[:, s, :],
                                         start=True, stop=True)
                    last.then_inc(av_mm, 1)
                t = s - 1
                if 0 <= t < TILES:
                    pe.wait_ge(av_lo, t + 1)
                    if t == 0:
                        pe.wait_ge(w_lo[JOB["ao"]], 1)
                    if t >= 2:
                        pe.wait_ge(x2_add, t - 1)
                    split_products(pe, pKV[t % 2][:, :], tile_of(lhs_p, t % 2), weight(w_slot[:, 1]),
                                   C).then_inc(ao_mm, 1)
                t = s - 2
                if 0 <= t < TILES:
                    ln_turn(2 * TILES + t)
                t = s - 3
                if t >= 0:
                    pe.wait_ge(ln_lo, 2 * TILES + t + 1)
                    split_products(pe, p_gate[:, t, :], rows_of(xT, t), weight(gw_p, 0, E), C).then_inc(g_mm, 1)

            def hidden_turn(n, u, reused):
                pe.wait_ge(u_h, n + 1)
                if reused:
                    pe.wait_ge(h_lo, n - 1)
                for c in range(2):
                    last = pe.transpose(pTT[u][:, c, :], xn[:, u, c * P:(c + 1) * P], ident[:, :])
                last.then_inc(h_t, 1)

            def hidden_out(n, u, w, reused):
                pe.wait_ge(h_lo, n + 1)
                if reused:
                    pe.wait_ge(y_add, n - 1)
                w2_of = lambda s, c: e_p[w][:, s, (C + c) * D:(C + c + 1) * D]
                split_products(pe, pY[u], tile_of(hT, u), w2_of, 2).then_inc(y_mm, 1)

            def expert(e, u, prev=True):
                pe.wait_ge(e_lo, e + 1)
                w13 = lambda s, c: e_p[u][:, s, c * D:(c + 1) * D]
                for t in range(TILES):
                    n = e * TILES + t
                    if prev or t >= 2:
                        pe.wait_ge(u_h, n - 1)
                    split_products(pe, pKV[t % 2][:, :], rows_of(xT, t), w13, C).then_inc(u_mm, 1)
                    if prev or t >= 1:
                        hidden_turn(n - 1, (t - 1) % 2, prev or t >= 3)
                    if prev or t >= 2:
                        hidden_out(n - 2, t % 2, u if t >= 2 else 1 - u, prev or t >= 4)

            expert(0, 0, prev=False)
            with pe.Fori(0, (E - 2) // 2) as k:
                expert(k * 2 + 1, 1)
                expert(k * 2 + 2, 0)
            expert(E - 1, 1)
            hidden_turn(E * TILES - 1, 1, True)
            hidden_out(E * TILES - 2, 0, 1, True)
            hidden_out(E * TILES - 1, 1, 1, True)


_INS = ["x", "ctx_1024", "mask_BxSxS2_bk0", "L0_xattn_Wq", "L0_xattn_Wkv", "L0_xattn_Wo", "L0_xattn_qn_w",
        "L0_xattn_kn_w", "L0_attn_Wq", "L0_attn_gq", "L0_attn_bq", "L0_attn_mq", "L0_attn_vq", "L0_attn_Wk",
        "L0_attn_gk", "L0_attn_bk", "L0_attn_mk", "L0_attn_vk", "L0_attn_Wv", "L0_attn_gv", "L0_attn_bv",
        "L0_attn_mv", "L0_attn_vv", "L0_attn_Wo", "L0_attn_bo", "L0_ffn_gate_w", "L0_ffn_w1", "L0_ffn_w2",
        "L0_ffn_w3"]


def kernel(**inputs):
    import numpy as _np
    import concourse.bacc as _bacc
    from concourse import mybir as _mybir
    from concourse.bass_utils import run_bass_kernel_spmd as _run

    nc = _bacc.Bacc("TRN2", target_bir_lowering=False, num_devices=1)
    arrays, args = {}, []
    for name in _INS:
        a = _np.ascontiguousarray(inputs[name])
        arrays[f"in_{name}_dram"] = a
        args.append(nc.dram_tensor(f"in_{name}_dram", a.shape, _mybir.dt.from_np(a.dtype), kind="ExternalInput").ap())
    shape = inputs["x"].shape
    args.append(nc.dram_tensor("out_0_dram", shape, _mybir.dt.float32, kind="ExternalOutput").ap())
    perceiver_block(nc, *args)
    r = _run(nc, [arrays], core_ids=[0])
    return r.results[0]["out_0_dram"]
```

```python
from contextlib import ExitStack

import concourse.bass as bass
from concourse import mybir

F32 = mybir.dt.float32
F32R = mybir.dt.float32r
U8 = mybir.dt.uint8
ALU = mybir.AluOpType
ACT = mybir.ActivationFunctionType
AX = mybir.AxisListType

P = 128
HI, LO = 0, 1
BIG = 3.0e38
ROOTS = "natural_log_exp_and_others"
LN_EPS, HEAD_EPS, BN_EPS = 1e-5, 1e-6, 1e-5
V_TH, SLOPE = 1.0, 4.0
A_STDP, TAU, W_OFF = 0.9, 0.5, 0.9


def split_products(pe, out, lhs, rhs, chunks, start=True, stop=True, first=0):
    last = None
    for c in range(first, chunks):
        for n, (a, b) in enumerate(((HI, HI), (HI, LO), (LO, HI))):
            last = pe.matmul(out, lhs(a, c), rhs(b, c), start=start and c == first and n == 0,
                             stop=stop and c == chunks - 1 and n == 2)
    return last


def perceiver_block(nc, x, ctx, mask, xWq, xWkv, xWo, qn_w, kn_w, aWq, gq, bq, mq, vq, aWk, gk, bk, mk, vk,
                    aWv, gv, bv, mv, vv, aWo, bo, gate_w, w1, w2, w3, out):
    B, S, D = x.shape
    M = ctx.shape[1]
    H, HD = qn_w.shape
    E, _, F = w1.shape
    TILES = B * S // P
    C = D // P
    BT = P // S
    MT = M // P
    HG = P // S
    G = H // HG
    RAW = C * D + 2 * D
    SCALE = float(HD) ** -0.5
    assert M == MT * P + 1 and MT == 2 and G == 2 and C == 4 and 2 * HD == P and H == 8 and F == 2 * P
    assert B == TILES * BT and TILES == 8 and B % 2 == 0 and E == 8

    x_t = x.rearrange("b s d -> (b s) d").rearrange("(t p) d -> p t d", p=P)
    out_t = out.rearrange("b s d -> (b s) d").rearrange("(t p) d -> p t d", p=P)

    def chunked(w):
        return w.rearrange("(c p) n -> p c n", p=P)

    def spread(v):
        return v.partition_broadcast(P)

    with ExitStack() as es:
        def sb(name, shape, dt=F32):
            return es.enter_context(nc.sbuf_tensor(name, shape, dt))

        def ps(name, shape):
            return es.enter_context(nc.psum_tensor(name, shape, F32))

        def sem(name):
            return es.enter_context(nc.semaphore(name))

        ident = sb("ident", [P, P])
        ones = sb("ones", [P, P])
        same_seq = sb("same_seq", [P, P])
        col = sb("col", [P, P])
        batch_col = sb("batch_col", [P, P])
        x_all = sb("x_all", [P, TILES, D])
        bias = sb("bias", [P, 4])
        LN_B, HEAD_B, BN_B, SIG_B = (bias[:, i:i + 1] for i in range(4))
        xn = sb("xn", [P, 2, D])
        bst = sb("bst", [P, 2, 6])
        mean_var = sb("mean_var", [P, 2, 2])
        ln_log = sb("ln_log", [P, 2, 1])
        ln_rs = sb("ln_rs", [P, 2, 1])
        wide = sb("wide", [P, 2 * RAW])
        w_raw = wide[:, 0:2 * C * D].rearrange("p (u c n) -> p u c n", u=2, c=C)
        ctx_raw = wide[:, 2 * C * D:2 * RAW].rearrange("p (u t d) -> p u t d", u=2, t=MT)
        raw_of = {"ao": wide[:, 2 * C * D:3 * C * D].rearrange("p (c n) -> p c n", c=C)}
        e_raw = wide[:, :].rearrange("p (u n) -> p u n", u=2)
        qoT = sb("qoT", [P, C, TILES * P])
        v_self = qoT[:, :, :].rearrange("p c n -> p (c n)").rearrange("p (t d) -> p t d", t=TILES)
        sq = sb("sq", [P, 2, D])
        kn = sb("kn", [P, 2, D])
        head_ss = sb("head_ss", [P, 2, H])
        head_log = sb("head_log", [P, 2, H])
        head_rs = sb("head_rs", [P, 2, H])
        head_mean = sb("head_mean", [P, C, H])
        qkw = sb("qkw", [P, 2, D])
        qk_col = sb("qk_col", [P, 3, C])
        kT_rem = sb("kT_rem", [P, C, B])
        rem_raw = sb("rem_raw", [P, D])
        s_m = sb("s_m", [P, G, M + 1])
        prob = sb("prob", [P, G, M + 1])
        neg_max = sb("neg_max", [P, G])
        p_sum = sb("p_sum", [P, G])
        p_den = sb("p_den", [P, G])
        p_inv = sb("p_inv", [P, G])
        p_scale = sb("p_scale", [P, G])
        p_rem = sb("p_rem", [P, G, P])
        mask_f = sb("mask_f", [P, B * M // 4])
        masked = mask_f[:, :].bitcast(U8).rearrange("p (b m) -> p b m", b=B)
        bn_vec = mask_f[:, 0:4 * D].rearrange("p (v d) -> p v d", v=4)
        rows = sb("rows", [P, 2, TILES])
        gw_raw = sb("gw_raw", [P, C, E])
        tri = sb("tri", [P, E, E])
        gates = sb("gates", [P, TILES, E])
        g_tmp = sb("g_tmp", [P, TILES, E])
        g_red = sb("g_red", [P, TILES])
        g_now = sb("g_now", [P, 2, TILES])
        parts = sb("parts", [P, 8 * C * D], F32R)
        wkv = parts[:, 0:4 * C * D].rearrange("p (s c n) -> p s c n", s=2, c=C)
        ctxT = parts[:, 4 * C * D:6 * C * D].rearrange("p (u s c n) -> p u s c n", u=2, s=2, c=C)
        ctxN = parts[:, 6 * C * D:8 * C * D].rearrange("p (u s t d) -> p u s t d", u=2, s=2, t=MT)
        xT = parts[:, 0:4 * C * D].rearrange("p (s c n) -> p s c n", s=2, c=C)
        lhs_p = parts[:, 7 * C * D:8 * C * D].rearrange("p (u s c n) -> p u s c n", u=2, s=2, c=C)
        out_p = parts[:, 6 * C * D:7 * C * D].rearrange("p (u s c n) -> p u s c n", u=2, s=2, c=C)
        hT = parts[:, 7 * C * D:7 * C * D + 8 * P].rearrange("p (u s c n) -> p u s c n", u=2, s=2, c=2)
        kT = sb("kT", [P, 2, C, M + 1], F32R)
        qblk = sb("qblk", [P, 2, C, P], F32R)
        pT = sb("pT", [P, 2, MT, G * P], F32R)
        w_p = sb("w_p", [P, 4 * C * D], F32R)
        w_slot = w_p[:, :].rearrange("p (u s c n) -> p u s c n", u=2, s=2, c=C)
        z_p = w_p[:, :].rearrange("p (s c n) -> p s c n", s=2, c=C)
        z_b = w_p[:, :].rearrange("p (s c h b q) -> p s c h b q", s=2, c=C, h=H, b=BT)
        rem_p = sb("rem_p", [P, D], F32R)
        pT_rem = sb("pT_rem", [P, G * P], F32R)
        gw_p = sb("gw_p", [P, 2, C, E], F32R)
        e_p = [parts[:, 4 * C * D:4 * C * D + 2 * RAW].rearrange("p (s n) -> p s n", s=2),
               w_p[:, 0:2 * RAW].rearrange("p (s n) -> p s n", s=2)]

        pK0, pK1, pV1 = ps("pK0", [P, D]), ps("pK1", [P, D]), ps("pV1", [P, D])
        pT0, pT1 = ps("pT0", [P, C, P]), ps("pT1", [P, C, P])
        pS = ps("pS", [P, G, 512])
        pP = ps("pP", [P, MT, G * P])
        pKV, pTT, pZ = (pK0, pK1), (pT0, pT1), (pV1, pK0, pK1)

        const_set = sem("const_set")
        ident_step = sem("ident_step")
        x_in = [sem("x_in0"), sem("x_in1")]
        qn_in, kn_in, rem_in, mask_in, gate_in, bo_in = (sem(n) for n in (
            "qn_in", "kn_in", "rem_in", "mask_in", "gate_in", "bo_in"))
        JOBS = ("xq", "xk", "xv", "xo", "aq", "ak", "av", "ao")
        w_in, w_pre, w_hi, w_lo = ([sem(f"{what}_{j}") for j in JOBS] for what in ("w_in", "w_pre", "w_hi", "w_lo"))
        w_sum = sem("w_sum")
        ln_bst, ln_mv, ln_lg, ln_rsd, ln_x, ln_t, ln_hi, ln_lo = (sem(n) for n in (
            "ln_bst", "ln_mv", "ln_lg", "ln_rsd", "ln_x", "ln_t", "ln_hi", "ln_lo"))
        bias_set, qk_set = sem("bias_set"), sem("qk_set")
        q_mm, q_sq, q_ss, q_lg, q_rs, q_n, q_t, q_out = (sem(n) for n in (
            "q_mm", "q_sq", "q_ss", "q_lg", "q_rs", "q_n", "q_t", "q_out"))
        rem_pe, rem_act, rem_dve = sem("rem_pe"), sem("rem_act"), sem("rem_dve")
        not_mask = sem("not_mask")
        ctx_in = [sem("ctx_in0"), sem("ctx_in1")]
        ctx_t, ctx_hi, ctx_lo = sem("ctx_t"), sem("ctx_hi"), sem("ctx_lo")
        k_mm, k_sq, k_ss, k_lg, k_rs, k_n, k_t, k_hi, k_lo, k_rem = (sem(n) for n in (
            "k_mm", "k_sq", "k_ss", "k_lg", "k_rs", "k_n", "k_t", "k_hi", "k_lo", "k_rem"))
        cn_hi, cn_lo = sem("cn_hi"), sem("cn_lo")
        pc_mm, pc_hi, pc_lo = sem("pc_mm"), sem("pc_hi"), sem("pc_lo")
        qb_hi = sem("qb_hi")
        sc_mm, sc_m, sc_max, sc_exp, sc_step, p_n, p_r = (sem(n) for n in (
            "sc_mm", "sc_m", "sc_max", "sc_exp", "sc_step", "p_n", "p_r"))
        p_t, p_rt, p_hi, p_lo, p_rh, p_rl, o_mm, o_out = (sem(n) for n in (
            "p_t", "p_rt", "p_hi", "p_lo", "p_rh", "p_rl", "o_mm", "o_out"))
        oT_hi, oT_lo, xo_mm, x1_add = sem("oT_hi"), sem("oT_lo"), sem("xo_mm"), sem("x1_add")
        bn_in = [sem(f"bn_in{i}") for i in range(3)]
        bn_lg, bn_rs, bn_a, bn_ma, bn_c = (sem(n) for n in ("bn_lg", "bn_rs", "bn_a", "bn_ma", "bn_c"))
        z_mm, z_c, z_sig = sem("z_mm"), sem("z_c"), sem("z_sig")
        t_step, t_pe, t_act = sem("t_step"), sem("t_pe"), sem("t_act")
        av_mm, av_hi, av_lo, ao_mm, bo_add, x2_add = (sem(n) for n in (
            "av_mm", "av_hi", "av_lo", "ao_mm", "bo_add", "x2_add"))
        gw_hi, gw_lo, g_mm, g_row, g_t, g_step, g_exp = (sem(n) for n in (
            "gw_hi", "gw_lo", "g_mm", "g_row", "g_t", "g_step", "g_exp"))
        e_in = [sem("e_in0"), sem("e_in1")]
        e_hi, e_lo, g_col = sem("e_hi"), sem("e_lo"), sem("g_col")
        u_mm, u_sig, u_h, h_t, h_hi, h_lo, y_mm, y_add = (sem(n) for n in (
            "u_mm", "u_sig", "u_h", "h_t", "h_hi", "h_lo", "y_mm", "y_add"))
        stored = sem("stored")

        xo_p = parts[:, 4 * C * D:6 * C * D].rearrange("p (s c n) -> p s c n", s=2, c=C)
        jobs = {
            "xq": (chunked(xWq), w_slot[:, 0]),
            "xk": (chunked(xWkv[:, 0:D]), wkv[:, :, :, 0:D]),
            "xv": (chunked(xWkv[:, D:2 * D]), wkv[:, :, :, D:2 * D]),
            "xo": (chunked(xWo), xo_p),
            "aq": (chunked(aWq), w_slot[:, 0]),
            "ak": (chunked(aWk), w_slot[:, 1]),
            "av": (chunked(aWv), w_slot[:, 0]),
            "ao": (chunked(aWo), w_slot[:, 1]),
        }
        JOB = {n: i for i, n in enumerate(JOBS)}
        bn_src = ((gq, bq, mq, vq), (gk, bk, mk, vk), (gv, bv, mv, vv))
        bn_ac = ((qkw[:, 0, :], qkw[:, 1, :]),
                 (s_m[:, :, :].rearrange("p g m -> p (g m)")[:, 0:D], prob[:, :, :].rearrange("p g m -> p (g m)")[:, 0:D]),
                 (qkw[:, 0, :], qkw[:, 1, :]))
        raw = lambda name: raw_of.get(name, w_raw[:, JOB[name] % 2])
        heads = lambda ap: ap.rearrange("p (h d) -> p h d", h=H)
        per_head = lambda ap: ap.unsqueeze(2).broadcast_to([P, H, HD])

        dt_all = xn[:, :, :].rearrange("p u d -> p (u d)").rearrange("p (t n) -> p t n", t=TILES)
        a_all = kn[:, :, :].rearrange("p u d -> p (u d)").rearrange("p (t n) -> p t n", t=TILES)
        pAV = (pP[:, :, :].rearrange("p t n -> p (t n)").rearrange("p (c n) -> p c n", c=C),
               pV1[:, :].rearrange("p (c n) -> p c n", c=C))
        pY = (pV1[:, :], pP[:, :, :].rearrange("p t n -> p (t n)"))
        pP_flat = pP[:, :, :].rearrange("p t n -> p (t n)")
        p_gate = pS[:, 0, 0:TILES * E].rearrange("p (t e) -> p t e", t=TILES)
        cmp_gt = s_m[:, :, :].rearrange("p g m -> p (g m)")[:, 0:TILES * E * E].rearrange(
            "p (t e j) -> p t e j", t=TILES, e=E)
        cmp_eq = prob[:, :, :].rearrange("p g m -> p (g m)")[:, 0:TILES * E * E].rearrange(
            "p (t e j) -> p t e j", t=TILES, e=E)

        pC = (pV1[:, :], pP_flat)
        prob_ctx = lambda g: pC[g].rearrange("p (c h q) -> p c h q", c=2, h=H)

        block = es.enter_context(nc.Block())

        @block.sync
        def _(sp):
            def load_weight(name, freed_by=None):
                j = JOB[name]
                if freed_by is not None:
                    sp.wait_ge(w_lo[JOB[freed_by]], C)
                    sp.wait_ge(w_hi[JOB[freed_by]], C)
                sp.dma_start(raw(name), jobs[name][0]).then_inc(w_in[j], 16)

            sp.dma_start(x_all[:, 0:2, :], x_t[:, 0:2, :]).then_inc(x_in[0], 16)
            load_weight("xq")
            sp.dma_start(x_all[:, 2:TILES, :], x_t[:, 2:TILES, :]).then_inc(x_in[1], 16)
            for i, (w, loaded) in enumerate(((qn_w, qn_in), (kn_w, kn_in))):
                cols = w.rearrange("(c e) d -> (e d) c", c=C)
                sp.dma_start(qk_col[:, i, :], cols, allow_slow_non_contiguous=True).then_inc(loaded, 16)
            load_weight("xk")
            sp.wait_ge(const_set, 1)
            for r in range(3):
                sp.dma_start(rem_raw[r * B:(r + 1) * B, :], ctx[:, M - 1, :]).then_inc(rem_in, 16)
            load_weight("xv", "xq")
            for b in range(2):
                sp.dma_start(ctx_raw[:, b], ctx[b, 0:MT * P, :].rearrange("(t p) d -> p t d", p=P)).then_inc(ctx_in[b], 16)
            for g in range(HG):
                sp.dma_start(masked[g * S:(g + 1) * S], mask.rearrange("b s m -> s b m")).then_inc(mask_in, 16)
            sp.dma_start(gw_raw[:, :, :], chunked(gate_w)).then_inc(gate_in, 16)
            load_weight("xo", "xk")
            load_weight("aq", "xv")

            with sp.Fori(0, (B - 2) // 2) as k:
                for u in range(2):
                    sp.wait_ge(ctx_t, (k * 2 + u + 1) * MT)
                    sp.wait_ge(cn_lo, (k * 2 + u + 1))
                    src = ctx[bass.ds(k * 2 + u + 2, 1), 0:MT * P, :].rearrange("b (t p) d -> p (b t) d", p=P)
                    sp.dma_start(ctx_raw[:, u], src).then_inc(ctx_in[u], 16)
            sp.wait_ge(sc_m, B)
            for i in range(4):
                sp.dma_start(bn_vec[:, i, :], spread(bn_src[0][i])).then_inc(bn_in[0], 16)
            sp.dma_start(rem_raw[:, :], spread(bo)).then_inc(bo_in, 16)
            sp.wait_ge(cn_lo, B)
            load_weight("ao")
            load_weight("ak", "xo")
            for w in range(1, 3):
                sp.wait_ge(bn_c, w)
                for i in range(4):
                    sp.dma_start(bn_vec[:, i, :], spread(bn_src[w][i])).then_inc(bn_in[w], 16)
                if w == 1:
                    load_weight("av", "aq")

            def load_expert(e, u):
                w13 = e_raw[:, u, 0:C * D].rearrange("p (c n) -> p c n", c=C)
                for lo, w in ((0, w1), (F, w3)):
                    sp.dma_start(w13[:, :, lo:lo + F],
                                 w[bass.ds(e, 1)].rearrange("e (c p) f -> p (e c) f", p=P)).then_inc(e_in[u], 16)
                sp.dma_start(e_raw[:, u, C * D:RAW].rearrange("p (c n) -> p c n", c=2),
                             w2[bass.ds(e, 1)].rearrange("e (c p) d -> p (e c) d", p=P)).then_inc(e_in[u], 16)

            for e, name in enumerate(("av", "ao")):
                sp.wait_ge(w_hi[JOB[name]], C)
                sp.wait_ge(w_lo[JOB[name]], C)
                load_expert(e, e)
            with sp.Fori(0, (E - 2) // 2) as k:
                for u in range(2):
                    sp.wait_ge(e_hi, (k * 2 + u) + 1)
                    sp.wait_ge(e_lo, (k * 2 + u) + 1)
                    load_expert(k * 2 + u + 2, u)
            for t in range(TILES):
                sp.wait_ge(y_add, (E - 1) * TILES + t + 1)
                sp.dma_start(out_t[:, t, :], x_all[:, t, :]).then_inc(stored, 16)
            sp.wait_ge(stored, 16 * TILES)

        @block.gpsimd
        def _(pool):
            nc.gpsimd.memset(bias[:, 0:1], LN_EPS)
            nc.gpsimd.memset(bias[:, 1:2], HEAD_EPS)
            nc.gpsimd.memset(bias[:, 2:3], BN_EPS)
            nc.gpsimd.memset(bias[:, 3:4], -SLOPE * V_TH).then_inc(bias_set, 1)
            nc.gpsimd.memset(ident[:, :], 0.0).then_inc(ident_step, 1)
            nc.gpsimd.memset(rem_raw[:, :], 0.0).then_inc(const_set, 1)
            nc.gpsimd.memset(ones[:, :], 1.0)
            nc.gpsimd.memset(same_seq[:, :], 0.0)
            nc.gpsimd.memset(kT[:, :, :, M:M + 1].bitcast(F32), 0.0)
            nc.gpsimd.memset(qblk[:, :, :, :].bitcast(F32), 0.0)
            nc.gpsimd.memset(tri[:, :, :], 1.0)
            nc.gpsimd.memset(rem_p[:, :].bitcast(F32), 0.0)
            nc.gpsimd.memset(batch_col[:, 3 * B:P], -1.0)
            nc.gpsimd.iota(col[:, :], [[1, P]], base=0, channel_multiplier=0, allow_small_or_imprecise_dtypes=True).then_inc(ident_step, 1)
            nc.gpsimd.iota(batch_col[:, 0:3 * B], [[0, 3], [1, B]], base=0, channel_multiplier=0,
                           allow_small_or_imprecise_dtypes=True).then_inc(ident_step, 1)
            pool.wait_ge(ident_step, 3)
            for g in range(BT):
                nc.gpsimd.memset(same_seq[g * S:(g + 1) * S, g * S:(g + 1) * S], 1.0).then_inc(ident_step, 1)
                pool.wait_ge(ident_step, 4 + g)
            nc.gpsimd.affine_select(out=tri[:, :, :], in_=tri[:, :, :], compare_op=ALU.is_ge, fill=0.0, base=-1,
                                    pattern=[[1, E], [-1, E]], channel_multiplier=0)
            nc.gpsimd.affine_select(out=ident[:, :], in_=ident[:, :], compare_op=ALU.not_equal, fill=1.0, base=0,
                                    pattern=[[-1, P]], channel_multiplier=1).then_inc(const_set, 1)

            def low_part(name, chunks=range(C)):
                j = JOB[name]
                dst = jobs[name][1]
                for c in chunks:
                    pool.wait_ge(w_hi[j], c + 1)
                    nc.gpsimd.tensor_tensor(dst[:, LO, c], raw(name)[:, c], dst[:, HI, c].bitcast(F32),
                                            ALU.subtract).then_inc(w_lo[j], 1)

            for name in JOBS[:3]:
                low_part(name)
            pool.wait_ge(mask_in, 16 * HG)
            nc.gpsimd.tensor_scalar(mask_f[:, :].bitcast(U8), mask_f[:, :].bitcast(U8), -1.0, 1.0,
                                    ALU.mult, ALU.add).then_inc(not_mask, 1)
            def ctx_parts(b, u):
                pool.wait_ge(cn_hi, b + 1)
                nc.gpsimd.tensor_tensor(ctxN[:, u, LO], ctx_raw[:, u], ctxN[:, u, HI].bitcast(F32),
                                        ALU.subtract).then_inc(cn_lo, 1)

            with pool.Fori(0, B // 2) as k:
                ctx_parts(k * 2, 0)
                ctx_parts(k * 2 + 1, 1)
            def out_low(t):
                pool.wait_ge(oT_hi, t + 1)
                nc.gpsimd.tensor_tensor(out_p[:, t % 2, LO], qoT[:, :, t * P:(t + 1) * P],
                                        out_p[:, t % 2, HI].bitcast(F32), ALU.subtract).then_inc(oT_lo, 1)

            def bn_weight(w, c):
                name = ("aq", "ak", "av")[w]
                pool.wait_ge(w_in[JOB[name]], 16)
                pool.wait_ge(bn_a, w + 1)
                nc.gpsimd.tensor_tensor(raw(name)[:, c], raw(name)[:, c], bn_ac[w][0],
                                        ALU.mult).then_inc(w_pre[JOB[name]], 1)

            low_part("xo", range(C // 2, C))
            for t in range(TILES):
                if t == C + 1:
                    for c in range(C):
                        bn_weight(0, c)
                out_low(t)
            low_part("aq")
            for c in range(C):
                bn_weight(1, c)
            low_part("ak")
            for c in range(C):
                bn_weight(2, c)
            low_part("av")
            pool.wait_ge(bo_in, 16)
            for t in range(TILES):
                pool.wait_ge(ln_x, TILES + t + 1)
                nc.gpsimd.tensor_tensor(x_all[:, t, :], x_all[:, t, :], rem_raw[:, :], ALU.add).then_inc(bo_add, 1)
            low_part("ao")

            def expert_low(e, u):
                pool.wait_ge(e_hi, e + 1)
                nc.gpsimd.tensor_tensor(e_p[u][:, LO, :], e_raw[:, u, :], e_p[u][:, HI, :].bitcast(F32),
                                        ALU.subtract).then_inc(e_lo, 1)

            expert_low(0, 0)
            with pool.Fori(0, (E - 2) // 2) as k:
                expert_low(k * 2 + 1, 1)
                expert_low(k * 2 + 2, 0)
            expert_low(E - 1, 1)

        @block.scalar
        def _(act):
            def ln_root(n):
                act.wait_ge(ln_mv, n + 1)
                act.activation(ln_log[:, n % 2], mean_var[:, n % 2, 1:2], ACT.Ln, bias=LN_B).then_inc(ln_lg, 1)
                act.wait_ge(ln_lg, n + 1)
                act.activation(ln_rs[:, n % 2], ln_log[:, n % 2], ACT.Exp, scale=-0.5).then_inc(ln_rsd, 1)

            def ln_high(n, dst):
                act.wait_ge(ln_t, n + 1)
                act.activation(dst, pTT[n % 2][:, :, :], ACT.Copy).then_inc(ln_hi, 1)

            def high_part(name, chunks=range(C)):
                j = JOB[name]
                for c in chunks:
                    if name in ("xv", "xo", "ao"):
                        act.wait_ge(w_in[j], 16)
                    else:
                        act.wait_ge(w_pre[j], c + 1)
                    act.activation(jobs[name][1][:, HI, c], raw(name)[:, c], ACT.Copy).then_inc(w_hi[j], 1)

            def ctx_high(n, u):
                for t in range(MT):
                    act.wait_ge(ctx_t, n * MT + t + 1)
                    act.activation(ctxT[:, u, HI, :, t * P:(t + 1) * P], pTT[t][:, :, :], ACT.Copy).then_inc(ctx_hi, 1)

            def k_square(b, t):
                act.wait_ge(k_mm, b * MT + t + 1)
                act.activation(sq[:, t], pKV[t][:, :], ACT.Square).then_inc(k_sq, 1)

            def k_root(b, t):
                act.wait_ge(k_ss, b * MT + t + 1)
                act.activation(head_log[:, t], head_ss[:, t], ACT.Ln, bias=HEAD_B, scale=1.0 / HD).then_inc(k_lg, 1)
                act.wait_ge(k_lg, b * MT + t + 1)
                act.activation(head_rs[:, t], head_log[:, t], ACT.Exp, scale=-0.5).then_inc(k_rs, 1)

            act.preload_act_table_set(ROOTS)
            act.wait_ge(bias_set, 1)
            ln_root(0)
            ln_root(1)
            for s in range(TILES + 2):
                if s == 0:
                    ln_high(0, lhs_p[:, 0, HI])
                    high_part("xq")
                if s == TILES:
                    act.wait_ge(rem_pe, 1)
                    act.activation(ctxT[:, 1, HI, :, 0:P], pAV[0], ACT.Copy).then_inc(rem_act, 1)
                t = s - 1
                if 0 <= t < TILES:
                    act.wait_ge(q_mm, t + 1)
                    if t >= 2:
                        act.wait_ge(q_ss, t - 1)
                    act.activation(sq[:, t % 2], pKV[t % 2][:, :], ACT.Square).then_inc(q_sq, 1)
                    act.wait_ge(q_ss, t + 1)
                    act.activation(head_log[:, t % 2], head_ss[:, t % 2], ACT.Ln, bias=HEAD_B,
                                   scale=1.0 / HD).then_inc(q_lg, 1)
                    act.wait_ge(q_lg, t + 1)
                    if t >= 2:
                        act.wait_ge(q_n, t - 1)
                    act.activation(head_rs[:, t % 2], head_log[:, t % 2], ACT.Exp, scale=-0.5).then_inc(q_rs, 1)
                if s + 2 < TILES:
                    ln_root(s + 2)
                if s + 1 < TILES:
                    if s >= 1:
                        act.wait_ge(q_mm, s)
                    ln_high(s + 1, lhs_p[:, (s + 1) % 2, HI])
                if s == TILES:
                    ctx_high(0, 0)
                if 2 <= s <= C + 1:
                    high_part("xk", (s - 2,))
                if C + 1 < s <= 2 * C + 1:
                    high_part("xv", (s - 2 - C,))
                t = s - 2
                if t >= 0:
                    if t == 0:
                        act.wait_ge(qk_set, 1)
                    act.wait_ge(q_t, t + 1)
                    for c in range(C):
                        act.activation(qoT[:, c, t * P:(t + 1) * P], pS[:, t % 2, c * P:(c + 1) * P], ACT.Copy,
                                       scale=qk_col[:, 2, c:c + 1]).then_inc(q_out, 1)
            act.wait_ge(rem_in, 48)
            act.activation(rem_p[0:3 * B, :], rem_raw[0:3 * B, :], ACT.Copy).then_inc(rem_act, 1)
            act.wait_ge(rem_pe, 2)
            act.activation(sq[:, 1], pV1[:, :], ACT.Square).then_inc(rem_act, 1)
            act.wait_ge(rem_dve, 3)
            act.activation(head_log[:, 1], head_ss[:, 1], ACT.Ln, bias=HEAD_B, scale=1.0 / HD).then_inc(rem_act, 1)
            act.wait_ge(rem_act, 4)
            act.wait_ge(q_n, TILES)
            act.activation(head_rs[:, 1], head_log[:, 1], ACT.Exp, scale=-0.5).then_inc(rem_act, 1)
            k_square(0, 0)
            k_root(0, 0)

            def batch(tile, r, main=True, prev=True, nxt=True, first=False):
                b = tile * BT + r
                u, pr = r % 2, (r - 1) % BT
                if nxt:
                    ctx_high(b + 1, 1 - u)
                if prev:
                    act.wait_ge(sc_max, b)
                    if not first:
                        act.wait_ge(p_rt, b - 1)
                    for g in range(G):
                        act.activation(prob[:, g, 0:M], s_m[:, g, 0:M], ACT.Exp, bias=neg_max[:, g:g + 1],
                                       accum_out=p_sum[:, g:g + 1]).then_inc(sc_exp, 1)
                if main:
                    act.activation(ctxN[:, u, HI], ctx_raw[:, u], ACT.Copy).then_inc(cn_hi, 1)
                    k_square(b, 1)
                if not prev:
                    act.wait_ge(rem_pe, 3)
                    act.activation(kT_rem[:, :, :], pAV[0][:, :, 0:B], ACT.Copy).then_inc(rem_act, 1)
                if prev:
                    act.wait_ge(sc_step, b * 3)
                    for g in range(G):
                        act.activation(prob[:, g, 0:M], prob[:, g, 0:M], ACT.Copy,
                                       scale=p_scale[:, g:g + 1]).then_inc(p_n, 1)
                if not main:
                    out_high(2)
                if main:
                    k_root(b, 1)
                if prev:
                    act.wait_ge(p_t, b)
                    act.activation(pT[:, HI], pP[:, :, :], ACT.Copy).then_inc(p_hi, 1)
                    act.wait_ge(p_rt, b)
                    act.activation(pT_rem[:, :], pV1[:, 0:G * P], ACT.Copy).then_inc(p_rh, 1)
                if not main:
                    out_high(3)
                    ln_root(TILES)
                    bn_root(0)
                if nxt:
                    k_square(b + 1, 0)
                if main:
                    for t in range(MT):
                        act.wait_ge(k_t, b * MT + t + 1)
                        act.activation(kT[:, HI, :, t * P:(t + 1) * P], pTT[t][:, :, :], ACT.Copy).then_inc(k_hi, 1)
                if nxt:
                    k_root(b + 1, 0)
                if main and not nxt:
                    high_part("xo")
                if prev:
                    if pr == 0 and not first:
                        act.wait_ge(o_mm, tile * 2)
                    for g in (1, 0):
                        act.wait_ge(pc_mm, (b - 1) * 2 + 2 - g)
                        act.activation(z_b[:, HI, 2 * g:2 * g + 2, :, pr, :], prob_ctx(g), ACT.Copy).then_inc(pc_hi, 1)

            def bn_root(w):
                act.wait_ge(bn_in[w], 64)
                act.activation(bn_vec[:, 3, :], bn_vec[:, 3, :], ACT.Ln, bias=BN_B).then_inc(bn_lg, 1)
                act.wait_ge(bn_lg, w + 1)
                act.activation(bn_vec[:, 3, :], bn_vec[:, 3, :], ACT.Exp, scale=-0.5).then_inc(bn_rs, 1)

            def out_high(t):
                if t >= 2:
                    act.wait_ge(xo_mm, t - 1)
                act.activation(out_p[:, t % 2, HI], qoT[:, :, t * P:(t + 1) * P], ACT.Copy).then_inc(oT_hi, 1)

            for r in range(BT):
                batch(0, r, prev=r > 0, first=r == 1)
            with act.Fori(1, TILES - 1) as k:
                for r in range(BT):
                    batch(k, r)
            for r in range(BT):
                batch(TILES - 1, r, nxt=r < BT - 1)
            out_high(0)
            out_high(1)
            batch(TILES, 0, main=False, nxt=False)

            out_high(4)
            ln_root(TILES + 1)
            out_high(5)
            for t in range(2, TILES + 2):
                if t < TILES:
                    ln_root(TILES + t)
                ln_high(TILES + t - 2, xT[:, HI, :, (t - 2) * P:(t - 1) * P])
                if t + 4 < TILES:
                    if t + 5 == TILES:
                        act.wait_ge(o_out, 4 * TILES)
                    out_high(t + 4)
                if t == 5:
                    bn_root(1)
                if 3 <= t < 5:
                    high_part("aq", (2 * (t - 3), 2 * (t - 3) + 1))
            bn_root(2)

            def expert_high(e, u, turn):
                act.wait_ge(e_in[u], turn * 48)
                act.activation(e_p[u][:, HI, :], e_raw[:, u, :], ACT.Copy).then_inc(e_hi, 1)

            for n in range(3 * TILES):
                w, t = divmod(n, TILES)
                act.wait_ge(z_c, n + 1)
                if w < 2:
                    act.wait_ge(ln_t, 2 * TILES)
                    if n >= 2:
                        act.wait_ge(z_sig, n - 1)
                    act.activation(xn[:, n % 2], sq[:, n % 2], ACT.Sigmoid, bias=SIG_B, scale=SLOPE,
                                   accum_out=rows[:, w, t:t + 1]).then_inc(z_sig, 1)
                else:
                    act.activation(v_self[:, t], sq[:, n % 2], ACT.Sigmoid, bias=SIG_B, scale=SLOPE).then_inc(z_sig, 1)
                if n < C:
                    high_part("ak", (n,))
                if TILES + 3 <= n < TILES + 3 + C:
                    high_part("av", (n - TILES - 3,))
                if n == 2 * TILES - 1:
                    act.wait_ge(gate_in, 16)
                    act.activation(gw_p[:, HI], gw_raw[:, :, :], ACT.Copy).then_inc(gw_hi, 1)
                if n == 2 * TILES:
                    high_part("ao")
                if n == 2 * TILES + 2:
                    expert_high(0, 0, 1)
                if n == 2 * TILES + 4:
                    act.wait_ge(t_step, TILES + 4)
                    act.activation(kn[:, :, :], kn[:, :, :], ACT.Exp, scale=-1.0 / TAU).then_inc(t_act, 1)
            def gate_copy(k):
                act.wait_ge(g_mm, k + 1)
                act.activation(sq[0:E, k % 2, 0:2 * P], pS[0:E, 1, 0:2 * P], ACT.Copy).then_inc(g_row, 1)

            def self_high(t):
                act.wait_ge(av_mm, t + 1)
                if t >= 2:
                    act.wait_ge(ao_mm, t - 1)
                act.activation(lhs_p[:, t % 2, HI], pAV[t % 2], ACT.Copy).then_inc(av_hi, 1)

            self_high(0)
            for s in range(TILES + 2):
                if s > C and s % 2:
                    gate_copy((s - 5) // 2)
                if s + 1 < TILES:
                    self_high(s + 1)
                if s == 0:
                    act.preload_act_table_set(ROOTS)
                if 0 <= s - 1 < TILES:
                    ln_root(2 * TILES + s - 1)
                if s - 2 >= 0:
                    t = s - 2
                    ln_high(2 * TILES + t, xT[:, HI, :, t * P:(t + 1) * P])
            gate_copy(TILES // 2 - 1)
            act.wait_ge(g_step, 2)
            act.activation(gates[:, :, :], g_tmp[:, :, :], ACT.Exp).then_inc(g_exp, 1)

            def expert(e, u, prev=True, nxt=None):
                act.wait_ge(g_col, e + 1)
                for t in range(TILES):
                    act.wait_ge(u_mm, e * TILES + t + 1)
                    if prev or t >= 2:
                        act.wait_ge(u_h, e * TILES + t - 1)
                    sg = sq[:, t % 2, 0:F]
                    act.activation(sg, pKV[t % 2][:, 0:F], ACT.Silu, scale=g_now[:, u, t:t + 1]).then_inc(u_sig, 1)
                    if prev or t >= 1:
                        hidden_high(e * TILES + t - 1, (t - 1) % 2, prev or t >= 3)
                    if nxt is not None and t == 3:
                        act.wait_ge(y_mm, e * TILES)
                        expert_high(e + 1, 1 - u, nxt)

            def hidden_high(n, u, reused):
                act.wait_ge(h_t, n + 1)
                if reused:
                    act.wait_ge(y_mm, n - 1)
                act.activation(hT[:, u, HI], pTT[u][:, 0:2, :], ACT.Copy).then_inc(h_hi, 1)

            expert(0, 0, prev=False, nxt=1)
            with act.Fori(0, (E - 2) // 2) as k:
                expert(k * 2 + 1, 1, nxt=k + 2)
                expert(k * 2 + 2, 0, nxt=k + 2)
            expert(E - 1, 1)
            hidden_high(E * TILES - 1, 1, True)

        @block.vector
        def _(dve):
            tt, ts, stt = nc.vector.tensor_tensor, nc.vector.tensor_scalar, nc.vector.scalar_tensor_tensor

            def ln_stats(n, src):
                nc.vector.bn_stats(bst[:, n % 2], src).then_inc(ln_bst, 1)
                dve.wait_ge(ln_bst, n + 1)
                nc.vector.bn_aggr(mean_var[:, n % 2], bst[:, n % 2]).then_inc(ln_mv, 1)

            def ln_norm(n, src):
                dve.wait_ge(ln_rsd, n + 1)
                if n >= 2:
                    dve.wait_ge(ln_t, n - 1)
                ts(xn[:, n % 2], src, mean_var[:, n % 2, 0:1], ln_rs[:, n % 2], ALU.subtract,
                   ALU.mult).then_inc(ln_x, 1)

            def ln_low(n, dst_lo, dst_hi):
                dve.wait_ge(ln_hi, n + 1)
                tt(dst_lo, pTT[n % 2][:, :, :], dst_hi.bitcast(F32), ALU.subtract).then_inc(ln_lo, 1)

            def head_sums(name, c):
                dve.wait_ge(w_in[JOB[name]], 16)
                nc.vector.tensor_reduce(head_mean[:, c], heads(raw(name)[:, c]), AX.X, ALU.add).then_inc(w_sum, 1)

            def centre(name, c, count):
                dve.wait_ge(w_sum, count)
                w = heads(raw(name)[:, c])
                stt(w, per_head(head_mean[:, c]), -1.0 / HD, w, ALU.mult, ALU.add).then_inc(w_pre[JOB[name]], 1)

            def ctx_low(n, u):
                for t in range(MT):
                    dve.wait_ge(ctx_hi, n * MT + t + 1)
                    tt(ctxT[:, u, LO, :, t * P:(t + 1) * P], pTT[t][:, :, :],
                       ctxT[:, u, HI, :, t * P:(t + 1) * P].bitcast(F32), ALU.subtract).then_inc(ctx_lo, 1)

            def k_sum(b, t):
                dve.wait_ge(k_sq, b * MT + t + 1)
                nc.vector.tensor_reduce(head_ss[:, t], heads(sq[:, t]), AX.X, ALU.add).then_inc(k_ss, 1)

            def k_norm(b, t, reused=True):
                dve.wait_ge(k_rs, b * MT + t + 1)
                if reused:
                    dve.wait_ge(k_t, b * MT + t - 1)
                tt(heads(kn[:, t]), heads(pKV[t][:, :]), per_head(head_rs[:, t]), ALU.mult).then_inc(k_n, 1)

            dve.wait_ge(x_in[0], 16)
            for s in range(2):
                ln_stats(s, x_all[:, s])
            for s in range(2):
                ln_norm(s, x_all[:, s])
            head_sums("xq", 0)
            for c in range(C):
                if c + 1 < C:
                    head_sums("xq", c + 1)
                centre("xq", c, c + 1)
                if c == 1:
                    ln_low(0, lhs_p[:, 0, LO], lhs_p[:, 0, HI])
            for s in range(TILES + 1):
                if 0 < s < TILES:
                    ln_low(s, lhs_p[:, s % 2, LO], lhs_p[:, s % 2, HI])
                if s == TILES:
                    dve.wait_ge(rem_act, 1)
                    tt(ctxT[:, 1, LO, :, 0:P], pAV[0], ctxT[:, 1, HI, :, 0:P].bitcast(F32),
                       ALU.subtract).then_inc(rem_dve, 1)
                if 0 < s and s + 1 < TILES:
                    ln_norm(s + 1, x_all[:, s + 1])
                t = s - 1
                if t >= 0:
                    dve.wait_ge(q_sq, t + 1)
                    nc.vector.tensor_reduce(head_ss[:, t % 2], heads(sq[:, t % 2]), AX.X, ALU.add).then_inc(q_ss, 1)
                if s + 2 < TILES:
                    if s == 0:
                        dve.wait_ge(x_in[1], 16)
                    ln_stats(s + 2, x_all[:, s + 2])
                if t >= 0:
                    dve.wait_ge(q_rs, t + 1)
                    if t >= 2:
                        dve.wait_ge(q_t, t - 1)
                    tt(heads(kn[:, t % 2]), heads(pKV[t % 2][:, :]), per_head(head_rs[:, t % 2]),
                       ALU.mult).then_inc(q_n, 1)
                if s == 0:
                    dve.wait_ge(qn_in, 16)
                    dve.wait_ge(kn_in, 16)
                    stt(qk_col[:, 2, :], qk_col[:, 0, :], SCALE, qk_col[:, 1, :], ALU.mult, ALU.mult).then_inc(qk_set, 1)
                if 1 <= s <= C:
                    head_sums("xk", s - 1)
                    centre("xk", s - 1, C + s)
            ctx_low(0, 0)
            dve.wait_ge(rem_act, 2)
            tt(rem_p[B:2 * B, :], rem_raw[B:2 * B, :], rem_p[B:2 * B, :].bitcast(F32), ALU.subtract).then_inc(rem_dve, 1)
            dve.wait_ge(rem_act, 3)
            nc.vector.tensor_reduce(head_ss[:, 1], heads(sq[:, 1]), AX.X, ALU.add).then_inc(rem_dve, 1)
            dve.wait_ge(rem_act, 5)
            dve.wait_ge(q_t, TILES)
            tt(heads(kn[:, 1]), heads(pV1[:, :]), per_head(head_rs[:, 1]), ALU.mult).then_inc(rem_dve, 1)
            k_sum(0, 0)
            k_norm(0, 0, reused=False)

            def out_copy(t):
                for i, bank in enumerate((pV1[:, :], pP_flat)):
                    dve.wait_ge(o_mm, t * 2 + i + 1)
                    o = bank.rearrange("p (c e n) -> p c e n", c=2, e=2)
                    for e in range(2):
                        a = slice(e * HD, (e + 1) * HD)
                        ts(qoT[a, 2 * i:2 * i + 2, bass.ds(t * P, P)], o[a, :, e, :], 1.0, None,
                           ALU.mult).then_inc(o_out, 1)

            def batch(tile, r, main=True, prev=True, nxt=True, first=False):
                b = tile * BT + r
                p = b - 1
                u, pr = r % 2, (r - 1) % BT
                if prev:
                    dve.wait_ge(sc_mm, b)
                    stt(s_m[:, :, 0:M], masked[:, bass.ds(p, 1), :].broadcast_to([P, G, M]), -BIG,
                        pS[:, :, 0:M], ALU.mult, ALU.add).then_inc(sc_m, 1)
                    dve.wait_ge(sc_m, b)
                    nc.vector.tensor_reduce(neg_max[:, :], s_m[:, :, 0:M], AX.X, ALU.max, negate=True).then_inc(sc_max, 1)
                if nxt:
                    ctx_low(b + 1, 1 - u)
                if prev:
                    dve.wait_ge(sc_exp, b * G)
                    stt(p_den[:, :], neg_max[:, :], BIG / 2, p_sum[:, :], ALU.is_lt, ALU.mult).then_inc(sc_step, 1)
                    dve.wait_ge(sc_step, p * 3 + 1)
                    nc.vector.reciprocal(p_inv[:, :], p_den[:, :]).then_inc(sc_step, 1)
                    dve.wait_ge(sc_step, p * 3 + 2)
                    stt(p_scale[:, :], neg_max[:, :], BIG / 2, p_inv[:, :], ALU.is_lt, ALU.mult).then_inc(sc_step, 1)
                if main:
                    if not prev:
                        dve.wait_ge(q_out, C * TILES)
                        dve.wait_ge(rem_act, 6)
                    for e in range(2):
                        a = slice(e * HD, (e + 1) * HD)
                        ts(qblk[a, HI, :, e * S:(e + 1) * S], qoT[a, :, bass.ds(b * S, S)], 1.0, None,
                           ALU.mult).then_inc(qb_hi, 1)
                    dve.wait_ge(qb_hi, b * 2 + 2)
                    for e in range(2):
                        a = slice(e * HD, (e + 1) * HD)
                        tt(qblk[a, LO, :, e * S:(e + 1) * S], qoT[a, :, bass.ds(b * S, S)],
                           qblk[a, HI, :, e * S:(e + 1) * S].bitcast(F32), ALU.subtract)
                    ts(kT[:, HI, :, M - 1:M], kT_rem[:, :, bass.ds(b, 1)], 1.0, None, ALU.mult).then_inc(k_rem, 1)
                    dve.wait_ge(k_rem, b * 2 + 1)
                    tt(kT[:, LO, :, M - 1:M], kT_rem[:, :, bass.ds(b, 1)], kT[:, HI, :, M - 1:M].bitcast(F32),
                       ALU.subtract).then_inc(k_rem, 1)
                    k_sum(b, 1)
                if prev:
                    dve.wait_ge(p_n, b * G)
                    if not first:
                        dve.wait_ge(p_rt, p)
                    for g in range(G):
                        ts(p_rem[:, g, :], batch_col[:, :], batch_col[:, bass.ds(p, 1)], prob[:, g, M - 1:M],
                           ALU.is_equal, ALU.mult).then_inc(p_r, 1)
                if not main:
                    out_add(0)
                if main:
                    k_norm(b, 1, reused=prev)
                if prev and pr == 0 and not first:
                    out_copy(tile - 1)
                if prev:
                    dve.wait_ge(p_hi, b)
                    tt(pT[:, LO], pP[:, :, :], pT[:, HI].bitcast(F32), ALU.subtract).then_inc(p_lo, 1)
                    dve.wait_ge(p_rh, b)
                    a = slice(2 * B, 3 * B)
                    tt(pT_rem[a, :], pV1[a, 0:G * P], pT_rem[a, :].bitcast(F32), ALU.subtract).then_inc(p_rl, 1)
                if not main:
                    out_add(1)
                    ln_norm(TILES, x_all[:, 0])
                if main:
                    for t in range(MT):
                        dve.wait_ge(k_hi, b * MT + t + 1)
                        tt(kT[:, LO, :, t * P:(t + 1) * P], pTT[t][:, :, :],
                           kT[:, HI, :, t * P:(t + 1) * P].bitcast(F32), ALU.subtract).then_inc(k_lo, 1)
                if main and not nxt:
                    for c in range(C // 2):
                        dve.wait_ge(w_hi[JOB["xo"]], c + 1)
                        tt(xo_p[:, LO, c], raw("xo")[:, c], xo_p[:, HI, c].bitcast(F32),
                           ALU.subtract).then_inc(w_lo[JOB["xo"]], 1)
                if nxt:
                    k_sum(b + 1, 0)
                    k_norm(b + 1, 0)
                if prev:
                    for g in (1, 0):
                        dve.wait_ge(pc_hi, p * 2 + 2 - g)
                        z = z_b[:, :, 2 * g:2 * g + 2, :, pr, :]
                        tt(z[:, LO], prob_ctx(g), z[:, HI].bitcast(F32), ALU.subtract).then_inc(pc_lo, 1)

            def bn_terms(w):
                a, c = bn_ac[w]
                dve.wait_ge(bn_rs, w + 1)
                tt(a, bn_vec[:, 0, :], bn_vec[:, 3, :], ALU.mult).then_inc(bn_a, 1)
                dve.wait_ge(bn_a, w + 1)
                tt(bn_vec[:, 2, :], bn_vec[:, 2, :], a, ALU.mult).then_inc(bn_ma, 1)
                dve.wait_ge(bn_ma, w + 1)
                tt(c, bn_vec[:, 1, :], bn_vec[:, 2, :], ALU.subtract).then_inc(bn_c, 1)

            def out_add(t):
                dve.wait_ge(xo_mm, t + 1)
                tt(x_all[:, t], x_all[:, t], pKV[t % 2][:, :], ALU.add).then_inc(x1_add, 1)
                dve.wait_ge(x1_add, t + 1)
                ln_stats(TILES + t, x_all[:, t])

            for r in range(BT):
                if r == 1:
                    dve.wait_ge(not_mask, 1)
                batch(0, r, prev=r > 0, first=r == 1)
            with dve.Fori(1, TILES - 1) as k:
                for r in range(BT):
                    batch(k, r)
            for r in range(BT):
                batch(TILES - 1, r, nxt=r < BT - 1)
            batch(TILES, 0, main=False, nxt=False)
            out_add(2)
            ln_norm(TILES + 1, x_all[:, 1])
            out_add(3)
            bn_terms(0)
            out_copy(TILES - 1)

            for t in range(2, TILES + 2):
                if t < TILES:
                    ln_norm(TILES + t, x_all[:, t])
                ln_low(TILES + t - 2, xT[:, LO, :, (t - 2) * P:(t - 1) * P], xT[:, HI, :, (t - 2) * P:(t - 1) * P])
                if t + 2 < TILES:
                    out_add(t + 2)
                if t == 6:
                    bn_terms(1)
            dve.wait_ge(bn_c, 2)
            for n in range(3 * TILES):
                w, t = divmod(n, TILES)
                if n == 2 * TILES:
                    dve.wait_ge(z_sig, 2 * TILES)
                    for r in range(TILES):
                        ts(a_all[:, r, :], ident[:, :], rows[:, 0, r:r + 1], 1.0 / D, ALU.mult,
                           ALU.mult).then_inc(t_step, 1)
                    ts(rows[:, 1, :], rows[:, 1, :], 1.0 / D, None, ALU.mult).then_inc(t_step, 1)
                if n == 2 * TILES + 4:
                    dve.wait_ge(t_pe, 1)
                    dve.wait_ge(t_step, TILES + 1)
                    for g in range(2):
                        half = slice(g * C, (g + 1) * C)
                        tt(dt_all[:, half, :], rows[:, 1, half].unsqueeze(2).broadcast_to([P, C, P]),
                           pS[:, g, :].rearrange("p (t n) -> p t n", t=C), ALU.subtract).then_inc(t_step, 1)
                    dve.wait_ge(t_step, TILES + 3)
                    stt(a_all[:, :, :], dt_all[:, :, :], -1.0, dt_all[:, :, :], ALU.mult, ALU.max).then_inc(t_step, 1)
                if n == 2 * TILES + 1:
                    dve.wait_ge(gw_hi, 1)
                    tt(gw_p[:, LO], gw_raw[:, :, :], gw_p[:, HI].bitcast(F32), ALU.subtract).then_inc(gw_lo, 1)
                if n == 3 * TILES - 2:
                    ts(dt_all[:, :, :], dt_all[:, :, :], 0.0, 2 * A_STDP, ALU.is_lt, ALU.mult).then_inc(t_step, 1)
                    dve.wait_ge(t_step, TILES + 5)
                    dve.wait_ge(t_act, 1)
                    stt(dt_all[:, :, :], dt_all[:, :, :], -A_STDP, a_all[:, :, :], ALU.add, ALU.mult).then_inc(t_step, 1)
                    dve.wait_ge(t_step, TILES + 6)
                    stt(a_all[:, :, :], dt_all[:, :, :], W_OFF, same_seq[:, :].unsqueeze(1).broadcast_to([P, TILES, P]),
                        ALU.add, ALU.mult).then_inc(t_step, 1)
                dve.wait_ge(z_mm, n + 1)
                if n >= 2:
                    dve.wait_ge(z_sig, n - 1)
                tt(sq[:, n % 2], pZ[n % 3][:, :], bn_ac[w][1], ALU.add).then_inc(z_c, 1)
                if n == TILES + 1:
                    dve.wait_ge(w_pre[JOB["aq"]], C)
                    bn_terms(2)
                    dve.wait_ge(bn_c, 3)
            def self_low(t):
                dve.wait_ge(av_hi, t + 1)
                tt(lhs_p[:, t % 2, LO], pAV[t % 2], lhs_p[:, t % 2, HI].bitcast(F32), ALU.subtract).then_inc(av_lo, 1)

            self_low(0)
            for s in range(TILES + 2):
                t = s - 1
                if 0 <= t < TILES:
                    dve.wait_ge(ao_mm, t + 1)
                    dve.wait_ge(bo_add, t + 1)
                    tt(x_all[:, t], x_all[:, t], pKV[t % 2][:, :], ALU.add).then_inc(x2_add, 1)
                    dve.wait_ge(x2_add, t + 1)
                    ln_stats(2 * TILES + t, x_all[:, t])
                if s + 1 < TILES:
                    self_low(s + 1)
                if 0 <= t < TILES:
                    ln_norm(2 * TILES + t, x_all[:, t])
                t = s - 2
                if t >= 0:
                    ln_low(2 * TILES + t, xT[:, LO, :, t * P:(t + 1) * P], xT[:, HI, :, t * P:(t + 1) * P])
            step = [0]

            def gate(ins):
                step[0] += 1
                ins.then_inc(g_step, 1)

            per_token = lambda ap: ap.unsqueeze(2).broadcast_to([P, TILES, E])
            dve.wait_ge(g_t, TILES // 2)
            gate(nc.vector.tensor_reduce(g_red[:, :], p_gate, AX.X, ALU.max))
            dve.wait_ge(g_step, 1)
            gate(tt(g_tmp[:, :, :], p_gate, per_token(g_red[:, :]), ALU.subtract))
            dve.wait_ge(g_exp, 1)
            gate(nc.vector.tensor_reduce(g_red[:, :], gates[:, :, :], AX.X, ALU.add))
            dve.wait_ge(g_step, 3)
            gate(nc.vector.reciprocal(g_red[:, :], g_red[:, :]))
            dve.wait_ge(g_step, 4)
            gate(tt(gates[:, :, :], gates[:, :, :], per_token(g_red[:, :]), ALU.mult))
            dve.wait_ge(g_step, 5)
            other = gates[:, :, :].unsqueeze(2).broadcast_to([P, TILES, E, E])
            own = gates[:, :, :].unsqueeze(3).broadcast_to([P, TILES, E, E])
            gate(tt(cmp_gt, other, own, ALU.is_gt))
            gate(tt(cmp_eq, other, own, ALU.is_equal))
            dve.wait_ge(g_step, 7)
            gate(tt(cmp_eq, cmp_eq, tri[:, :, :].unsqueeze(1).broadcast_to([P, TILES, E, E]), ALU.mult))
            dve.wait_ge(g_step, 8)
            gate(tt(cmp_gt, cmp_gt, cmp_eq, ALU.add))
            dve.wait_ge(g_step, 9)
            gate(nc.vector.tensor_reduce(g_tmp[:, :, :], cmp_gt, AX.X, ALU.add))
            dve.wait_ge(g_step, 10)
            gate(stt(gates[:, :, :], g_tmp[:, :, :], 1.5, gates[:, :, :], ALU.is_lt, ALU.mult))
            dve.wait_ge(g_step, 11)

            def hidden_low(n, u):
                dve.wait_ge(h_hi, n + 1)
                tt(hT[:, u, LO], pTT[u][:, 0:2, :], hT[:, u, HI].bitcast(F32), ALU.subtract).then_inc(h_lo, 1)

            def expert_add(n, t):
                dve.wait_ge(y_mm, n + 1)
                tt(x_all[:, t % TILES], x_all[:, t % TILES], pY[t % 2], ALU.add).then_inc(y_add, 1)

            def expert(e, u, prev=True):
                ts(g_now[:, u, :], gates[:, :, bass.ds(e, 1)].rearrange("p t e -> p (t e)"), 1.0, None,
                   ALU.mult).then_inc(g_col, 1)
                dve.wait_ge(g_col, e + 1)
                for t in range(TILES):
                    n = e * TILES + t
                    dve.wait_ge(u_sig, n + 1)
                    if prev or t >= 2:
                        dve.wait_ge(h_t, n - 1)
                    stt(xn[:, t % 2, 0:F], pKV[t % 2][:, F:2 * F], g_now[:, u, t:t + 1], sq[:, t % 2, 0:F],
                        ALU.mult, ALU.mult).then_inc(u_h, 1)
                    if prev or t >= 1:
                        hidden_low(n - 1, (t - 1) % 2)
                    if prev or t >= 2:
                        expert_add(n - 2, t - 2)

            expert(0, 0, prev=False)
            with dve.Fori(0, (E - 2) // 2) as k:
                expert(k * 2 + 1, 1)
                expert(k * 2 + 2, 0)
            expert(E - 1, 1)
            hidden_low(E * TILES - 1, 1)
            expert_add(E * TILES - 2, TILES - 2)
            expert_add(E * TILES - 1, TILES - 1)

        @block.tensor
        def _(pe):
            def ln_turn(n):
                pe.wait_ge(ln_x, n + 1)
                if n >= 2:
                    pe.wait_ge(ln_lo, n - 1)
                for c in range(C):
                    last = pe.transpose(pTT[n % 2][:, c, :], xn[:, n % 2, c * P:(c + 1) * P], ident[:, :])
                last.then_inc(ln_t, 1)

            def tile_of(buf, u):
                return lambda s, c: buf[:, u, s, c, :]

            def rows_of(buf, t):
                return lambda s, c: buf[:, s, c, t * P:(t + 1) * P]

            def weight(buf, lo=0, hi=D):
                return lambda s, c: buf[:, s, c, lo:hi]

            ctx_rows = lambda u, t: (lambda s, c: ctxT[:, u, s, c, t * P:(t + 1) * P])
            wk = weight(wkv, 0, D)

            def ctx_turn(n, u, turn):
                pe.wait_ge(ctx_in[u], turn * 16)
                for t in range(MT):
                    for c in range(C):
                        last = pe.transpose(pTT[t][:, c, :], ctx_raw[:, u, t, c * P:(c + 1) * P], ident[:, :])
                    last.then_inc(ctx_t, 1)

            def k_half(b, t, u):
                pe.wait_ge(ctx_lo, b * MT + t + 1)
                split_products(pe, pKV[t][:, :], ctx_rows(u, t), wk, C).then_inc(k_mm, 1)

            pe.wait_ge(const_set, 2)
            for s in range(TILES + 2):
                if s < TILES:
                    ln_turn(s)
                if s == TILES:
                    pe.wait_ge(rem_in, 48)
                    for c in range(C):
                        last = pe.transpose(pAV[0][:, c, :], rem_raw[:, c * P:(c + 1) * P], ident[:, :])
                    last.then_inc(rem_pe, 1)
                t = s - 1
                if 0 <= t < TILES:
                    pe.wait_ge(ln_lo, t + 1)
                    if t >= 2:
                        pe.wait_ge(q_n, t - 1)
                    for c in range(C):
                        if t == 0:
                            pe.wait_ge(w_lo[JOB["xq"]], c + 1)
                        last = split_products(pe, pKV[t % 2][:, :], tile_of(lhs_p, t % 2), weight(w_slot[:, 0]),
                                              c + 1, start=c == 0, stop=c == C - 1, first=c)
                    last.then_inc(q_mm, 1)
                if s == TILES:
                    ctx_turn(0, 0, 1)
                    pe.wait_ge(rem_dve, 1)
                    pe.wait_ge(w_lo[JOB["xk"]], C)
                    split_products(pe, pV1[:, :], ctx_rows(1, 0), wk, C).then_inc(rem_pe, 1)
                if s == TILES + 1:
                    pe.wait_ge(q_n, TILES - 1)
                    k_half(0, 0, 0)
                t = s - 2
                if t >= 0:
                    pe.wait_ge(q_n, t + 1)
                    if t >= 2:
                        pe.wait_ge(q_out, C * (t - 1))
                    for c in range(C):
                        last = pe.transpose(pS[:, t % 2, c * P:(c + 1) * P], kn[:, t % 2, c * P:(c + 1) * P], ident[:, :])
                    last.then_inc(q_t, 1)

            def out_tile(t):
                pe.wait_ge(pc_lo, (t + 1) * BT * 2)
                for c in range(C):
                    o = (pV1[:, :], pP_flat)[c // 2][:, (c % 2) * 2 * P:(c % 2 + 1) * 2 * P]
                    last = split_products(pe, o, lambda s, k: wkv[:, s, k, D + c * P:D + (c + 1) * P],
                                          lambda s, k: z_p[:, s, k, c * 2 * P:(c + 1) * 2 * P], C)
                    if c % 2:
                        last.then_inc(o_mm, 1)

            def project(t):
                pe.wait_ge(oT_lo, t + 1)
                if t == 0:
                    pe.wait_ge(w_lo[JOB["xo"]], C)
                if t >= 2:
                    pe.wait_ge(x1_add, t - 1)
                split_products(pe, pKV[t % 2][:, :], tile_of(out_p, t % 2), weight(xo_p), C).then_inc(xo_mm, 1)

            def z_product(n):
                w, t = divmod(n, TILES)
                if t == 0:
                    pe.wait_ge(w_lo[JOB[("aq", "ak", "av")[w]]], C)
                if w == 0:
                    pe.wait_ge(ln_lo, TILES + t + 1)
                if n == 0:
                    pe.wait_ge(o_out, 4 * TILES)
                elif n < 3:
                    pe.wait_ge(x1_add, TILES - 2 + n)
                else:
                    pe.wait_ge(z_c, n - 2)
                split_products(pe, pZ[n % 3][:, :], rows_of(xT, t), weight(w_slot[:, w % 2]), C).then_inc(z_mm, 1)

            def batch(tile, r, main=True, prev=True, nxt=True, first=False):
                b = tile * BT + r
                u, pr = r % 2, (r - 1) % BT
                if prev:
                    pe.wait_ge(k_lo, b * MT)
                    for g in range(G):
                        for j in range(2):
                            c = 2 * g + j
                            qb = lambda s, _: qblk[:, s].rearrange("p c n -> p (c n)")[:, c * P - j * HD:(c + 1) * P - j * HD]
                            last = split_products(pe, pS[:, g, 0:M + 1], qb, lambda s, _: kT[:, s, c, :], 1,
                                                  start=j == 0, stop=j == 1)
                    last.then_inc(sc_mm, 1)
                if nxt:
                    if not prev:
                        pe.wait_ge(ctx_lo, b * MT + 2)
                    ctx_turn(b + 1, 1 - u, tile * 2 + (r + 1) // 2 + 1)
                if main:
                    if prev:
                        pe.wait_ge(k_n, b * MT)
                    k_half(b, 1, u)
                if not prev:
                    pe.wait_ge(rem_dve, 4)
                    for c in range(C):
                        last = pe.transpose(pAV[0][:, c, :], kn[:, 1, c * P:(c + 1) * P], ident[:, :])
                    last.then_inc(rem_pe, 1)
                if prev and pr == 0 and not first:
                    out_tile(tile - 1)
                if nxt:
                    pe.wait_ge(k_n, b * MT + 1)
                    pe.wait_ge(ctx_lo, b * MT + 3)
                    split_products(pe, pK0[:, :], ctx_rows(1 - u, 0), wk, C - 1, stop=False)
                if not main:
                    project(0)
                    project(1)
                if prev:
                    pe.wait_ge(p_n, b * G)
                    if not first:
                        pe.wait_ge(pc_lo, b * 2 - 2)
                        if pr == 0:
                            pe.wait_ge(o_out, tile * 4)
                    for t in range(MT):
                        for g in range(G):
                            last = pe.transpose(pP[:, t, g * P:(g + 1) * P], prob[:, g, t * P:(t + 1) * P], ident[:, :])
                    last.then_inc(p_t, 1)
                if nxt:
                    split_products(pe, pK0[:, :], ctx_rows(1 - u, 0), wk, C, start=False, first=C - 1).then_inc(k_mm, 1)
                if prev:
                    pe.wait_ge(p_r, b * G)
                    for g in range(G):
                        last = pe.transpose(pV1[:, g * P:(g + 1) * P], p_rem[:, g, :], ident[:, :])
                    last.then_inc(p_rt, 1)
                if not main:
                    project(2)
                if main:
                    pe.wait_ge(k_n, b * MT + 2)
                    if nxt:
                        pe.wait_ge(ctx_lo, b * MT + 4)
                    for t in range(MT):
                        for c in range(C):
                            last = pe.transpose(pTT[t][:, c, :], kn[:, t, c * P:(c + 1) * P], ident[:, :])
                        last.then_inc(k_t, 1)
                if prev:
                    pe.wait_ge(cn_lo, b)
                    pe.wait_ge(p_lo, b)
                    for g in (1, 0):
                        for j in range(2):
                            c = 2 * g + j
                            o = pC[g][:, j * G * P:(j + 1) * G * P]
                            split_products(pe, o, lambda s, t: ctxN[:, 1 - u, s, t, c * P:(c + 1) * P],
                                           lambda s, t: pT[:, s, t, :], MT, stop=False)
                            if (g, j) == (1, 0):
                                pe.wait_ge(p_rl, b)
                            last = pe.matmul(o, rem_p[:, c * P:(c + 1) * P], pT_rem[:, :], start=False, stop=True)
                        last.then_inc(pc_mm, 1)

            for r in range(BT):
                if r == 1:
                    pe.wait_ge(q_out, C * TILES)
                    pe.wait_ge(w_lo[JOB["xv"]], C)
                batch(0, r, prev=r > 0, first=r == 1)
            with pe.Fori(1, TILES - 1) as k:
                for r in range(BT):
                    batch(k, r)
            for r in range(BT):
                batch(TILES - 1, r, nxt=r < BT - 1)
            batch(TILES, 0, main=False, nxt=False)
            project(3)
            out_tile(TILES - 1)

            for t in range(TILES):
                ln_turn(TILES + t)
                if t + 4 < TILES:
                    project(t + 4)
                elif t >= 5:
                    z_product(t - 5)
            for n in range(TILES - 5, 3 * TILES):
                z_product(n)
                if n == 2 * TILES + 1:
                    pe.wait_ge(t_step, TILES)
                    for g in range(2):
                        last = pe.matmul(pS[:, g, :], ones[:, :],
                                         a_all[:, g * C:(g + 1) * C, :].rearrange("p t n -> p (t n)"),
                                         start=True, stop=True)
                    last.then_inc(t_pe, 1)
            def gate_pair(k):
                pe.wait_ge(ln_lo, 2 * TILES + 2 * k + 2)
                if k:
                    pe.wait_ge(g_row, k)
                split_products(pe, pS[0:E, 1, 0:2 * P], lambda s, c: gw_p[:, s, c, :],
                               lambda s, c: xT[:, s, c, k * 2 * P:(k + 1) * 2 * P], C).then_inc(g_mm, 1)

            def gate_turn(k):
                pe.wait_ge(g_row, k + 1)
                for j in range(2):
                    last = pe.transpose(p_gate[:, 2 * k + j, :], sq[0:E, k % 2, j * P:(j + 1) * P], ident[0:E, 0:E])
                last.then_inc(g_t, 1)

            def first_hidden(t, lo, hi):
                pe.wait_ge(e_lo, 1)
                pe.wait_ge(x2_add, TILES - 1 + t)
                last = split_products(pe, pKV[t][:, :], rows_of(xT, t), lambda s, c: e_p[0][:, s, c * D:(c + 1) * D],
                                      hi, start=lo == 0, stop=hi == C, first=lo)
                if hi == C:
                    last.then_inc(u_mm, 1)

            pe.wait_ge(t_step, TILES + 7)
            pe.wait_ge(gw_lo, 1)
            for s in range(TILES + 3):
                if s < TILES:
                    pe.wait_ge(z_sig, 2 * TILES + s + 1)
                    if s == 1:
                        pe.wait_ge(z_c, 3 * TILES - 2)
                    if s >= 2:
                        pe.wait_ge(av_lo, s - 1)
                    for c in range(C):
                        last = pe.matmul(pAV[s % 2][:, c, :], v_self[:, s, c * P:(c + 1) * P], a_all[:, s, :],
                                         start=True, stop=True)
                    last.then_inc(av_mm, 1)
                if s == TILES + 1:
                    first_hidden(0, 0, 2)
                t = s - 1
                if 0 <= t < TILES:
                    pe.wait_ge(av_lo, t + 1)
                    if t == 0:
                        pe.wait_ge(w_lo[JOB["ao"]], C)
                    if t < 2:
                        pe.wait_ge(z_c, 3 * TILES - 1 + t)
                    else:
                        pe.wait_ge(x2_add, t - 1)
                    split_products(pe, pKV[t % 2][:, :], tile_of(lhs_p, t % 2), weight(w_slot[:, 1]),
                                   C).then_inc(ao_mm, 1)
                t = s - 2
                if 0 <= t < TILES:
                    ln_turn(2 * TILES + t)
                if s == TILES + 1:
                    first_hidden(0, 2, C)
                t = s - 3
                if t > 0 and t % 2:
                    gate_pair(t // 2)
                elif t > 0:
                    gate_turn(t // 2 - 1)

            first_hidden(1, 0, 1)
            gate_turn(TILES // 2 - 1)
            first_hidden(1, 1, C)

            def hidden_turn(n, u, reused):
                pe.wait_ge(u_h, n + 1)
                if reused:
                    pe.wait_ge(h_lo, n - 1)
                for c in range(2):
                    last = pe.transpose(pTT[u][:, c, :], xn[:, u, c * P:(c + 1) * P], ident[:, :])
                last.then_inc(h_t, 1)

            def hidden_out(n, u, w, reused):
                pe.wait_ge(h_lo, n + 1)
                if reused:
                    pe.wait_ge(y_add, n - 1)
                w2_of = lambda s, c: e_p[w][:, s, (C + c) * D:(C + c + 1) * D]
                split_products(pe, pY[u], tile_of(hT, u), w2_of, 2).then_inc(y_mm, 1)

            def expert(e, u, prev=True):
                pe.wait_ge(e_lo, e + 1)
                w13 = lambda s, c: e_p[u][:, s, c * D:(c + 1) * D]
                for t in range(TILES):
                    n = e * TILES + t
                    if prev or t >= 2:
                        pe.wait_ge(u_h, n - 1)
                        split_products(pe, pKV[t % 2][:, :], rows_of(xT, t), w13, C).then_inc(u_mm, 1)
                    if prev or t >= 1:
                        hidden_turn(n - 1, (t - 1) % 2, prev or t >= 3)
                    if prev or t >= 2:
                        hidden_out(n - 2, t % 2, u if t >= 2 else 1 - u, prev or t >= 4)

            expert(0, 0, prev=False)
            with pe.Fori(0, (E - 2) // 2) as k:
                expert(k * 2 + 1, 1)
                expert(k * 2 + 2, 0)
            expert(E - 1, 1)
            hidden_turn(E * TILES - 1, 1, True)
            hidden_out(E * TILES - 2, 0, 1, True)
            hidden_out(E * TILES - 1, 1, 1, True)


_INS = ["x", "ctx_1024", "mask_BxSxS2_bk0", "L0_xattn_Wq", "L0_xattn_Wkv", "L0_xattn_Wo", "L0_xattn_qn_w",
        "L0_xattn_kn_w", "L0_attn_Wq", "L0_attn_gq", "L0_attn_bq", "L0_attn_mq", "L0_attn_vq", "L0_attn_Wk",
        "L0_attn_gk", "L0_attn_bk", "L0_attn_mk", "L0_attn_vk", "L0_attn_Wv", "L0_attn_gv", "L0_attn_bv",
        "L0_attn_mv", "L0_attn_vv", "L0_attn_Wo", "L0_attn_bo", "L0_ffn_gate_w", "L0_ffn_w1", "L0_ffn_w2",
        "L0_ffn_w3"]


def kernel(**inputs):
    import numpy as _np
    import concourse.bacc as _bacc
    from concourse import mybir as _mybir
    from concourse.bass_utils import run_bass_kernel_spmd as _run

    nc = _bacc.Bacc("TRN2", target_bir_lowering=False, num_devices=1)
    arrays, args = {}, []
    for name in _INS:
        a = _np.ascontiguousarray(inputs[name])
        arrays[f"in_{name}_dram"] = a
        args.append(nc.dram_tensor(f"in_{name}_dram", a.shape, _mybir.dt.from_np(a.dtype), kind="ExternalInput").ap())
    shape = inputs["x"].shape
    args.append(nc.dram_tensor("out_0_dram", shape, _mybir.dt.float32, kind="ExternalOutput").ap())
    perceiver_block(nc, *args)
    r = _run(nc, [arrays], core_ids=[0])
    return r.results[0]["out_0_dram"]
```
